# Optimizing a Trainium2 kernel written in Bass

```python
import numpy as np
import jax
import jax.numpy as jnp

def _softmax(x, axis=-1):
    return jax.nn.softmax(x, axis=axis)

def _gelu(x):
    return jax.nn.gelu(x, approximate=True)

def _silu(x):
    return jax.nn.silu(x)

def _sigmoid(x):
    return jax.nn.sigmoid(x)

def _layernorm(x, axis=-1, eps=1e-05):
    m = jnp.mean(x, axis=axis, keepdims=True)
    v = jnp.var(x, axis=axis, keepdims=True)
    return (x - m) / jnp.sqrt(v + eps)

def _scatter_add(tgt, idx, src, axis=0):
    return tgt.at[idx].add(src)

def _segment_sum(src, seg, n):
    return jax.ops.segment_sum(src, seg, n)
kernel_name = 'mk_gnn_preln_d4_gnn_r32_546595'

def setup_inputs(seed: int=0):
    np.random.seed(seed)
    _w = jnp.asarray

    def _rec_inputs():
        import jax
        import jax.numpy as jnp
        _gk = jax.random.key(seed)
        x = -0.0009044 + 1 * jax.random.normal(jax.random.fold_in(_gk, 1), (3125, 32), jnp.float32)
        _s = jax.random.randint(jax.random.fold_in(_gk, 2), (25000,), 0, 3125, jnp.int32)
        _d = jax.random.randint(jax.random.fold_in(_gk, 3), (25000,), 0, 3125, jnp.int32)
        _loop = jnp.arange(3125, dtype=jnp.int32)
        src = jnp.concatenate([_s, _d, _loop])
        dst = jnp.concatenate([_d, _s, _loop])
        _o = jnp.argsort(dst, stable=True)
        src = src[_o]
        dst = dst[_o]
        edge_attr_10 = jax.random.uniform(jax.random.fold_in(_gk, 13), (53125, 10), jnp.float32, 0.0, 1)
        edge_attr_16 = 0.000196303 + 1.00016 * jax.random.normal(jax.random.fold_in(_gk, 14), (53125, 16), jnp.float32)
        edge_attr_3 = 0.00109039 + 0.999626 * jax.random.normal(jax.random.fold_in(_gk, 15), (53125, 3), jnp.float32)
        edge_weight = jax.random.uniform(jax.random.fold_in(_gk, 17), (53125,), jnp.float32, 0.0, 0.999997)
        edge_weight1 = 0.000614103 + 0.999867 * jax.random.normal(jax.random.fold_in(_gk, 18), (53125, 1), jnp.float32)
        return (x, src, dst, edge_attr_10, edge_attr_16, edge_attr_3, edge_weight, edge_weight1)
    x, src, dst, edge_attr_10, edge_attr_16, edge_attr_3, edge_weight, edge_weight1 = _rec_inputs()

    def _L0_gnn_setup():
        import jax, jax.numpy as jnp
        import numpy as np
        N = 50000
        E = 50000
        D_IN = 32
        D_EF = 16
        D_H = 64
        D_MSG = 32
        D_UP = 32

        def mlp2(h, W1, b1, W2, b2):
            return jax.nn.relu(h @ W1 + b1) @ W2 + b2
        key = jax.random.key(seed)
        ks = jax.random.split(key, 10)
        s = 0.05
        return {'x': jax.random.normal(ks[0], (N, D_IN), dtype=jnp.float32), 'degrees': jax.random.uniform(ks[1], (N, 1), dtype=jnp.float32), 'edge_features': jax.random.normal(ks[2], (E, D_EF), dtype=jnp.float32), 'W1m': jax.random.normal(ks[3], (2 * D_IN + D_EF, D_H), dtype=jnp.float32) * s, 'b1m': jnp.zeros((D_H,), dtype=jnp.float32), 'W2m': jax.random.normal(ks[4], (D_H, D_MSG), dtype=jnp.float32) * s, 'b2m': jnp.zeros((D_MSG,), dtype=jnp.float32), 'W1u': jax.random.normal(ks[5], (D_IN + D_MSG, D_H), dtype=jnp.float32) * s, 'b1u': jnp.zeros((D_H,), dtype=jnp.float32), 'W2u': jax.random.normal(ks[6], (D_H, D_UP), dtype=jnp.float32) * s, 'b2u': jnp.zeros((D_UP,), dtype=jnp.float32), 'edge_index': jax.random.randint(ks[7], (2, E), 0, N, dtype=jnp.int64)}
    _L0_gnn_all = _L0_gnn_setup()
    _L0_gnn_in = {k: v for k, v in _L0_gnn_all.items() if k in ('W1m', 'b1m', 'W2m', 'b2m', 'W1u', 'b1u', 'W2u', 'b2u')}
    del _L0_gnn_all

    def _L1_gnn_setup():
        import jax, jax.numpy as jnp
        import numpy as np
        N = 50000
        E = 25000
        H = 8
        C = 32
        L = 3
        NEG_SLOPE = 0.2
        BN_EPS = 1e-05

        def gatv2_layer(x, Wl, bl, Wr, br, att, bias, src, dst, n):
            xl = (x @ Wl + bl).reshape(n, H, C)
            xr = (x @ Wr + br).reshape(n, H, C)
            e = jax.nn.leaky_relu(xl[src] + xr[dst], NEG_SLOPE)
            logits = jnp.einsum('ehc,hc->eh', e, att)
            m = jax.ops.segment_max(logits, dst, num_segments=n)
            m = jnp.where(jnp.isfinite(m), m, 0.0)
            p = jnp.exp(logits - jax.lax.stop_gradient(m)[dst])
            denom = jax.ops.segment_sum(p, dst, num_segments=n)
            alpha = p / (denom[dst] + 1e-16)
            out = jax.ops.segment_sum(xl[src] * alpha[:, :, None], dst, num_segments=n)
            return out.mean(axis=1) + bias

        def batchnorm_train(x, gamma, beta):
            mu = x.mean(axis=0)
            var = x.var(axis=0)
            return (x - mu) * jax.lax.rsqrt(var + BN_EPS) * gamma + beta
        key = jax.random.key(seed)
        ks = jax.random.split(key, 8)
        s = 1.0 / np.sqrt(C)
        return {'patch_embs': jax.random.normal(ks[0], (N, C), jnp.float32), 'edge_index': jax.random.randint(ks[1], (2, E), 0, N, dtype=jnp.int32), 'edge_attr': jax.random.normal(ks[2], (E, 1), jnp.float32), 'Wl': jax.random.normal(ks[3], (L, C, H * C), jnp.float32) * s, 'bl': jnp.zeros((L, H * C), jnp.float32), 'Wr': jax.random.normal(ks[4], (L, C, H * C), jnp.float32) * s, 'br': jnp.zeros((L, H * C), jnp.float32), 'att': jax.random.normal(ks[5], (L, H, C), jnp.float32) * s, 'conv_bias': jnp.zeros((L, C), jnp.float32), 'bn_gamma': jnp.ones((L, C), jnp.float32), 'bn_beta': jnp.zeros((L, C), jnp.float32)}
    _L1_gnn_all = _L1_gnn_setup()
    _L1_gnn_in = {k: v for k, v in _L1_gnn_all.items() if k in ('Wl', 'bl', 'Wr', 'br', 'att', 'conv_bias', 'bn_gamma', 'bn_beta')}
    del _L1_gnn_all

    def _L2_gnn_setup():
        import jax, jax.numpy as jnp
        import numpy as np
        MUL = 16
        MOUT = 8
        TANH_GAIN = 1.593
        INV_SQRT3 = 0.5773502691896258
        PW_S = 0.17677669529663687
        PW_V = 0.25

        def _w3j_121():
            s2, s6 = (2 ** 0.5, 6 ** 0.5)
            M = np.zeros((5, 3, 3))
            M[0, 0, 1] = M[0, 1, 0] = 1 / s2
            M[1, 1, 2] = M[1, 2, 1] = 1 / s2
            M[2] = np.diag([-1.0, -1.0, 2.0]) / s6
            M[3, 0, 2] = M[3, 2, 0] = 1 / s2
            M[4] = np.diag([1.0, -1.0, 0.0]) / s2
            return jnp.asarray(np.transpose(M, (1, 0, 2)) / 5 ** 0.5, jnp.float32)
        W3J121 = _w3j_121()

        def _sph(edge_vec):
            n = edge_vec / jnp.linalg.norm(edge_vec, axis=1, keepdims=True)
            x, y, z = (n[:, 0], n[:, 1], n[:, 2])
            y1 = 3.0 ** 0.5 * n
            s15 = 15.0 ** 0.5
            y2 = jnp.stack([s15 * x * y, s15 * y * z, 5.0 ** 0.5 / 2 * (3 * z * z - 1), s15 * x * z, s15 / 2 * (x * x - y * y)], axis=1)
            return (y1, y2)

        def _forward(x, edge_src, edge_dst, edge_vec, emb, norm, W1, W2):
            N, E = (x.shape[0], edge_src.shape[0])
            xs = jnp.concatenate([x[edge_src, :8], x[edge_dst, :8]], axis=1)
            xv = jnp.concatenate([x[edge_src, 8:].reshape(E, 8, 3), x[edge_dst, 8:].reshape(E, 8, 3)], axis=1)
            y1, y2 = _sph(edge_vec)
            h = 2.0 ** 0.5 * jax.nn.relu(emb @ W1 / 10.0 ** 0.5)
            w = (h @ W2 / 16.0 ** 0.5).reshape(E, 7, MUL, MOUT)
            wa_s, wb_s, wa_g, wb_g, wc, wd, we = [w[:, i] for i in range(7)]
            s_out = PW_S * (jnp.einsum('eu,euw->ew', xs, wa_s) + INV_SQRT3 * jnp.einsum('eui,ei,euw->ew', xv, y1, wb_s))
            g_out = PW_S * (jnp.einsum('eu,euw->ew', xs, wa_g) + INV_SQRT3 * jnp.einsum('eui,ei,euw->ew', xv, y1, wb_g))
            v_out = PW_V * (INV_SQRT3 * jnp.einsum('eu,ek,euw->ewk', xs, y1, wc) + INV_SQRT3 * jnp.einsum('eui,euw->ewi', xv, wd) + jnp.einsum('eui,ea,iak,euw->ewk', xv, y2, W3J121, we))
            s_act = TANH_GAIN * jnp.tanh(s_out)
            gates = TANH_GAIN * jnp.tanh(g_out)
            edge_ftr = jnp.concatenate([s_act, (gates[:, :, None] * v_out).reshape(E, 24)], axis=1) * norm[:, None]
            return jax.ops.segment_sum(edge_ftr, edge_dst, num_segments=N)
        key = jax.random.key(seed)
        ks = jax.random.split(key, 8)
        N, E = (50000, 9375)
        return {'x': jax.random.normal(ks[0], (N, 32), jnp.float32), 'edge_src': jax.random.randint(ks[1], (E,), 0, N), 'edge_dst': jax.random.randint(ks[2], (E,), 0, N), 'edge_vec': jax.random.normal(ks[3], (E, 3), jnp.float32), 'emb': jax.random.uniform(ks[4], (E, 10), jnp.float32), 'norm': jax.random.uniform(ks[5], (E,), jnp.float32), 'W1': jax.random.normal(ks[6], (10, 16), jnp.float32), 'W2': jax.random.normal(ks[7], (16, 896), jnp.float32)}
    _L2_gnn_all = _L2_gnn_setup()
    _L2_gnn_in = {k: v for k, v in _L2_gnn_all.items() if k in ('W1', 'W2')}
    del _L2_gnn_all

    def _L3_gnn_setup():
        import jax, jax.numpy as jnp
        import numpy as np
        N, E, D, K = (3125, 50000, 32, 2)
        NEG_SLOPE = 0.01
        BN_EPS = 1e-05

        def _tag_conv(x, W, b, src, dst, ew):
            n = x.shape[0]
            out = x @ W[0]
            h = x
            for k in range(1, K + 1):
                msg = h[src] * ew[:, None]
                h = jax.ops.segment_sum(msg, dst, num_segments=n)
                out = out + h @ W[k]
            return out + b

        def _batch_norm(x, gamma, beta):
            m = jnp.mean(x, axis=0)
            v = jnp.mean(jnp.square(x - m), axis=0)
            return (x - m) * jax.lax.rsqrt(v + BN_EPS) * gamma + beta
        key = jax.random.key(seed)
        ks = jax.random.split(key, 8)
        y = jax.random.normal(ks[0], (N, D), jnp.float32)
        edge_index = jax.random.randint(ks[1], (2, E), 0, N, dtype=jnp.int32)
        edge_weight = jax.random.uniform(ks[2], (E,), jnp.float32)
        s = 1.0 / np.sqrt(D)
        W1 = jax.random.uniform(ks[3], (K + 1, D, D), jnp.float32, -s, s)
        W2 = jax.random.uniform(ks[4], (K + 1, D, D), jnp.float32, -s, s)
        bias1 = jax.random.uniform(ks[5], (D,), jnp.float32, -s, s)
        bias2 = jax.random.uniform(ks[6], (D,), jnp.float32, -s, s)
        gamma1 = jnp.ones((D,), jnp.float32)
        beta1 = jnp.zeros((D,), jnp.float32)
        gamma2 = jnp.ones((D,), jnp.float32)
        beta2 = jnp.zeros((D,), jnp.float32)
        return dict(y=y, edge_index=edge_index, edge_weight=edge_weight, W1=W1, bias1=bias1, gamma1=gamma1, beta1=beta1, W2=W2, bias2=bias2, gamma2=gamma2, beta2=beta2)
    _L3_gnn_all = _L3_gnn_setup()
    _L3_gnn_in = {k: v for k, v in _L3_gnn_all.items() if k in ('W1', 'bias1', 'gamma1', 'beta1', 'W2', 'bias2', 'gamma2', 'beta2')}
    del _L3_gnn_all
    return {'x': x, 'src': src, 'dst': dst, 'edge_attr_10': edge_attr_10, 'edge_attr_16': edge_attr_16, 'edge_attr_3': edge_attr_3, 'edge_weight': edge_weight, 'edge_weight1': edge_weight1, 'L0_gnn_W1m': _L0_gnn_in['W1m'], 'L0_gnn_b1m': _L0_gnn_in['b1m'], 'L0_gnn_W2m': _L0_gnn_in['W2m'], 'L0_gnn_b2m': _L0_gnn_in['b2m'], 'L0_gnn_W1u': _L0_gnn_in['W1u'], 'L0_gnn_b1u': _L0_gnn_in['b1u'], 'L0_gnn_W2u': _L0_gnn_in['W2u'], 'L0_gnn_b2u': _L0_gnn_in['b2u'], 'L1_gnn_Wl': _L1_gnn_in['Wl'], 'L1_gnn_bl': _L1_gnn_in['bl'], 'L1_gnn_Wr': _L1_gnn_in['Wr'], 'L1_gnn_br': _L1_gnn_in['br'], 'L1_gnn_att': _L1_gnn_in['att'], 'L1_gnn_conv_bias': _L1_gnn_in['conv_bias'], 'L1_gnn_bn_gamma': _L1_gnn_in['bn_gamma'], 'L1_gnn_bn_beta': _L1_gnn_in['bn_beta'], 'L2_gnn_W1': _L2_gnn_in['W1'], 'L2_gnn_W2': _L2_gnn_in['W2'], 'L3_gnn_W1': _L3_gnn_in['W1'], 'L3_gnn_bias1': _L3_gnn_in['bias1'], 'L3_gnn_gamma1': _L3_gnn_in['gamma1'], 'L3_gnn_beta1': _L3_gnn_in['beta1'], 'L3_gnn_W2': _L3_gnn_in['W2'], 'L3_gnn_bias2': _L3_gnn_in['bias2'], 'L3_gnn_gamma2': _L3_gnn_in['gamma2'], 'L3_gnn_beta2': _L3_gnn_in['beta2']}

def reference(x, src, dst, edge_attr_10, edge_attr_16, edge_attr_3, edge_weight, edge_weight1, L0_gnn_W1m, L0_gnn_b1m, L0_gnn_W2m, L0_gnn_b2m, L0_gnn_W1u, L0_gnn_b1u, L0_gnn_W2u, L0_gnn_b2u, L1_gnn_Wl, L1_gnn_bl, L1_gnn_Wr, L1_gnn_br, L1_gnn_att, L1_gnn_conv_bias, L1_gnn_bn_gamma, L1_gnn_bn_beta, L2_gnn_W1, L2_gnn_W2, L3_gnn_W1, L3_gnn_bias1, L3_gnn_gamma1, L3_gnn_beta1, L3_gnn_W2, L3_gnn_bias2, L3_gnn_gamma2, L3_gnn_beta2):
    import jax
    import jax.numpy as jnp

    def _L0_gnn_ref(x, degrees, edge_features, W1m, b1m, W2m, b2m, W1u, b1u, W2u, b2u, edge_index):
        import jax, jax.numpy as jnp
        import numpy as np
        N = 50000
        E = 50000
        D_IN = 32
        D_EF = 16
        D_H = 64
        D_MSG = 32
        D_UP = 32

        def mlp2(h, W1, b1, W2, b2):
            return jax.nn.relu(h @ W1 + b1) @ W2 + b2
        src = edge_index[0]
        dst = edge_index[1]
        x_i = x[dst]
        x_j = x[src]
        msg_in = jnp.concatenate([x_i, x_j, edge_features], axis=-1)
        msgs = mlp2(msg_in, W1m, b1m, W2m, b2m)
        agg = jax.ops.segment_sum(msgs, dst, num_segments=x.shape[0])
        upd_in = jnp.concatenate([x, agg], axis=-1)
        return mlp2(upd_in, W1u, b1u, W2u, b2u)

    def _L1_gnn_ref(patch_embs, edge_index, edge_attr, Wl, bl, Wr, br, att, conv_bias, bn_gamma, bn_beta):
        import jax, jax.numpy as jnp
        import numpy as np
        N = 50000
        E = 25000
        H = 8
        C = 32
        L = 3
        NEG_SLOPE = 0.2
        BN_EPS = 1e-05

        def gatv2_layer(x, Wl, bl, Wr, br, att, bias, src, dst, n):
            xl = (x @ Wl + bl).reshape(n, H, C)
            xr = (x @ Wr + br).reshape(n, H, C)
            e = jax.nn.leaky_relu(xl[src] + xr[dst], NEG_SLOPE)
            logits = jnp.einsum('ehc,hc->eh', e, att)
            m = jax.ops.segment_max(logits, dst, num_segments=n)
            m = jnp.where(jnp.isfinite(m), m, 0.0)
            p = jnp.exp(logits - jax.lax.stop_gradient(m)[dst])
            denom = jax.ops.segment_sum(p, dst, num_segments=n)
            alpha = p / (denom[dst] + 1e-16)
            out = jax.ops.segment_sum(xl[src] * alpha[:, :, None], dst, num_segments=n)
            return out.mean(axis=1) + bias

        def batchnorm_train(x, gamma, beta):
            mu = x.mean(axis=0)
            var = x.var(axis=0)
            return (x - mu) * jax.lax.rsqrt(var + BN_EPS) * gamma + beta
        n = patch_embs.shape[0]
        loops = jnp.arange(n, dtype=edge_index.dtype)
        src = jnp.concatenate([edge_index[0], loops])
        dst = jnp.concatenate([edge_index[1], loops])
        x = patch_embs
        h1 = gatv2_layer(x, Wl[0], bl[0], Wr[0], br[0], att[0], conv_bias[0], src, dst, n)
        x = batchnorm_train(jax.nn.leaky_relu(h1, 0.01) + x, bn_gamma[0], bn_beta[0])
        h2 = gatv2_layer(x, Wl[1], bl[1], Wr[1], br[1], att[1], conv_bias[1], src, dst, n)
        x = batchnorm_train(jax.nn.leaky_relu(h2, 0.01) + x, bn_gamma[1], bn_beta[1])
        h3 = gatv2_layer(x, Wl[2], bl[2], Wr[2], br[2], att[2], conv_bias[2], src, dst, n)
        x = batchnorm_train(h3 + x, bn_gamma[2], bn_beta[2])
        return x

    def _L2_gnn_ref(x, edge_src, edge_dst, edge_vec, emb, norm, W1, W2):
        import jax, jax.numpy as jnp
        import numpy as np
        MUL = 16
        MOUT = 8
        TANH_GAIN = 1.593
        INV_SQRT3 = 0.5773502691896258
        PW_S = 0.17677669529663687
        PW_V = 0.25

        def _w3j_121():
            s2, s6 = (2 ** 0.5, 6 ** 0.5)
            M = np.zeros((5, 3, 3))
            M[0, 0, 1] = M[0, 1, 0] = 1 / s2
            M[1, 1, 2] = M[1, 2, 1] = 1 / s2
            M[2] = np.diag([-1.0, -1.0, 2.0]) / s6
            M[3, 0, 2] = M[3, 2, 0] = 1 / s2
            M[4] = np.diag([1.0, -1.0, 0.0]) / s2
            return jnp.asarray(np.transpose(M, (1, 0, 2)) / 5 ** 0.5, jnp.float32)
        W3J121 = _w3j_121()

        def _sph(edge_vec):
            n = edge_vec / jnp.linalg.norm(edge_vec, axis=1, keepdims=True)
            x, y, z = (n[:, 0], n[:, 1], n[:, 2])
            y1 = 3.0 ** 0.5 * n
            s15 = 15.0 ** 0.5
            y2 = jnp.stack([s15 * x * y, s15 * y * z, 5.0 ** 0.5 / 2 * (3 * z * z - 1), s15 * x * z, s15 / 2 * (x * x - y * y)], axis=1)
            return (y1, y2)

        def _forward(x, edge_src, edge_dst, edge_vec, emb, norm, W1, W2):
            N, E = (x.shape[0], edge_src.shape[0])
            xs = jnp.concatenate([x[edge_src, :8], x[edge_dst, :8]], axis=1)
            xv = jnp.concatenate([x[edge_src, 8:].reshape(E, 8, 3), x[edge_dst, 8:].reshape(E, 8, 3)], axis=1)
            y1, y2 = _sph(edge_vec)
            h = 2.0 ** 0.5 * jax.nn.relu(emb @ W1 / 10.0 ** 0.5)
            w = (h @ W2 / 16.0 ** 0.5).reshape(E, 7, MUL, MOUT)
            wa_s, wb_s, wa_g, wb_g, wc, wd, we = [w[:, i] for i in range(7)]
            s_out = PW_S * (jnp.einsum('eu,euw->ew', xs, wa_s) + INV_SQRT3 * jnp.einsum('eui,ei,euw->ew', xv, y1, wb_s))
            g_out = PW_S * (jnp.einsum('eu,euw->ew', xs, wa_g) + INV_SQRT3 * jnp.einsum('eui,ei,euw->ew', xv, y1, wb_g))
            v_out = PW_V * (INV_SQRT3 * jnp.einsum('eu,ek,euw->ewk', xs, y1, wc) + INV_SQRT3 * jnp.einsum('eui,euw->ewi', xv, wd) + jnp.einsum('eui,ea,iak,euw->ewk', xv, y2, W3J121, we))
            s_act = TANH_GAIN * jnp.tanh(s_out)
            gates = TANH_GAIN * jnp.tanh(g_out)
            edge_ftr = jnp.concatenate([s_act, (gates[:, :, None] * v_out).reshape(E, 24)], axis=1) * norm[:, None]
            return jax.ops.segment_sum(edge_ftr, edge_dst, num_segments=N)
        return _forward(x, edge_src, edge_dst, edge_vec, emb, norm, W1, W2)

    def _L3_gnn_ref(y, edge_index, edge_weight, W1, bias1, gamma1, beta1, W2, bias2, gamma2, beta2):
        import jax, jax.numpy as jnp
        import numpy as np
        N, E, D, K = (3125, 50000, 32, 2)
        NEG_SLOPE = 0.01
        BN_EPS = 1e-05

        def _tag_conv(x, W, b, src, dst, ew):
            n = x.shape[0]
            out = x @ W[0]
            h = x
            for k in range(1, K + 1):
                msg = h[src] * ew[:, None]
                h = jax.ops.segment_sum(msg, dst, num_segments=n)
                out = out + h @ W[k]
            return out + b

        def _batch_norm(x, gamma, beta):
            m = jnp.mean(x, axis=0)
            v = jnp.mean(jnp.square(x - m), axis=0)
            return (x - m) * jax.lax.rsqrt(v + BN_EPS) * gamma + beta
        src, dst = (edge_index[0], edge_index[1])
        h = _tag_conv(y, W1, bias1, src, dst, edge_weight)
        h = jax.nn.leaky_relu(_batch_norm(h, gamma1, beta1), NEG_SLOPE)
        h = _tag_conv(h, W2, bias2, src, dst, edge_weight)
        h = jax.nn.leaky_relu(_batch_norm(h, gamma2, beta2), NEG_SLOPE)
        return h
    edge_index = jnp.stack([src, dst])
    deg = jnp.maximum(jax.ops.segment_sum(jnp.ones(dst.shape, jnp.float32), dst, num_segments=3125), 1.0)
    deg_isqrt = deg ** (-0.5)
    h = jnp.maximum(_layernorm(x, axis=-1), 0.0)
    x = x + _L0_gnn_ref(h, deg_isqrt[:, None], edge_attr_16, L0_gnn_W1m, L0_gnn_b1m, L0_gnn_W2m, L0_gnn_b2m, L0_gnn_W1u, L0_gnn_b1u, L0_gnn_W2u, L0_gnn_b2u, edge_index)
    h = jnp.maximum(_layernorm(x, axis=-1), 0.0)
    x = x + _L1_gnn_ref(h, edge_index, edge_weight1, L1_gnn_Wl, L1_gnn_bl, L1_gnn_Wr, L1_gnn_br, L1_gnn_att, L1_gnn_conv_bias, L1_gnn_bn_gamma, L1_gnn_bn_beta)
    h = jnp.maximum(_layernorm(x, axis=-1), 0.0)
    x = x + _L2_gnn_ref(h, src, dst, edge_attr_3, edge_attr_10, edge_weight, L2_gnn_W1, L2_gnn_W2)
    h = jnp.maximum(_layernorm(x, axis=-1), 0.0)
    x = x + _L3_gnn_ref(h, edge_index, edge_weight, L3_gnn_W1, L3_gnn_bias1, L3_gnn_gamma1, L3_gnn_beta1, L3_gnn_W2, L3_gnn_bias2, L3_gnn_gamma2, L3_gnn_beta2)
    return x

_drawn_inputs = setup_inputs


def setup_inputs(seed=0):
    import zlib

    import numpy as np

    out = dict(_drawn_inputs(seed))
    spreads = {'L0_gnn_b1m': (0.0, 0.1),
     'L0_gnn_b2m': (0.0, 0.1),
     'L0_gnn_b1u': (0.0, 0.471),
     'L0_gnn_b2u': (0.0, 0.1),
     'L1_gnn_bl': (0.0, 2.0),
     'L1_gnn_br': (0.0, 2.0),
     'L1_gnn_conv_bias': (0.0, 1.044),
     'L1_gnn_bn_gamma': (1.0, 0.2),
     'L1_gnn_bn_beta': (0.0, 0.1),
     'L3_gnn_gamma1': (1.0, 0.2),
     'L3_gnn_beta1': (0.0, 0.1),
     'L3_gnn_gamma2': (1.0, 0.2),
     'L3_gnn_beta2': (0.0, 0.365)}
    factors = {'edge_attr_16': 2.814, 'L1_gnn_Wr': 2.69, 'L3_gnn_bias1': 200.0, 'L3_gnn_bias2': 200.0}
    for name, (base, spread) in spreads.items():
        noise = np.random.default_rng([zlib.crc32(name.encode()), seed]).standard_normal(out[name].shape)
        drawn = base * np.exp(spread * noise) if base else spread * noise
        out[name] = jnp.asarray(drawn.astype(out[name].dtype))
    for name, factor in factors.items():
        out[name] = (out[name] * factor).astype(out[name].dtype)
    return out
```

```python
import concourse.bass as bass
from concourse import mybir
from concourse.alu_op_type import AluOpType as ALU
from contextlib import ExitStack
import numpy as np

F32, I32, BF16, U8 = mybir.dt.float32, mybir.dt.int32, mybir.dt.bfloat16, mybir.dt.uint8
ACT = mybir.ActivationFunctionType
AX = mybir.AxisListType

N, D, E = 3125, 32, 53125
PN, BN = 125, 25
R, J, W = 4, 4, 512
C = -(-E // (R * W))
RW = C * W
EP = R * RW
T = R * J
RS, SW = 16, EP // 16
H = 8
DS = D + H
SR, ZD = EP + 128 * BN, 7
BIG = 1.0e30
HALF = C // 2
CREDIT = 4
EPS = 1e-5


def went(n, back=0):
    return n + 1 + CREDIT - back


class Mem:
    pass


class Step:

    def __init__(self, nc, name):
        self.nc, self.name, self.stack, self.semaphores = nc, name, ExitStack(), []

    def __enter__(self):
        self.stack.__enter__()
        return self

    def __exit__(self, *e):
        done = self.stack.__exit__(*e)
        if self.semaphores:
            self.nc.clear_and_free_semaphores(self.semaphores)
            self.nc.all_engine_barrier()
        return done

    def sb(self, name, shape, dt=F32):
        return self.stack.enter_context(self.nc.sbuf_tensor(f"{self.name}_{name}", shape, dt))

    def ps(self, name, shape, dt=F32):
        return self.stack.enter_context(self.nc.psum_tensor(f"{self.name}_ps_{name}", shape, dt))

    def sems(self, *names):
        made = {n: self.nc.alloc_semaphore(f"{self.name}_{n}") for n in names}
        self.semaphores += made.values()
        return made

    def block(self):
        return self.stack.enter_context(self.nc.Block())


def allocate(nc, ctx, a):
    m = Mem()

    def sb(name, shape, dt):
        return ctx.enter_context(nc.sbuf_tensor(name, shape, dt))

    m.ident = sb("ident", [128, 128], F32)
    m.keep = sb("keep", [128, RW], U8)
    m.keep_pair = sb("keep_pair", [128, 2, RW], U8)
    m.src = sb("src_ids", [128, (C + 2) * T], I32)
    m.ew = sb("edge_weight_sb", [128, C * T], F32)
    m.first = sb("first_edge", [PN, BN], I32)
    m.last = sb("last_edge", [PN, BN], I32)
    m.some = sb("some_edges", [PN, BN], F32)
    m.cross = sb("crosses", [PN, R - 1, BN], F32)
    m.range_dst = sb("range_dst", [R, 1], I32)
    m.x = sb("x_nodes", [PN, BN * D], F32)
    m.h = sb("h_nodes", [PN, BN * D], F32)
    m.h_self = sb("h_self_nodes", [PN, BN, DS], F32)
    m.agg = sb("agg_nodes", [PN, BN * D], F32)
    m.rows = sb("last_rows", [PN, BN, D], F32)
    m.ones = sb("ones_over_n", [PN, PN], F32)
    m.table = nc.dram_tensor("node_table", [N, D], F32).ap()
    m.starts = nc.dram_tensor("starts_dram", [SR, DS], F32).ap()
    m.wide = nc.dram_tensor("node_wide_table", [N, DS], F32).ap()
    m.sums = nc.dram_tensor("sums_dram", [EP, D], F32).ap()
    m.sums_chunks = m.sums.rearrange("(r c p j) f -> c p r (j f)", r=R, c=C, p=128, j=J)
    m.starts_chunks = m.starts[0:EP, :].rearrange("(r c p j) f -> c p j r f", r=R, c=C, p=128, j=J)[..., 0:D]
    m.self_chunks = m.starts[0:EP, :].rearrange("(r c p j) f -> c p j r f", r=R, c=C, p=128, j=J)[..., D:DS]
    m.a = a
    return m


def link(eng, sem, count, ins):
    count[0] += 1
    ins.then_inc(sem, 1)
    eng.wait_ge(sem, count[0])


def graph_step(nc, m):
    a = m.a
    QW = RW // 4
    with Step(nc, "graph") as st:
        sb = st.sb
        s = st.sems("consts_made", "dst_loaded", "small_loaded", "run_loaded0", "run_loaded1", "prep",
                 "onehots_made", "counted", "keep_made", "tot_ready", "base_ready", "zero_made", "zero_stored",
                 "pair_copied", "src_loaded", "chain")
        run = [sb(f"dst_run{k}", [128, QW + 1], I32) for k in range(2)]
        dst = sb("dst_ids", [128, C * T], I32)
        dstf = sb("dst_f", [128, C * T], F32)
        hi = sb("dst_hi", [128, C * T], F32)
        lo = sb("dst_lo", [128, C * T], F32)
        iota_i = sb("iota_i", [128, PN], I32)
        iota = sb("iota_f", [128, PN], F32)
        node_i = sb("node_i", [PN, BN], I32)
        node = sb("node_f", [PN, BN], F32)
        upper = sb("upper", [PN, PN], F32)
        oh_hi = sb("oh_hi", [128, 2, T, PN], BF16)
        oh_lo = sb("oh_lo", [128, 2, T, BN], BF16)
        zeros = sb("zeros", [128, SR * DS // (128 * ZD)], F32)
        cnt = sb("cnt", [PN, BN], F32)
        incl = sb("incl", [PN, BN], F32)
        fst = sb("fst", [PN, BN], F32)
        lst = sb("lst", [PN, BN], F32)
        tmp = sb("tmp", [PN, BN], F32)
        tmp2 = sb("tmp2", [PN, BN], F32)
        base = sb("base", [PN, 1], F32)
        ps_cnt = st.ps("ps_cnt", [PN, BN], F32)
        ps_base = st.ps("ps_base", [PN, 1], F32)
        block = st.block()

        @block.sync
        def _(sp):
            sp.dma_start(dst[:, :], a.dst_t).then_inc(s["dst_loaded"], 16)
            sp.dma_start(m.src[:, 0:C * T], a.src_t).then_inc(s["src_loaded"], 16)
            sp.dma_start(m.ew[:, :], a.ew_t).then_inc(s["small_loaded"], 16)
            sp.dma_start(m.x[:, :], a.x.rearrange("(p b) f -> p (b f)", b=BN)).then_inc(s["small_loaded"], 16)
            sp.dma_start(m.range_dst[:, :], a.dst_ext[1:1 + EP].rearrange("(r e) -> r e", r=R)[:, 0:1],
                         allow_slow_non_contiguous=True).then_inc(s["small_loaded"], 16)
            for q in range(4):
                if q >= 2:
                    sp.wait_ge(s["keep_made"], q)
                for r in range(R):
                    sp.dma_start(run[q % 2][32 * r:32 * r + 32, :],
                                 a.dst_ext[r * RW + q * QW:r * RW + q * QW + QW + 1].partition_broadcast(32))\
                      .then_inc(s["run_loaded0" if q % 2 == 0 else "run_loaded1"], 16)
            sp.wait_ge(s["zero_made"], 1)
            blank = m.starts.rearrange("(p z a) b -> p z (a b)", p=128, z=ZD)
            for z in range(ZD):
                sp.dma_start(blank[:, z, :], zeros[:, :]).then_inc(s["zero_stored"], 16)
            sp.wait_ge(s["keep_made"], 5)
            for q in range(2):
                for rr in range(2):
                    r = 2 * q + rr
                    sp.dma_start(m.keep_pair[64 * rr + 32:64 * rr + 64, q, :], m.keep[32 * r:32 * r + 32, :])\
                      .then_inc(s["pair_copied"], 16)
            sp.wait_ge(s["pair_copied"], 64)
            sp.wait_ge(s["zero_stored"], 16 * ZD)
            sp.wait_ge(s["small_loaded"], 48)
            sp.wait_ge(s["src_loaded"], 16)

        @block.gpsimd
        def _(pool):
            pool.memset(m.ident[:, :], 0.0).then_inc(s["prep"], 1)
            pool.memset(upper[:, :], 1.0).then_inc(s["prep"], 1)
            pool.memset(m.ones[:, :], 1.0 / N)
            pool.memset(m.src[:, C * T:], 0)
            pool.memset(zeros[:, :], 0.0).then_inc(s["zero_made"], 1)
            pool.iota(iota_i[:, :], [[1, PN]], base=0, channel_multiplier=0)
            pool.iota(node_i[:, :], [[1, BN]], base=0, channel_multiplier=BN)
            pool.wait_ge(s["prep"], 2)
            pool.affine_select(out=m.ident[:, :], in_=m.ident[:, :], compare_op=ALU.not_equal, fill=1.0, base=0,
                               pattern=[[-1, 128]], channel_multiplier=1)
            pool.affine_select(out=upper[:, :], in_=upper[:, :], compare_op=ALU.is_gt, fill=0.0, base=0,
                               pattern=[[1, PN]], channel_multiplier=-1).then_inc(s["consts_made"], 1)

        @block.vector
        def _(dve):
            n = [0]
            dve.sem_inc(s["onehots_made"], CREDIT)
            dve.memset(m.h_self[:, :, :], 0.0)
            dve.wait_ge(s["dst_loaded"], 16)
            dve.wait_ge(s["consts_made"], 1)
            dve.tensor_copy(iota[:, :], iota_i[:, :])
            dve.tensor_copy(node[:, :], node_i[:, :])
            link(dve, s["chain"], n, dve.tensor_copy(dstf[:, :], dst[:, :]))
            link(dve, s["chain"], n, dve.tensor_scalar(hi[:, :], dstf[:, :], 1.0 / BN, 0.48, ALU.mult, ALU.subtract))
            link(dve, s["chain"], n, dve.tensor_scalar(hi[:, :], hi[:, :], 12582912.0, None, ALU.add))
            link(dve, s["chain"], n, dve.tensor_scalar(hi[:, :], hi[:, :], 12582912.0, None, ALU.subtract))
            link(dve, s["chain"], n, dve.scalar_tensor_tensor(lo[:, :], hi[:, :], -float(BN), dstf[:, :], ALU.mult, ALU.add))

            def onehots(c, k):
                dve.wait_ge(s["counted"], went(c, 2))
                dve.tensor_tensor(oh_hi[:, k, :, :], iota[:, :].unsqueeze(1).broadcast_to([128, T, PN]),
                                  hi[:, bass.ds(c * T, T)].unsqueeze(2).broadcast_to([128, T, PN]), ALU.is_equal)
                dve.tensor_tensor(oh_lo[:, k, :, :], iota[:, 0:BN].unsqueeze(1).broadcast_to([128, T, BN]),
                                  lo[:, bass.ds(c * T, T)].unsqueeze(2).broadcast_to([128, T, BN]), ALU.is_equal)\
                   .then_inc(s["onehots_made"], 1)

            with dve.Fori(0, HALF) as i:
                for k in range(2):
                    onehots(i * 2 + k, k)

            dve.memset(m.keep_pair[:, :, :], 0).then_inc(s["keep_made"], 1)
            for q in range(4):
                dve.wait_ge(s["run_loaded0" if q % 2 == 0 else "run_loaded1"], 64 * (q // 2 + 1))
                dve.tensor_tensor(m.keep[:, q * QW:(q + 1) * QW], run[q % 2][:, 1:QW + 1], run[q % 2][:, 0:QW],
                                  ALU.is_equal).then_inc(s["keep_made"], 1)

            dve.wait_ge(s["counted"], went(C))
            link(dve, s["chain"], n, dve.tensor_copy(cnt[:, :], ps_cnt[:, :]))
            link(dve, s["chain"], n, dve.memset(tmp[:, :], 1.0))
            link(dve, s["chain"], n, dve.tensor_tensor_scan(incl[:, :], tmp[:, :], cnt[:, :], 0.0, ALU.mult, ALU.add))
            dve.sem_inc(s["tot_ready"], 1)
            dve.wait_ge(s["base_ready"], 1)
            link(dve, s["chain"], n, dve.tensor_copy(base[:, :], ps_base[:, :]))
            link(dve, s["chain"], n, dve.tensor_scalar(lst[:, :], incl[:, :], base[:, 0:1], 1.0, ALU.add, ALU.subtract))
            link(dve, s["chain"], n, dve.scalar_tensor_tensor(fst[:, :], lst[:, :], 1.0, cnt[:, :], ALU.add, ALU.subtract))
            link(dve, s["chain"], n, dve.tensor_scalar(m.some[:, :], cnt[:, :], 1.0, None, ALU.min))
            for r in range(1, R):
                link(dve, s["chain"], n, dve.tensor_scalar(tmp[:, :], fst[:, :], float(r * RW), None, ALU.is_lt))
                link(dve, s["chain"], n, dve.tensor_scalar(tmp2[:, :], lst[:, :], float(r * RW), None, ALU.is_ge))
                link(dve, s["chain"], n, dve.tensor_tensor(m.cross[:, r - 1, :], tmp[:, :], tmp2[:, :], ALU.mult))
            link(dve, s["chain"], n, dve.tensor_scalar(m.last[:, :], lst[:, :], 0.0, None, ALU.max))
            link(dve, s["chain"], n, dve.scalar_tensor_tensor(tmp[:, :], node[:, :], float(EP), fst[:, :], ALU.add, ALU.subtract))
            link(dve, s["chain"], n, dve.tensor_scalar(tmp2[:, :], m.some[:, :], -1.0, 1.0, ALU.mult, ALU.add))
            link(dve, s["chain"], n, dve.tensor_tensor(tmp[:, :], tmp[:, :], tmp2[:, :], ALU.mult))
            link(dve, s["chain"], n, dve.tensor_tensor(m.first[:, :], tmp[:, :], fst[:, :], ALU.add))

        @block.tensor
        def _(pe):
            pe.sem_inc(s["counted"], CREDIT)
            pe.wait_ge(s["zero_made"], 1)
            pe.wait_ge(s["onehots_made"], went(0))
            pe.matmul(ps_cnt[:, :], zeros[:, 0:PN], zeros[:, 0:BN], start=True, stop=False)
            with pe.Fori(0, HALF) as i:
                for k in range(2):
                    pe.wait_ge(s["onehots_made"], went(i * 2 + k))
                    for t in range(T):
                        last = pe.matmul(ps_cnt[:, :], oh_hi[:, k, t, :], oh_lo[:, k, t, :], start=False, stop=False)
                    last.then_inc(s["counted"], 1)
            pe.matmul(ps_cnt[:, :], zeros[:, 0:PN], zeros[:, 0:BN], start=False, stop=True).then_inc(s["counted"], 1)
            pe.wait_ge(s["tot_ready"], 1)
            pe.wait_ge(s["consts_made"], 1)
            pe.matmul(ps_base[:, :], upper[:, :], incl[:, BN - 1:BN], start=True, stop=True).then_inc(s["base_ready"], 1)


def norm_step(nc, m, name):
    with Step(nc, name) as st:
        s = st.sems("chain", "var_ready", "std_ready")
        tmp = st.sb("tmp", [PN, BN * D])
        mean = st.sb("mean", [PN, BN])
        var = st.sb("var", [PN, BN])
        block = st.block()

        @block.vector
        def _(dve):
            n = [0]

            def step(ins):
                link(dve, s["chain"], n, ins)

            x3 = m.x[:, :].rearrange("p (b f) -> p b f", f=D)
            t3 = tmp[:, :].rearrange("p (b f) -> p b f", f=D)
            o3 = m.h[:, :].rearrange("p (b f) -> p b f", f=D)
            step(dve.tensor_reduce(mean[:, :], x3, AX.X, ALU.add))
            step(dve.tensor_scalar(mean[:, :], mean[:, :], 1.0 / D, None, ALU.mult))
            step(dve.tensor_tensor(o3, x3, mean[:, :].unsqueeze(2).broadcast_to([PN, BN, D]), ALU.subtract))
            step(dve.tensor_tensor(t3, o3, o3, ALU.mult))
            step(dve.tensor_reduce(var[:, :], t3, AX.X, ALU.add))
            dve.tensor_scalar(var[:, :], var[:, :], 1.0 / D, EPS, ALU.mult, ALU.add).then_inc(s["var_ready"], 1)
            dve.wait_ge(s["std_ready"], 1)
            step(dve.reciprocal(var[:, :], var[:, :]))
            step(dve.tensor_tensor(t3, o3, var[:, :].unsqueeze(2).broadcast_to([PN, BN, D]), ALU.mult))
            step(dve.tensor_scalar(m.h[:, :], tmp[:, :], 0.0, None, ALU.max))

        @block.scalar
        def _(act):
            act.wait_ge(s["var_ready"], 1)
            act.activation(var[:, :], var[:, :], ACT.Sqrt).then_inc(s["std_ready"], 1)


def publish_step(nc, m, name):
    with Step(nc, name) as st:
        s = st.sems("rows_ready", "table_stored", "rows_scattered", "border_rows", "border_stored")
        border = st.sb("border", [R, DS])
        block = st.block()

        @block.vector
        def _(dve):
            dve.tensor_copy(m.h_self[:, :, 0:D], m.h[:, :].rearrange("p (b f) -> p b f", f=D)).then_inc(s["rows_ready"], 1)

        @block.sync
        def _(sp):
            sp.dma_start(m.table.rearrange("(p b) f -> p (b f)", b=BN), m.h[:, :]).then_inc(s["table_stored"], 16)
            sp.wait_ge(s["rows_ready"], 1)
            sp.dma_start(m.wide.rearrange("(p b) f -> p (b f)", b=BN), m.h_self[:, :, :].rearrange("p b f -> p (b f)"))\
              .then_inc(s["table_stored"], 16)
            sp.wait_ge(s["table_stored"], 32)
            sp.wait_ge(s["rows_scattered"], 16 * BN)
            sp.wait_ge(s["border_rows"], 16)
            sp.dma_start(m.starts[0:EP, :].rearrange("(r e) f -> r e f", r=R)[:, 0, :], border[:, :])\
              .then_inc(s["border_stored"], 16)
            sp.wait_ge(s["border_stored"], 16)

        @block.gpsimd
        def _(pool):
            pool.wait_ge(s["rows_ready"], 1)
            for b in range(BN):
                pool.indirect_dma_start(m.starts, bass.IndirectOffsetOnAxis(ap=m.first[:, b:b + 1], axis=0),
                                        m.h_self[:, b, :], None).then_inc(s["rows_scattered"], 16)
            pool.wait_ge(s["table_stored"], 32)
            pool.indirect_dma_start(border[:, :], None, m.wide,
                                    bass.IndirectOffsetOnAxis(ap=m.range_dst[:, 0:1], axis=0))\
                .then_inc(s["border_rows"], 16)
            pool.wait_ge(s["border_rows"], 16)


def collect_step(nc, m, name, sums, rows, to=None):
    width = rows.shape[2]
    with Step(nc, name) as st:
        s = st.sems("chain", "border_loaded", "rows_gathered")
        tmp = st.sb("tmp", [PN, BN, D])
        edge = st.sb("edge", [PN, R - 1, D])
        block = st.block()

        @block.sync
        def _(sp):
            for r in range(1, R):
                sp.dma_start(edge[:, r - 1, :], sums[r * RW - 1, 0:D].partition_broadcast(PN))\
                  .then_inc(s["border_loaded"], 16)
            sp.wait_ge(s["border_loaded"], 16 * (R - 1))

        @block.gpsimd
        def _(pool):
            for b in range(BN):
                pool.indirect_dma_start(rows[:, b, :], None, sums,
                                        bass.IndirectOffsetOnAxis(ap=m.last[:, b:b + 1], axis=0))\
                    .then_inc(s["rows_gathered"], 16)
            pool.wait_ge(s["rows_gathered"], 16 * BN)

        @block.vector
        def _(dve):
            n = [0]
            a3 = m.agg[:, :].rearrange("p (b f) -> p b f", f=D) if to is None else to
            dve.wait_ge(s["rows_gathered"], 16 * BN)
            dve.wait_ge(s["border_loaded"], 16 * (R - 1))
            link(dve, s["chain"], n, dve.tensor_tensor(a3, rows[:, :, 0:D], m.some[:, :].unsqueeze(2).broadcast_to([PN, BN, D]), ALU.mult))
            for r in range(R - 1):
                link(dve, s["chain"], n, dve.tensor_tensor(
                    tmp[:, :, :], m.cross[:, r, :].unsqueeze(2).broadcast_to([PN, BN, D]),
                    edge[:, r, :].unsqueeze(1).broadcast_to([PN, BN, D]), ALU.mult))
                link(dve, s["chain"], n, dve.tensor_tensor(a3, a3, tmp[:, :, :], ALU.add))


def front_sems():
    return ["ids_copied", "src_rows0", "src_rows1", "dst_rows0", "dst_rows1", "rows_transposed", "x_scanned",
            "pool_turn"]


def gather_sources(pool, m, s, rows, ids, c, k, i):
    pool.wait_ge(s["rows_transposed"], went(c, 2))
    pool.wait_ge(s["ids_copied"], went(c))
    pool.sem_inc(s["pool_turn"], 1)
    alone = len(rows[k].shape) == 4
    for j in range(J):
        for r in range(R):
            pool.indirect_dma_start(rows[k][:, j, r, :] if alone else rows[k][:, j, r, 0, :], None, m.table,
                                    bass.IndirectOffsetOnAxis(ap=ids[k][:, j * R + r:j * R + r + 1], axis=0))\
                .then_inc(s[f"src_rows{k}"], 16)


def copy_ids(act, m, s, ids, c, k):
    act.wait_ge(s["rows_transposed"], went(c, 2))
    act.activation(ids[k][:, :], m.src[:, bass.ds(c * T, T)], ACT.Copy).then_inc(s["ids_copied"], 1)


def load_starts(sp, m, s, rows, c, k):
    sp.wait_ge(s["rows_transposed"], went(c, 2))
    for j in range(J):
        sp.dma_start(rows[k][:, j, :, 1, :], m.starts_chunks[c, :, j, :, :]).then_inc(s[f"dst_rows{k}"], 16)


def transpose_rows(pe, m, s, rows, ps_x, c, k, i):
    pe.wait_ge(s[f"src_rows{k}"], (i + 1) * (16 * T))
    pe.wait_ge(s[f"dst_rows{k}"], (i + 1) * (16 * J))
    pe.wait_ge(s["x_scanned"], went(c, 1))
    for q in range(2):
        for j in range(J):
            last = pe.transpose(ps_x[:, q, j::J], rows[k][:, j, 2 * q:2 * q + 2, :, :], m.ident[:, :])
    last.then_inc(s["rows_transposed"], 1)


def scan_rows(dve, m, s, ps_x, xt, c, k):
    dve.wait_ge(s["rows_transposed"], went(c))
    dve.wait_ge(s["x_scanned"], went(c, 1))
    dve.tensor_tensor_scan(xt[k][:, 0, :], m.keep_pair[:, 0, bass.ds(c * W, W)], ps_x[:, 0, :],
                           xt[1 - k][:, 0, W - 1:W], ALU.mult, ALU.add)
    dve.tensor_tensor_scan(xt[k][:, 1, :], m.keep_pair[:, 1, bass.ds(c * W, W)], ps_x[:, 1, :],
                           xt[1 - k][:, 1, W - 1:W], ALU.mult, ALU.add).then_inc(s["x_scanned"], 1)


def tail_sems():
    return ["msg_ready", "msg_scanned", "sums_transposed", "sums_copied", "sums_stored0", "sums_stored1", "out_free"]


def scan_messages(dve, m, s, msg, sc, c, k, ready):
    dve.wait_ge(s[ready], went(c))
    dve.wait_ge(s["sums_transposed"], went(c, 2))
    dve.wait_ge(s["msg_scanned"], went(c, 1))
    dve.tensor_tensor_scan(sc[k][:, :], m.keep[:, bass.ds(c * W, W)], msg, sc[1 - k][:, W - 1:W],
                           ALU.mult, ALU.add).then_inc(s["msg_scanned"], 1)


def transpose_sums(pe, m, s, sc, ps_s, c, k):
    pe.wait_ge(s["msg_scanned"], went(c))
    pe.wait_ge(s["sums_copied"], went(c, 1))
    for j in range(J):
        last = pe.transpose(ps_s[:, j, :], sc[k][:, j::J], m.ident[:, :])
    last.then_inc(s["sums_transposed"], 1)


def copy_sums(act, s, ps_s, ob, c, k):
    act.wait_ge(s["sums_transposed"], went(c))
    act.wait_ge(s["out_free"], went(c, 2))
    act.activation(ob[k][:, :].rearrange("p (r j f) -> p j r f", r=R, j=J),
                   ps_s[:, :, :].rearrange("p j (r f) -> p j r f", r=R), ACT.Copy).then_inc(s["sums_copied"], 1)


def store_sums(sp, m, s, ob, c, k, i):
    sp.wait_ge(s["sums_copied"], went(c))
    sp.dma_start(m.sums_chunks[c], ob[k][:, :].rearrange("p (r n) -> p r n", r=R)).then_inc(s[f"sums_stored{k}"], 16)
    sp.wait_ge(s[f"sums_stored{k}"], (i + 1) * 16)
    sp.sem_inc(s["out_free"], 1)


def grant(eng, s, *names):
    for n in names:
        eng.sem_inc(s[n], CREDIT)


def mp_edges_step(nc, m):
    a = m.a
    with Step(nc, "mp_edges") as st:
        sb = st.sb
        ps = st.ps
        s = st.sems(*front_sems(), *tail_sems(), "w_zeroed", "w_loaded", "ef_loaded0", "ef_loaded1",
                 "hidden_ready", "msg_made", "state_zeroed", "x_used")
        rows = [sb(f"rows{k}", [128, J, R, 2, D]) for k in range(2)]
        ids = [sb(f"ids{k}", [128, T], I32) for k in range(2)]
        xt = [sb(f"xt{k}", [128, 2, W]) for k in range(2)]
        ef = [sb(f"ef{k}", [R * 16, W]) for k in range(2)]
        hid = [sb(f"hid{k}", [128, 2, W]) for k in range(2)]
        msg = [sb(f"msg{k}", [128, W]) for k in range(2)]
        sc = [sb(f"sc{k}", [128, W]) for k in range(2)]
        ob = [sb(f"ob{k}", [128, R * J * D]) for k in range(2)]
        w1x = sb("w1x", [128, 2 * 64])
        w1e = sb("w1e", [R * 16, 2, 2 * 64])
        w2 = sb("w2m", [128, 2, 128])
        b1 = sb("b1m", [128, 1])
        b2 = sb("b2m", [128, 1])
        ps_x = ps("ps_x", [128, 2, W])
        ps_u = ps("ps_u", [128, 2, W])
        ps_m = ps("ps_m", [128, W])
        ps_s = ps("ps_s", [128, J, 128])
        block = st.block()
        n_w = 4 + 4 + 4 + 2 + 4

        @block.sync
        def _(sp):
            grant(sp, s, "out_free")
            for c in range(2):
                load_starts(sp, m, s, rows, c, c)
                sp.dma_start(ef[c][:, :], a.ef_t[:, c * W:(c + 1) * W]).then_inc(s[f"ef_loaded{c}"], 16)
            sp.wait_ge(s["w_zeroed"], 1)
            for rr in range(2):
                for sd in range(2):
                    sp.dma_start(w1x[64 * rr + 32 * sd:64 * rr + 32 * sd + 32, 64 * rr:64 * rr + 64],
                                 a.W1m[32 * (1 - sd):32 * (1 - sd) + 32, :]).then_inc(s["w_loaded"], 16)
                sp.dma_start(b1[64 * rr:64 * rr + 64, :], a.b1m.unsqueeze(1), allow_slow_non_contiguous=True).then_inc(s["w_loaded"], 16)
            for r in range(R):
                q, rr = r // 2, r % 2
                sp.dma_start(w1e[16 * r:16 * r + 16, q, 64 * rr:64 * rr + 64], a.W1m[64:80, :]).then_inc(s["w_loaded"], 16)
                sp.dma_start(w2[64 * rr:64 * rr + 64, q, 32 * r:32 * r + 32], a.W2m).then_inc(s["w_loaded"], 16)
                sp.dma_start(b2[32 * r:32 * r + 32, :], a.b2m.unsqueeze(1), allow_slow_non_contiguous=True).then_inc(s["w_loaded"], 16)

            def load(c, k):
                load_starts(sp, m, s, rows, c, k)
                sp.wait_ge(s["x_used"], went(c, 2))
                sp.dma_start(ef[k][:, :], a.ef_t[:, bass.ds(c * W, W)]).then_inc(s[f"ef_loaded{k}"], 16)

            with sp.Fori(0, HALF - 1) as i:
                for k in range(2):
                    load(i * 2 + k + 2, k)
                    store_sums(sp, m, s, ob, i * 2 + k, k, i)
            for k in range(2):
                store_sums(sp, m, s, ob, C - 2 + k, k, HALF - 1)

        @block.gpsimd
        def _(pool):
            pool.memset(w1x[:, :], 0.0)
            pool.memset(w1e[:, :, :], 0.0)
            pool.memset(w2[:, :, :], 0.0).then_inc(s["w_zeroed"], 1)
            with pool.Fori(0, HALF) as i:
                for k in range(2):
                    gather_sources(pool, m, s, rows, ids, i * 2 + k, k, i)

        @block.scalar
        def _(act):
            grant(act, s, "ids_copied", "hidden_ready", "msg_ready", "sums_copied")
            for k in range(2):
                copy_ids(act, m, s, ids, k, k)
            act.wait_ge(s["w_loaded"], 16 * n_w)
            with act.Fori(0, HALF) as i:
                for k in range(2):
                    c = i * 2 + k
                    copy_ids(act, m, s, ids, c + 2, k)
                    act.wait_ge(s["x_used"], went(c))
                    act.wait_ge(s["msg_made"], went(c, 2))
                    for q in range(2):
                        last = act.activation(hid[k][:, q, :], ps_u[:, q, :], ACT.Relu, bias=b1[:, 0:1])
                    last.then_inc(s["hidden_ready"], 1)
                    act.wait_ge(s["msg_made"], went(c))
                    act.wait_ge(s["msg_scanned"], went(c, 2))
                    act.activation(msg[k][:, :], ps_m[:, :], ACT.Identity, bias=b2[:, 0:1]).then_inc(s["msg_ready"], 1)
                    copy_sums(act, s, ps_s, ob, c, k)

        @block.tensor
        def _(pe):
            grant(pe, s, "rows_transposed", "x_used", "msg_made", "sums_transposed")
            pe.wait_ge(s["w_loaded"], 16 * n_w)
            with pe.Fori(0, HALF) as i:
                for k in range(2):
                    c = i * 2 + k
                    transpose_rows(pe, m, s, rows, ps_x, c, k, i)
                    pe.wait_ge(s["x_scanned"], went(c))
                    pe.wait_ge(s[f"ef_loaded{k}"], (i + 1) * 16)
                    pe.wait_ge(s["hidden_ready"], went(c, 1))
                    for q in range(2):
                        pe.matmul(ps_u[:, q, :], w1x[:, :], xt[k][:, q, :], start=True, stop=False)
                        last = pe.matmul(ps_u[:, q, :], w1e[:, q, :], ef[k][:, :], start=False, stop=True)
                    last.then_inc(s["x_used"], 1)
                    pe.wait_ge(s["hidden_ready"], went(c))
                    pe.wait_ge(s["msg_ready"], went(c, 1))
                    pe.matmul(ps_m[:, :], w2[:, 0, :], hid[k][:, 0, :], start=True, stop=False)
                    pe.matmul(ps_m[:, :], w2[:, 1, :], hid[k][:, 1, :], start=False, stop=True).then_inc(s["msg_made"], 1)
                    transpose_sums(pe, m, s, sc, ps_s, c, k)

        @block.vector
        def _(dve):
            grant(dve, s, "x_scanned", "msg_scanned")
            dve.memset(xt[1][:, :, :], 0.0).then_inc(s["state_zeroed"], 1)
            dve.memset(sc[1][:, :], 0.0).then_inc(s["state_zeroed"], 1)
            dve.wait_ge(s["state_zeroed"], 2)
            with dve.Fori(0, HALF) as i:
                for k in range(2):
                    c = i * 2 + k
                    dve.wait_ge(s["x_used"], went(c, 2))
                    scan_rows(dve, m, s, ps_x, xt, c, k)
                    scan_messages(dve, m, s, msg[k][:, :], sc, c, k, "msg_ready")


def mp_update_step(nc, m):
    a = m.a
    GB = 4
    with Step(nc, "mp_update") as st:
        sb = st.sb
        ps = st.ps
        s = st.sems("w_loaded", "joined", "transposed", "copied", "hidden_made", "hidden_ready", "out_made", "added", "bias_added")
        both = sb("both", [PN, BN, 2 * D])
        bt = sb("both_t", [2 * D, BN, PN])
        hid = sb("hid_u", [64, BN, PN])
        w1 = sb("w1u", [64, 64])
        w2 = sb("w2u", [64, D])
        b1 = sb("b1u", [64, 1])
        b2 = sb("b2u", [PN, D])
        ps_t = ps("ps_t", [64, 2, GB, 128])
        ps_h = ps("ps_h", [64, 2, GB * PN + 12])
        ps_o = ps("ps_o", [PN, 2, 512])
        groups = [list(range(g, min(g + GB, BN))) for g in range(0, BN, GB)]
        block = st.block()

        @block.sync
        def _(sp):
            sp.dma_start(w1[:, :], a.W1u).then_inc(s["w_loaded"], 16)
            sp.dma_start(w2[:, :], a.W2u).then_inc(s["w_loaded"], 16)
            sp.dma_start(b1[:, :], a.b1u.unsqueeze(1), allow_slow_non_contiguous=True).then_inc(s["w_loaded"], 16)
            sp.dma_start(b2[:, :], a.b2u.partition_broadcast(PN)).then_inc(s["w_loaded"], 16)

        @block.vector
        def _(dve):
            dve.tensor_copy(both[:, :, 0:D], m.h[:, :].rearrange("p (b f) -> p b f", f=D))
            dve.tensor_copy(both[:, :, D:2 * D], m.agg[:, :].rearrange("p (b f) -> p b f", f=D)).then_inc(s["joined"], 1)
            for g, bs in enumerate(groups):
                dve.wait_ge(s["transposed"], g + 1)
                dve.tensor_copy(bt[:, bs[0]:bs[-1] + 1, :], ps_t[:, g % 2, 0:len(bs), 0:PN]).then_inc(s["copied"], 1)
            dve.wait_ge(s["w_loaded"], 64)
            x3 = m.x[:, :].rearrange("p (b f) -> p b f", f=D)
            dve.tensor_tensor(x3, x3, b2[:, :].unsqueeze(1).broadcast_to([PN, BN, D]), ALU.add).then_inc(s["bias_added"], 1)
            dve.wait_ge(s["bias_added"], 1)
            dve.wait_ge(s["out_made"], 1)
            dve.tensor_tensor(m.x[:, 0:512], m.x[:, 0:512], ps_o[:, 0, :], ALU.add)
            dve.tensor_tensor(m.x[:, 512:800], m.x[:, 512:800], ps_o[:, 1, 0:288], ALU.add).then_inc(s["added"], 1)

        @block.scalar
        def _(act):
            act.wait_ge(s["w_loaded"], 64)
            for g, bs in enumerate(groups):
                act.wait_ge(s["hidden_made"], g + 1)
                act.activation(hid[:, bs[0]:bs[-1] + 1, :],
                               ps_h[:, g % 2, 0:len(bs) * PN].rearrange("p (b n) -> p b n", n=PN), ACT.Relu,
                               bias=b1[:, 0:1]).then_inc(s["hidden_ready"], 1)

        @block.tensor
        def _(pe):
            pe.wait_ge(s["joined"], 1)
            pe.wait_ge(s["w_loaded"], 64)
            for g, bs in enumerate(groups):
                if g >= 2:
                    pe.wait_ge(s["copied"], g - 1)
                for t, b in enumerate(bs):
                    last = pe.transpose(ps_t[:, g % 2, t, 0:PN], both[:, b, :], m.ident[0:PN, 0:PN])
                last.then_inc(s["transposed"], 1)
                pe.wait_ge(s["copied"], g + 1)
                if g >= 2:
                    pe.wait_ge(s["hidden_ready"], g - 1)
                pe.matmul(ps_h[:, g % 2, 0:len(bs) * PN], w1[:, :], bt[:, bs[0]:bs[-1] + 1, :], start=True, stop=True)\
                  .then_inc(s["hidden_made"], 1)
            pe.wait_ge(s["hidden_ready"], len(groups))
            for b in range(BN):
                last = pe.matmul(ps_o[:, b // 16, (b % 16) * D:(b % 16) * D + D], hid[:, b, :], w2[:, :],
                                 start=True, stop=True)
            last.then_inc(s["out_made"], 1)


BA = 13


def bn_sems():
    return ["chain", "stat_in", "stat_out", "bn_var", "bn_std"]


def bn_memory(st):
    return dict(sq=st.sb("bn_sq", [PN, BN * D]), part=st.sb("bn_part", [PN, 2, D]), mean=st.sb("bn_mean", [PN, D]),
                rstd=st.sb("bn_rstd", [PN, D]), ps=st.ps("bn_ps", [PN, 2, 512]))


def bn_dve(dve, s, n, b, y, out, gamma, beta):
    y3 = y[:, :].rearrange("p (b f) -> p b f", f=D)
    o3 = out[:, :].rearrange("p (b f) -> p b f", f=D)

    def over_nodes(turn, to):
        dve.sem_inc(s["stat_in"], 1)
        dve.wait_ge(s["stat_out"], turn)
        dve.tensor_reduce(b["part"][:, 0, :], b["ps"][:, 0, 0:BA * D].rearrange("p (b f) -> p f b", f=D), AX.X, ALU.add)
        link(dve, s["chain"], n, dve.tensor_reduce(
            b["part"][:, 1, :], b["ps"][:, 1, 0:(BN - BA) * D].rearrange("p (b f) -> p f b", f=D), AX.X, ALU.add))
        link(dve, s["chain"], n, dve.tensor_tensor(to[:, :], b["part"][:, 0, :], b["part"][:, 1, :], ALU.add))

    over_nodes(1, b["mean"])
    link(dve, s["chain"], n, dve.tensor_tensor(y3, y3, b["mean"][:, :].unsqueeze(1).broadcast_to([PN, BN, D]), ALU.subtract))
    link(dve, s["chain"], n, dve.tensor_tensor(b["sq"][:, :], y[:, :], y[:, :], ALU.mult))
    over_nodes(2, b["rstd"])
    dve.tensor_scalar(b["rstd"][:, :], b["rstd"][:, :], EPS, None, ALU.add).then_inc(s["bn_var"], 1)
    dve.wait_ge(s["bn_std"], 1)
    link(dve, s["chain"], n, dve.reciprocal(b["rstd"][:, :], b["rstd"][:, :]))
    link(dve, s["chain"], n, dve.tensor_tensor(b["rstd"][:, :], b["rstd"][:, :], gamma[:, :], ALU.mult))
    link(dve, s["chain"], n, dve.tensor_tensor(y3, y3, b["rstd"][:, :].unsqueeze(1).broadcast_to([PN, BN, D]), ALU.mult))
    link(dve, s["chain"], n, dve.tensor_tensor(o3, y3, beta[:, :].unsqueeze(1).broadcast_to([PN, BN, D]), ALU.add))


def bn_pe(pe, m, s, b, y):
    for turn, v in enumerate((y, b["sq"])):
        pe.wait_ge(s["stat_in"], turn + 1)
        pe.matmul(b["ps"][:, 0, 0:BA * D], m.ones[:, :], v[:, 0:BA * D], start=True, stop=True)
        pe.matmul(b["ps"][:, 1, 0:(BN - BA) * D], m.ones[:, :], v[:, BA * D:BN * D], start=True, stop=True)\
          .then_inc(s["stat_out"], 1)


def bn_act(act, s, b):
    act.wait_ge(s["bn_var"], 1)
    act.activation(b["rstd"][:, :], b["rstd"][:, :], ACT.Sqrt).then_inc(s["bn_std"], 1)


def gat_memory(nc, st, m):
    g = Mem()
    g.keep = st.sb("keep", [128, SW], U8)
    g.keep_back = st.sb("keep_back", [128, SW], U8)
    g.head = st.sb("head", [128, SW], U8)
    g.tail = st.sb("tail", [128, SW], U8)
    g.keep_pen = st.sb("keep_pen", [128, SW], BF16)
    g.back_pen = st.sb("back_pen", [128, SW], BF16)
    g.head_pen = st.sb("head_pen", [128, SW], BF16)
    g.tail_pen = st.sb("tail_pen", [128, SW], BF16)
    g.of_head = st.sb("of_head", [128, H])
    g.of_range = st.sb("of_range", [128, RS])
    g.of_head_t = st.sb("of_head_t", [H, 128])
    g.one_run = st.sb("one_run", [H, 2, RS])
    g.one_pen = st.sb("one_pen", [H, 2, RS])
    g.rep = st.sb("rep", [3 * R * H, H, 128], BF16)
    g.keep_heads = st.sb("keep_heads", [R * H, RW], U8)
    g.h_t = st.sb("h_t", [D, BN, PN])
    g.rows = st.sb("rows", [PN, BN, DS])
    g.self_logits = nc.dram_tensor("gat_self_logits", [R, H, RW], F32).ap()
    g.self_alpha = nc.dram_tensor("gat_self_alpha", [R * H, RW], F32).ap()
    g.sums = nc.dram_tensor("gat_sums", [EP, DS], F32).ap()
    g.values = nc.dram_tensor("gat_values", [128, RW], F32).ap()
    g.logits = nc.dram_tensor("gat_logits", [R, H, RW], F32).ap()
    g.alpha = nc.dram_tensor("gat_alpha", [3 * R * H, RW], BF16).ap()
    return g


def gat_prepare_step(nc, m, g):
    with Step(nc, "gat_prepare") as st:
        s = st.sems("keep_copied", "ids_loaded", "chain", "flags_ready", "flags_small", "head_ready", "head_t_made")
        run = st.sb("run", [128, SW + 2], I32)
        flags = st.sb("flags", [128, 2, RS])
        ps_f = st.ps("flags", [H, 2, RS])
        ps_h = st.ps("head_t", [H, 128])
        block = st.block()

        @block.sync
        def _(sp):
            for q in range(RS):
                sp.dma_start(run[H * q:H * q + H, :], m.a.dst_ext[q * SW:q * SW + SW + 2].partition_broadcast(H))\
                  .then_inc(s["ids_loaded"], 16)
            for r in range(R):
                sp.dma_start(g.keep_heads[H * r:H * r + H, :], m.keep[32 * r:32 * r + H, :]).then_inc(s["keep_copied"], 16)
            sp.wait_ge(s["keep_copied"], 16 * R)

        @block.vector
        def _(dve):
            n = [0]

            def step(ins):
                link(dve, s["chain"], n, ins)

            dve.wait_ge(s["ids_loaded"], 16 * RS)
            step(dve.tensor_tensor(g.keep[:, :], run[:, 1:SW + 1], run[:, 0:SW], ALU.is_equal))
            step(dve.tensor_tensor(g.keep_back[:, :], run[:, 1:SW + 1], run[:, 2:SW + 2], ALU.is_equal))
            step(dve.tensor_tensor_scan(g.head[:, :], g.keep[:, :], g.keep[:, :], 1.0, ALU.mult, ALU.mult))
            step(dve.tensor_tensor_scan(g.tail[:, ::-1], g.keep_back[:, ::-1], g.keep_back[:, ::-1], 1.0, ALU.mult, ALU.mult))
            for flag, pen in ((g.keep, g.keep_pen), (g.keep_back, g.back_pen), (g.head, g.head_pen), (g.tail, g.tail_pen)):
                step(dve.tensor_scalar(pen[:, :], flag[:, :], -1.0, BIG, ALU.add, ALU.mult))
            ident3 = m.ident[:, :].rearrange("p (r h) -> p r h", h=H)
            step(dve.tensor_reduce(g.of_range[:, :], ident3, AX.X, ALU.add))
            dve.tensor_reduce(g.of_head[:, :], m.ident[:, :].rearrange("p (r h) -> p h r", h=H), AX.X, ALU.add)\
               .then_inc(s["head_ready"], 1)
            step(dve.tensor_scalar(flags[:, 0, :], g.of_range[:, :], g.head[:, SW - 1:SW], None, ALU.mult))
            dve.tensor_scalar(flags[:, 1, :], g.of_range[:, :], g.tail[:, 0:1], None, ALU.mult).then_inc(s["flags_ready"], 1)
            dve.wait_ge(s["flags_small"], 1)
            step(dve.tensor_copy(g.one_run[:, :, :], ps_f[:, :, :]))
            step(dve.tensor_scalar(g.one_pen[:, :, :], g.one_run[:, :, :], -1.0, BIG, ALU.add, ALU.mult))
            dve.wait_ge(s["head_t_made"], 1)
            step(dve.tensor_copy(g.of_head_t[:, :], ps_h[:, :]))
            for h in range(H):
                step(dve.tensor_copy(g.rep[0:R * H, h, :].rearrange("p (r f) -> p r f", f=D),
                                     m.ident[0:R * H, 0:R * H].rearrange("p (r h) -> p h r", h=H)[:, h, :]
                                     .unsqueeze(2).broadcast_to([R * H, R, D])))
            for part in range(1, 3):
                step(dve.tensor_copy(g.rep[part * R * H:(part + 1) * R * H, :, :], g.rep[0:R * H, :, :]))

        @block.tensor
        def _(pe):
            pe.wait_ge(s["head_ready"], 1)
            pe.transpose(ps_h[:, :], g.of_head[:, :], m.ident[:, :]).then_inc(s["head_t_made"], 1)
            pe.wait_ge(s["flags_ready"], 1)
            pe.matmul(ps_f[:, :, :], g.of_head[:, :], flags[:, :, :], start=True, stop=True).then_inc(s["flags_small"], 1)


def gat_self_step(nc, m, g, layer):
    a = m.a
    GB = 4
    groups = [list(range(b, min(b + GB, BN))) for b in range(0, BN, GB)]
    with Step(nc, f"gat_self{layer}") as st:
        sb, ps = st.sb, st.ps
        s = st.sems("w_zeroed", "w_loaded", "w_ready", "transposed", "copied", "u_made", "u_biased", "u_leaky", "l_made", "chain")
        wl, wr = sb("wl", [D, 2, 128]), sb("wr", [D, 2, 128])
        bias = sb("bias", [128, 2, 2])
        bsum = sb("bsum", [128, 2])
        wa = sb("wa", [128, 2 * H])
        biased = sb("biased", [128, 2, GB, PN])
        leaky = sb("leaky", [128, 2, GB, PN])
        ps_t = ps("t", [D, 2, GB, 128])
        ps_u = ps("u", [128, 2, 512])
        ps_l = ps("l", [PN, BN, H])
        block = st.block()

        @block.sync
        def _(sp):
            for to, w in ((wl, a.Wl), (wr, a.Wr)):
                sp.dma_start(to[:, :, :], w[layer].rearrange("f (g n) -> f g n", n=128)).then_inc(s["w_loaded"], 16)
            for side, b in enumerate((a.bl, a.br)):
                sp.dma_start(bias[:, side, :], b[layer].rearrange("(g n) -> n g", n=128),
                             allow_slow_non_contiguous=True).then_inc(s["w_loaded"], 16)
            sp.wait_ge(s["w_zeroed"], 1)
            for hh in range(4):
                sp.dma_start(wa[32 * hh:32 * hh + 32, hh:hh + H + 5:H + 4],
                             a.att[layer].rearrange("(g hh) c -> hh c g", hh=4)[hh],
                             allow_slow_non_contiguous=True).then_inc(s["w_loaded"], 16)

        @block.vector
        def _(dve):
            n = [0]
            dve.memset(wa[:, :], 0.0).then_inc(s["w_zeroed"], 1)
            dve.wait_ge(s["w_loaded"], 16 * 8)
            dve.tensor_tensor(wl[:, :, :], wl[:, :, :], wr[:, :, :], ALU.add)
            dve.tensor_tensor(bsum[:, :], bias[:, 0, :], bias[:, 1, :], ALU.add).then_inc(s["w_ready"], 1)
            for t, bs in enumerate(groups):
                dve.wait_ge(s["transposed"], t + 1)
                dve.tensor_copy(g.h_t[:, bs[0]:bs[-1] + 1, :], ps_t[:, t % 2, 0:len(bs), 0:PN]).then_inc(s["copied"], 1)
            for t, bs in enumerate(groups):
                for half in range(2):
                    u = 2 * t + half
                    dve.wait_ge(s["u_biased"], u + 1)
                    if t >= 1:
                        dve.wait_ge(s["l_made"], t)
                    dve.scalar_tensor_tensor(leaky[:, half, 0:len(bs), :], biased[:, half, 0:len(bs), :], 0.2,
                                             biased[:, half, 0:len(bs), :], ALU.mult, ALU.max).then_inc(s["u_leaky"], 1)
            dve.wait_ge(s["l_made"], len(groups))
            link(dve, s["chain"], n, dve.tensor_copy(m.h_self[:, :, D:DS], ps_l[:, :, :]))

        @block.scalar
        def _(act):
            act.wait_ge(s["w_ready"], 1)
            for t, bs in enumerate(groups):
                for half in range(2):
                    u = 2 * t + half
                    act.wait_ge(s["u_made"], u + 1)
                    if t >= 1:
                        act.wait_ge(s["u_leaky"], u - 1)
                    act.activation(biased[:, half, 0:len(bs), :],
                                   ps_u[:, half, 0:len(bs) * PN].rearrange("p (b n) -> p b n", n=PN), ACT.Identity,
                                   bias=bsum[:, half:half + 1]).then_inc(s["u_biased"], 1)

        @block.tensor
        def _(pe):
            for t, bs in enumerate(groups):
                if t >= 2:
                    pe.wait_ge(s["copied"], t - 1)
                for x, b in enumerate(bs):
                    last = pe.transpose(ps_t[:, t % 2, x, 0:PN], m.h[:, b * D:(b + 1) * D], m.ident[0:PN, 0:PN])
                last.then_inc(s["transposed"], 1)
            pe.wait_ge(s["w_ready"], 1)
            for t, bs in enumerate(groups):
                pe.wait_ge(s["copied"], t + 1)
                for half in range(2):
                    if t >= 1:
                        pe.wait_ge(s["u_biased"], 2 * t + half - 1)
                    pe.matmul(ps_u[:, half, 0:len(bs) * PN], wl[:, half, :], g.h_t[:, bs[0]:bs[-1] + 1, :],
                              start=True, stop=True).then_inc(s["u_made"], 1)
                pe.wait_ge(s["u_leaky"], 2 * t + 2)
                for x, b in enumerate(bs):
                    pe.matmul(ps_l[:, b, :], leaky[:, 0, x, :], wa[:, 0:H], start=True, stop=False)
                    last = pe.matmul(ps_l[:, b, :], leaky[:, 1, x, :], wa[:, H:2 * H], start=False, stop=True)
                last.then_inc(s["l_made"], 1)


def gat_scores_step(nc, m, g, layer):
    a = m.a
    G = 2 * H // 2
    U = 4
    LAG = 2
    with Step(nc, f"gat_scores{layer}") as st:
        sb, ps = st.sb, st.ps
        s = st.sems(*front_sems(), "w_zeroed", "w_loaded", "bias_ready", "state_zeroed", "u_made", "u_biased", "u_leaky",
                    "l_made", "logits_copied", "self_rows0", "self_rows1", "self_made", "self_scanned", "chunk_stored0", "chunk_stored1", "out_free")
        rows = [sb(f"rows{k}", [128, J, R, 2, D]) for k in range(2)]
        selfs = [sb(f"selfs{k}", [128, J, R, H]) for k in range(2)]
        ls = [sb(f"self_logits{k}", [R * H, W]) for k in range(2)]
        ids = [sb(f"ids{k}", [128, T], I32) for k in range(2)]
        xt = [sb(f"xt{k}", [128, 2, W]) for k in range(2)]
        biased = [sb(f"biased{k}", [128, W]) for k in range(U)]
        leaky = [sb(f"leaky{k}", [128, W]) for k in range(U)]
        lg = [sb(f"logits{k}", [R * H, W]) for k in range(2)]
        wu = sb("wu", [128, H // 2, 128])
        wa = sb("wa", [128, 2, H // 2 * R * H])
        bias = sb("bias", [128, 2, H // 2])
        bsum = sb("bsum", [128, H // 2])
        ps_x = ps("x", [128, 2, W])
        ps_u = ps("u", [128, U, W])
        ps_l = ps("l", [R * H, W])
        ps_f = ps("self", [R * H, W])
        n_w = 4 + 8 + 4
        block = st.block()

        @block.sync
        def _(sp):
            grant(sp, s, "out_free")

            def load(c, k):
                load_starts(sp, m, s, rows, c, k)
                for j in range(J):
                    sp.dma_start(selfs[k][:, j, :, :], m.self_chunks[c, :, j, :, :]).then_inc(s[f"self_rows{k}"], 16)

            for c in range(2):
                load(c, c)
            sp.wait_ge(s["w_zeroed"], 1)
            for rr in range(2):
                for sd, w in enumerate((a.Wl, a.Wr)):
                    sp.dma_start(wu[64 * rr + 32 * sd:64 * rr + 32 * sd + 32, :, 64 * rr:64 * rr + 64],
                                 w[layer].rearrange("f (g n) -> f g n", n=64)).then_inc(s["w_loaded"], 16)
                for side, b in enumerate((a.bl, a.br)):
                    sp.dma_start(bias[64 * rr:64 * rr + 64, side, :], b[layer].rearrange("(g n) -> n g", n=64),
                                 allow_slow_non_contiguous=True).then_inc(s["w_loaded"], 16)
                for hh in range(2):
                    for q in range(2):
                        first = (2 * q + rr) * H + hh
                        stride = R * H + 2
                        sp.dma_start(wa[64 * rr + 32 * hh:64 * rr + 32 * hh + 32, q, first:first + 3 * stride + 1:stride],
                                     a.att[layer].rearrange("(g two) c -> two c g", two=2)[hh],
                                     allow_slow_non_contiguous=True).then_inc(s["w_loaded"], 16)

            def store(c, k, i):
                sp.wait_ge(s["x_scanned"], went(c))
                for r in range(R):
                    sp.dma_start(g.values[32 * r:32 * r + 32, bass.ds(c * W, W)],
                                 xt[k][64 * (r % 2):64 * (r % 2) + 32, r // 2, :]).then_inc(s[f"chunk_stored{k}"], 16)
                sp.wait_ge(s["self_scanned"], went(c))
                sp.dma_start(g.self_logits.rearrange("r h e -> (r h) e")[:, bass.ds(c * W, W)], ls[k][:, :])\
                  .then_inc(s[f"chunk_stored{k}"], 16)
                sp.wait_ge(s["logits_copied"], went(c))
                sp.dma_start(g.logits.rearrange("r h e -> (r h) e")[:, bass.ds(c * W, W)], lg[k][:, :])\
                  .then_inc(s[f"chunk_stored{k}"], 16)
                sp.wait_ge(s[f"chunk_stored{k}"], (i + 1) * (16 * (R + 2)))
                sp.sem_inc(s["out_free"], 1)

            with sp.Fori(0, HALF - 1) as i:
                for k in range(2):
                    load(i * 2 + k + 2, k)
                    store(i * 2 + k, k, i)
            for k in range(2):
                store(C - 2 + k, k, HALF - 1)

        @block.gpsimd
        def _(pool):
            pool.memset(wu[:, :, :], 0.0)
            pool.memset(wa[:, :, :], 0.0).then_inc(s["w_zeroed"], 1)
            with pool.Fori(0, HALF) as i:
                for k in range(2):
                    gather_sources(pool, m, s, rows, ids, i * 2 + k, k, i)

        @block.scalar
        def _(act):
            grant(act, s, "ids_copied", "u_biased")
            for k in range(2):
                copy_ids(act, m, s, ids, k, k)
            act.wait_ge(s["bias_ready"], 1)
            with act.Fori(0, HALF) as i:
                for k in range(2):
                    c = i * 2 + k
                    copy_ids(act, m, s, ids, c + 2, k)
                    for t in range(G):
                        n = c * G + t
                        act.wait_ge(s["u_made"], went(n))
                        act.wait_ge(s["u_leaky"], went(n, U))
                        act.activation(biased[t % U][:, :], ps_u[:, t % U, :], ACT.Identity,
                                       bias=bsum[:, t % 4:t % 4 + 1]).then_inc(s["u_biased"], 1)

        @block.tensor
        def _(pe):
            grant(pe, s, "rows_transposed", "self_made", "u_made", "l_made")
            pe.wait_ge(s["w_loaded"], 16 * n_w)

            def logits(c, t):
                n = c * G + t
                pe.wait_ge(s["u_leaky"], went(n))
                if t == 0:
                    pe.wait_ge(s["logits_copied"], went(c, 1))
                pe.matmul(ps_l[:, :], wa[:, t // 4, (t % 4) * R * H:(t % 4 + 1) * R * H], leaky[t % U][:, :],
                          start=(t == 0), stop=(t == G - 1)).then_inc(s["l_made"], 1)

            with pe.Fori(0, HALF) as i:
                for k in range(2):
                    c = i * 2 + k
                    pe.wait_ge(s[f"self_rows{k}"], (i + 1) * (16 * J))
                    pe.wait_ge(s["self_scanned"], went(c, 1))
                    for j in range(J):
                        last = pe.transpose(ps_f[:, j::J], selfs[k][:, j, :, :], m.ident[:, :])
                    last.then_inc(s["self_made"], 1)
                    transpose_rows(pe, m, s, rows, ps_x, c, k, i)
                    pe.wait_ge(s["x_scanned"], went(c))
                    for t in range(G):
                        n = c * G + t
                        pe.wait_ge(s["u_biased"], went(n, U))
                        pe.matmul(ps_u[:, t % U, :], wu[:, t % 4, :], xt[k][:, t // 4, :], start=True, stop=True)\
                          .then_inc(s["u_made"], 1)
                        if t >= LAG:
                            logits(c, t - LAG)
                    for t in range(G - LAG, G):
                        logits(c, t)

        @block.vector
        def _(dve):
            grant(dve, s, "x_scanned", "self_scanned", "u_leaky", "logits_copied")
            dve.memset(ls[1][:, :], 0.0).then_inc(s["state_zeroed"], 1)
            dve.memset(xt[1][:, :, :], 0.0).then_inc(s["state_zeroed"], 1)
            dve.wait_ge(s["w_loaded"], 16 * n_w)
            dve.tensor_tensor(bsum[:, :], bias[:, 0, :], bias[:, 1, :], ALU.add).then_inc(s["bias_ready"], 1)
            dve.wait_ge(s["state_zeroed"], 2)
            with dve.Fori(0, HALF) as i:
                for k in range(2):
                    c = i * 2 + k
                    dve.wait_ge(s["out_free"], went(c, 2))
                    scan_rows(dve, m, s, ps_x, xt, c, k)
                    dve.wait_ge(s["self_made"], went(c))
                    dve.wait_ge(s["self_scanned"], went(c, 1))
                    dve.tensor_tensor_scan(ls[k][:, :], g.keep_heads[:, bass.ds(c * W, W)], ps_f[:, :],
                                           ls[1 - k][:, W - 1:W], ALU.mult, ALU.add).then_inc(s["self_scanned"], 1)
                    for t in range(G):
                        n = c * G + t
                        dve.wait_ge(s["u_biased"], went(n))
                        dve.wait_ge(s["l_made"], went(n, U))
                        dve.scalar_tensor_tensor(leaky[t % U][:, :], biased[t % U][:, :], 0.2, biased[t % U][:, :],
                                                 ALU.mult, ALU.max).then_inc(s["u_leaky"], 1)
                    dve.wait_ge(s["l_made"], went(c * G + G - 1))
                    dve.tensor_copy(lg[k][:, :], ps_l[:, :]).then_inc(s["logits_copied"], 1)


def gat_softmax_step(nc, m, g, layer):
    with Step(nc, f"gat_softmax{layer}") as st:
        sb, ps = st.sb, st.ps
        s = st.sems("own_ready", "loaded", "chain", "ends_ready", "ends_small", "carry_ready", "carry_made", "shifted", "exp_made",
                    "parts_ready", "stored")
        lg = sb("logits", [128, SW])
        one = sb("one", [128, SW])
        two = sb("two", [128, SW])
        own = sb("own", [128, SW])
        parts = sb("parts", [128, 3, SW], BF16)
        ends = sb("ends", [128, 2, RS])
        small = sb("small", [H, 2, RS + 1])
        masked = sb("masked", [128, 2, RS])
        carry = sb("carry", [128, 2])
        ps_e = ps("ends", [H, 2, RS])
        ps_c = ps("carry", [128, 2, RS])
        block = st.block()

        @block.sync
        def _(sp):
            for q in range(RS):
                r, sub = q // 4, q % 4
                sp.dma_start(lg[H * q:H * q + H, :], g.logits[r, :, sub * SW:(sub + 1) * SW]).then_inc(s["loaded"], 16)
                sp.dma_start(own[H * q:H * q + H, :], g.self_logits[r, :, sub * SW:(sub + 1) * SW]).then_inc(s["loaded"], 16)
            sp.wait_ge(s["own_ready"], 1)
            for q in range(RS):
                r, sub = q // 4, q % 4
                sp.dma_start(g.self_alpha[H * r:H * r + H, sub * SW:(sub + 1) * SW], own[H * q:H * q + H, :])\
                  .then_inc(s["stored"], 16)
            for part in range(3):
                sp.wait_ge(s["parts_ready"], part + 1)
                for q in range(RS):
                    r, sub = q // 4, q % 4
                    first = (part * R + r) * H
                    sp.dma_start(g.alpha[first:first + H, sub * SW:(sub + 1) * SW], parts[H * q:H * q + H, part, :])\
                      .then_inc(s["stored"], 16)
            sp.wait_ge(s["stored"], 16 * 4 * RS)

        @block.tensor
        def _(pe):
            for turn in range(2):
                pe.wait_ge(s["ends_ready"], turn + 1)
                pe.matmul(ps_e[:, :, :], g.of_head[:, :], ends[:, :, :], start=True, stop=True).then_inc(s["ends_small"], 1)
                pe.wait_ge(s["carry_ready"], turn + 1)
                pe.matmul(ps_c[:, 0, :], g.of_head_t[:, :], small[:, 0, 0:RS], start=True, stop=True)
                pe.matmul(ps_c[:, 1, :], g.of_head_t[:, :], small[:, 1, 1:RS + 1], start=True, stop=True)\
                  .then_inc(s["carry_made"], 1)

        @block.scalar
        def _(act):
            act.wait_ge(s["shifted"], 1)
            act.activation(one[:, :], one[:, :], ACT.Exp).then_inc(s["exp_made"], 1)
            act.wait_ge(s["shifted"], 2)
            act.activation(own[:, :], own[:, :], ACT.Exp).then_inc(s["exp_made"], 1)

        @block.vector
        def _(dve):
            n = [0]

            def step(ins):
                link(dve, s["chain"], n, ins)

            def carries(turn, local, flags, op, op1, empty):
                step(dve.tensor_scalar(ends[:, 0, :], g.of_range[:, :], local[:, SW - 1:SW], None, ALU.mult))
                step(dve.tensor_scalar(ends[:, 1, :], g.of_range[:, :], local[:, 0:1], None, ALU.mult))
                step(dve.memset(small[:, :, :], empty))
                dve.sem_inc(s["ends_ready"], 1)
                dve.wait_ge(s["ends_small"], turn)
                step(dve.tensor_tensor_scan(small[:, 0, 1:RS + 1], flags[:, 0, :], ps_e[:, 0, :], empty, op, op1))
                step(dve.tensor_tensor_scan(small[:, 1, 0:RS][:, ::-1], flags[:, 1, ::-1], ps_e[:, 1, ::-1], empty, op, op1))
                dve.sem_inc(s["carry_ready"], 1)
                dve.wait_ge(s["carry_made"], turn)
                step(dve.tensor_tensor(masked[:, :, :], ps_c[:, :, :],
                                       g.of_range[:, :].unsqueeze(1).broadcast_to([128, 2, RS]), ALU.mult))
                step(dve.tensor_reduce(carry[:, :], masked[:, :, :], AX.X, ALU.add))

            dve.wait_ge(s["loaded"], 32 * RS)
            step(dve.tensor_tensor_scan(one[:, :], g.keep_pen[:, :], lg[:, :], -BIG, ALU.add, ALU.max))
            step(dve.tensor_tensor_scan(two[:, ::-1], g.back_pen[:, ::-1], one[:, ::-1], -BIG, ALU.add, ALU.max))
            carries(1, two, g.one_pen, ALU.add, ALU.max, -BIG)
            step(dve.scalar_tensor_tensor(two[:, :], g.head_pen[:, :], carry[:, 0:1], two[:, :], ALU.add, ALU.max))
            step(dve.scalar_tensor_tensor(two[:, :], g.tail_pen[:, :], carry[:, 1:2], two[:, :], ALU.add, ALU.max))
            step(dve.tensor_tensor(two[:, :], two[:, :], own[:, :], ALU.max))
            dve.tensor_tensor(one[:, :], lg[:, :], two[:, :], ALU.subtract).then_inc(s["shifted"], 1)
            dve.tensor_tensor(own[:, :], own[:, :], two[:, :], ALU.subtract).then_inc(s["shifted"], 1)
            dve.wait_ge(s["exp_made"], 1)
            step(dve.tensor_tensor_scan(lg[:, :], g.keep[:, :], one[:, :], 0.0, ALU.mult, ALU.add))
            step(dve.tensor_tensor_scan(two[:, ::-1], g.keep_back[:, ::-1], lg[:, ::-1], 0.0, ALU.mult, ALU.max))
            carries(2, two, g.one_run, ALU.mult, ALU.add, 0.0)
            step(dve.scalar_tensor_tensor(two[:, :], g.head[:, :], carry[:, 0:1], two[:, :], ALU.mult, ALU.add))
            step(dve.scalar_tensor_tensor(two[:, :], g.tail[:, :], carry[:, 1:2], two[:, :], ALU.mult, ALU.add))
            dve.wait_ge(s["exp_made"], 2)
            step(dve.scalar_tensor_tensor(two[:, :], two[:, :], 1e-16, own[:, :], ALU.add, ALU.add))
            step(dve.reciprocal(two[:, :], two[:, :]))
            dve.tensor_tensor(own[:, :], own[:, :], two[:, :], ALU.mult).then_inc(s["own_ready"], 1)
            step(dve.tensor_tensor(one[:, :], one[:, :], two[:, :], ALU.mult))
            dve.tensor_copy(parts[:, 0, :], one[:, :]).then_inc(s["parts_ready"], 1)
            dve.wait_ge(s["parts_ready"], 1)
            step(dve.tensor_tensor(one[:, :], one[:, :], parts[:, 0, :], ALU.subtract))
            dve.tensor_copy(parts[:, 1, :], one[:, :]).then_inc(s["parts_ready"], 1)
            dve.wait_ge(s["parts_ready"], 2)
            dve.tensor_tensor(parts[:, 2, :], one[:, :], parts[:, 1, :], ALU.subtract).then_inc(s["parts_ready"], 1)


def gat_messages_step(nc, m, g, layer):
    a = m.a
    with Step(nc, f"gat_messages{layer}") as st:
        sb, ps = st.sb, st.ps
        s = st.sems(*tail_sems(), "w_zeroed", "w_loaded", "w_scaled", "state_zeroed", "alpha_loaded0", "alpha_loaded1",
                    "values_loaded0", "values_loaded1", "own_loaded0", "own_loaded1",
                    "own_made", "a_made", "weighted", "m_made")
        al = [sb(f"alpha{k}", [3 * R * H, W], BF16) for k in range(2)]
        xv = [sb(f"values{k}", [128, W]) for k in range(2)]
        wx = [sb(f"weighted{k}", [128, W]) for k in range(2)]
        sc = [sb(f"sc{k}", [128, W]) for k in range(2)]
        ob = [sb(f"ob{k}", [128, R, J, DS]) for k in range(2)]
        own = [sb(f"own{k}", [R * H, W]) for k in range(2)]
        wl = sb("wl", [128, H, 128])
        ps_a = ps("a", [128, 2, W])
        ps_m = ps("m", [128, 2, W])
        ps_s = ps("s", [128, J, 128])
        ps_o = ps("own", [128, J, R * H])
        sums_chunks = g.sums.rearrange("(r c p j) f -> c p r (j f)", r=R, c=C, p=128, j=J)
        block = st.block()

        @block.sync
        def _(sp):
            grant(sp, s, "out_free")
            sp.wait_ge(s["w_zeroed"], 1)
            for r in range(R):
                sp.dma_start(wl[32 * r:32 * r + 32, :, 32 * r:32 * r + 32],
                             a.Wl[layer].rearrange("f (h c) -> f h c", h=H)).then_inc(s["w_loaded"], 16)

            def load(c, k):
                sp.wait_ge(s["own_made"], went(c, 2))
                sp.dma_start(al[k][:, :], g.alpha[:, bass.ds(c * W, W)]).then_inc(s[f"alpha_loaded{k}"], 16)
                sp.dma_start(xv[k][:, :], g.values[:, bass.ds(c * W, W)]).then_inc(s[f"values_loaded{k}"], 16)
                sp.dma_start(own[k][:, :], g.self_alpha[:, bass.ds(c * W, W)]).then_inc(s[f"own_loaded{k}"], 16)

            for k in range(2):
                sp.dma_start(al[k][:, :], g.alpha[:, k * W:(k + 1) * W]).then_inc(s[f"alpha_loaded{k}"], 16)
                sp.dma_start(xv[k][:, :], g.values[:, k * W:(k + 1) * W]).then_inc(s[f"values_loaded{k}"], 16)
                sp.dma_start(own[k][:, :], g.self_alpha[:, k * W:(k + 1) * W]).then_inc(s[f"own_loaded{k}"], 16)
            def store(c, k, i):
                sp.wait_ge(s["sums_copied"], went(c))
                sp.dma_start(sums_chunks[c], ob[k][:, :, :, :].rearrange("p r j f -> p r (j f)"))\
                  .then_inc(s[f"sums_stored{k}"], 16)
                sp.wait_ge(s[f"sums_stored{k}"], (i + 1) * 16)
                sp.sem_inc(s["out_free"], 1)

            with sp.Fori(0, HALF - 1) as i:
                for k in range(2):
                    load(i * 2 + k + 2, k)
                    store( i * 2 + k, k, i)
            for k in range(2):
                store( C - 2 + k, k, HALF - 1)

        @block.gpsimd
        def _(pool):
            pool.memset(wl[:, :, :], 0.0).then_inc(s["w_zeroed"], 1)
            pool.wait_ge(s["w_loaded"], 16 * R)
            pool.tensor_scalar(wl[:, :, :], wl[:, :, :], 1.0 / H, None, ALU.mult).then_inc(s["w_scaled"], 1)

        @block.tensor
        def _(pe):
            grant(pe, s, "own_made", "a_made", "m_made", "sums_transposed")
            pe.wait_ge(s["w_scaled"], 1)

            def product(c, k, h):
                pe.wait_ge(s["weighted"], went(c * H + h))
                if h == 0:
                    pe.wait_ge(s["msg_scanned"], went(c, 2))
                pe.matmul(ps_m[:, k, :], wl[:, h, :], wx[h % 2][:, :], start=(h == 0), stop=(h == H - 1))\
                  .then_inc(s["m_made"], 1)

            with pe.Fori(0, HALF) as i:
                for k in range(2):
                    c = i * 2 + k
                    pe.wait_ge(s[f"own_loaded{k}"], (i + 1) * 16)
                    pe.wait_ge(s[f"alpha_loaded{k}"], (i + 1) * 16)
                    for h in range(H):
                        pe.wait_ge(s["weighted"], went(c * H + h, 2))
                        pe.matmul(ps_a[:, h % 2, :], g.rep[:, h, :], al[k][:, :], start=True, stop=True)\
                          .then_inc(s["a_made"], 1)
                        if h >= 1:
                            product(c, k, h - 1)
                    product(c, k, H - 1)
                    transpose_sums(pe, m, s, sc, ps_s, c, k)
                    for j in range(J):
                        last = pe.transpose(ps_o[:, j, :], own[k][:, j::J], m.ident[0:R * H, 0:R * H])
                    last.then_inc(s["own_made"], 1)

        @block.vector
        def _(dve):
            grant(dve, s, "weighted", "msg_scanned")
            dve.memset(sc[1][:, :], 0.0).then_inc(s["state_zeroed"], 1)
            dve.wait_ge(s["state_zeroed"], 1)
            with dve.Fori(0, HALF) as i:
                for k in range(2):
                    c = i * 2 + k
                    dve.wait_ge(s[f"values_loaded{k}"], (i + 1) * 16)
                    for h in range(H):
                        dve.wait_ge(s["a_made"], went(c * H + h))
                        dve.wait_ge(s["m_made"], went(c * H + h, 2))
                        dve.tensor_tensor(wx[h % 2][:, :], ps_a[:, h % 2, :], xv[k][:, :], ALU.mult)\
                           .then_inc(s["weighted"], 1)
                    dve.wait_ge(s["m_made"], went(c * H + H - 1))
                    dve.wait_ge(s["sums_transposed"], went(c, 2))
                    dve.wait_ge(s["msg_scanned"], went(c, 1))
                    dve.tensor_tensor_scan(sc[k][:, :], m.keep[:, bass.ds(c * W, W)], ps_m[:, k, :],
                                           sc[1 - k][:, W - 1:W], ALU.mult, ALU.add).then_inc(s["msg_scanned"], 1)

        @block.scalar
        def _(act):
            grant(act, s, "sums_copied")
            with act.Fori(0, HALF) as i:
                for k in range(2):
                    c = i * 2 + k
                    act.wait_ge(s["own_made"], went(c))
                    act.wait_ge(s["sums_transposed"], went(c))
                    act.wait_ge(s["out_free"], went(c, 2))
                    act.activation(ob[k][:, :, :, D:DS].rearrange("p r j h -> p j r h"),
                                   ps_o[:, :, :].rearrange("p j (r h) -> p j r h", r=R), ACT.Copy)
                    act.activation(ob[k][:, :, :, 0:D].rearrange("p r j f -> p j r f"),
                                   ps_s[:, :, :].rearrange("p j (r f) -> p j r f", r=R), ACT.Copy)\
                       .then_inc(s["sums_copied"], 1)


def gat_norm_step(nc, m, g, layer):
    a = m.a
    with Step(nc, f"gat_norm{layer}") as st:
        sb = st.sb
        s = st.sems("w_loaded", "alpha_ready", "v_made", "v_used", *bn_sems())
        b = bn_memory(st)
        y = sb("y", [PN, BN * D])
        wl = sb("wl", [D, H * D])
        alpha = sb("alpha", [PN, BN, H])
        none = sb("none", [PN, BN])
        weighted = sb("weighted", [PN, 2, 2, H * D])
        ps_v = st.ps("v", [PN, 2, 2, H * D])
        bl = sb("bl", [PN, H * D])
        blm = sb("bl_mean", [PN, D])
        cb = sb("conv_bias", [PN, D])
        gamma = sb("gamma", [PN, D])
        beta = sb("beta", [PN, D])
        block = st.block()

        @block.sync
        def _(sp):
            for to, v in ((bl, a.bl), (cb, a.cb), (gamma, a.bng), (beta, a.bnb)):
                sp.dma_start(to[:, :], v[layer].partition_broadcast(PN)).then_inc(s["w_loaded"], 16)
            sp.dma_start(wl[:, :], a.Wl[layer]).then_inc(s["w_loaded"], 16)

        @block.vector
        def _(dve):
            n = [0]

            def step(ins):
                link(dve, s["chain"], n, ins)

            y3 = y[:, :].rearrange("p (b f) -> p b f", f=D)
            dve.wait_ge(s["w_loaded"], 80)
            step(dve.tensor_reduce(blm[:, :], bl[:, :].rearrange("p (h f) -> p f h", f=D), AX.X, ALU.add))
            step(dve.tensor_scalar(blm[:, :], blm[:, :], 1.0 / H, None, ALU.mult))
            step(dve.tensor_tensor(blm[:, :], blm[:, :], cb[:, :], ALU.add))
            step(dve.tensor_scalar(none[:, :], m.some[:, :], -1.0, 1.0, ALU.mult, ALU.add))
            step(dve.tensor_tensor(alpha[:, :, :], g.rows[:, :, D:DS], m.some[:, :].unsqueeze(2).broadcast_to([PN, BN, H]), ALU.mult))
            step(dve.tensor_tensor(alpha[:, :, :], alpha[:, :, :], none[:, :].unsqueeze(2).broadcast_to([PN, BN, H]), ALU.add))
            step(dve.tensor_scalar(alpha[:, :, :], alpha[:, :, :], 1.0 / H, None, ALU.mult))
            for t in range(0, BN, 2):
                u, nb = t // 2, min(2, BN - t)
                dve.wait_ge(s["v_made"], u + 1)
                dve.tensor_tensor(weighted[:, u % 2, 0:nb, :].rearrange("p b (h f) -> p (b h) f", f=D),
                                  ps_v[:, u % 2, 0:nb, :].rearrange("p b (h f) -> p (b h) f", f=D),
                                  alpha[:, t:t + nb, :].rearrange("p b h -> p (b h)").unsqueeze(2)
                                  .broadcast_to([PN, nb * H, D]), ALU.mult).then_inc(s["v_used"], 1)
                dve.wait_ge(s["v_used"], u + 1)
                last = dve.tensor_reduce(y3[:, t:t + nb, :], weighted[:, u % 2, 0:nb, :].rearrange("p b (h f) -> p b f h", f=D),
                                         AX.X, ALU.add)
            step(last)
            step(dve.tensor_tensor(y3, y3, blm[:, :].unsqueeze(1).broadcast_to([PN, BN, D]), ALU.add))
            step(dve.tensor_tensor(y[:, :], y[:, :], m.agg[:, :], ALU.add))
            if layer < 2:
                step(dve.scalar_tensor_tensor(y[:, :], y[:, :], 0.01, y[:, :], ALU.mult, ALU.max))
            step(dve.tensor_tensor(y[:, :], y[:, :], m.h[:, :], ALU.add))
            bn_dve(dve, s, n, b, y, m.h, gamma, beta)
            if layer == 2:
                step(dve.tensor_tensor(m.x[:, :], m.x[:, :], m.h[:, :], ALU.add))

        @block.tensor
        def _(pe):
            pe.wait_ge(s["w_loaded"], 80)
            for b0 in range(BN):
                u = b0 // 2
                if b0 % 2 == 0 and u >= 2:
                    pe.wait_ge(s["v_used"], u - 1)
                last = pe.matmul(ps_v[:, u % 2, b0 % 2, :], g.h_t[:, b0, :], wl[:, :], start=True, stop=True)
                if b0 % 2 == 1 or b0 == BN - 1:
                    last.then_inc(s["v_made"], 1)
            bn_pe(pe, m, s, b, y)

        @block.scalar
        def _(act):
            bn_act(act, s, b)


def gat_layers(nc, m):
    with Step(nc, "gat") as st:
        g = gat_memory(nc, st, m)
        gat_prepare_step(nc, m, g)
        norm_step(nc, m, "gat_layernorm")
        for layer in range(3):
            gat_self_step(nc, m, g, layer)
            publish_step(nc, m, f"gat_publish{layer}")
            gat_scores_step(nc, m, g, layer)
            gat_softmax_step(nc, m, g, layer)
            gat_messages_step(nc, m, g, layer)
            collect_step(nc, m, f"gat_collect{layer}", g.sums, g.rows)
            gat_norm_step(nc, m, g, layer)


K2, UA, OUT2 = 16, 80, 48
GAIN, PW_S, PW_V = 1.593, 0.17677669529663687, 0.25
W_SCALE = 2.0 ** 0.5 / 10.0 ** 0.5 / 4.0
INV_SQRT3 = 0.5773502691896258
SQRT_3_2 = 1.5 ** 0.5


def equi_memory(st):
    e = Mem()
    e.hidden = st.sb("hidden", [128, C * T, K2])
    e.unit = st.sb("unit", [128, C * T, 3])
    e.norm_s = st.sb("norm_s", [128, C * T])
    e.norm_v = st.sb("norm_v", [128, C * T])
    e.w = st.sb("w", [UA, K2 * OUT2])
    return e


def equi_prepare_step(nc, m, e):
    a = m.a
    with Step(nc, "equi_prepare") as st:
        sb, ps = st.sb, st.ps
        s = st.sems("vec_loaded", "w1_loaded", "w_zeroed", "w_loaded", "we_loaded", "chain", "sum_ready", "root_ready",
                    "emb_loaded0", "emb_loaded1", "h_made", "h_copied")
        vec = sb("vec", [128, C * T, 3])
        sq = sb("sq", [128, C * T, 3])
        rt = sb("root", [128, C * T])
        w1 = sb("w1", [10, K2])
        we = sb("we", [UA, K2 * OUT2])
        emb = [sb(f"emb{k}", [10, R, W]) for k in range(2)]
        ps_h = ps("h", [128, 2, 512])
        block = st.block()

        @block.sync
        def _(sp):
            sp.dma_start(vec[:, :, :].rearrange("p t i -> p (t i)"), a.vec_t).then_inc(s["vec_loaded"], 16)
            sp.dma_start(w1[:, :], a.W1e).then_inc(s["w1_loaded"], 16)
            for k in range(2):
                sp.dma_start(emb[k][:, :, :], a.emb_t[:, :, k * W:(k + 1) * W]).then_inc(s[f"emb_loaded{k}"], 16)
            sp.wait_ge(s["w_zeroed"], 1)

            def put(to, sem, first_row, path, first_out):
                sp.dma_start(to[first_row:first_row + 16, :].rearrange("u (k o) -> u k o", o=OUT2)[:, :, first_out:first_out + 8],
                             a.W2e[:, path, :, :]).then_inc(s[sem], 16)

            put(e.w, "w_loaded", 0, 0, 0)
            put(e.w, "w_loaded", 0, 2, 8)
            put(e.w, "w_loaded", 0, 4, 16)
            put(e.w, "w_loaded", 16, 1, 0)
            put(e.w, "w_loaded", 16, 3, 8)
            put(we, "we_loaded", 16, 6, 16)
            for i in range(3):
                put(e.w, "w_loaded", 32 + 16 * i, 5, 24 + 8 * i)
                put(we, "we_loaded", 32 + 16 * i, 6, 24 + 8 * i)
            with sp.Fori(0, HALF - 1) as i:
                for k in range(2):
                    c = i * 2 + k + 2
                    sp.wait_ge(s["h_made"], went(c, 2))
                    sp.dma_start(emb[k][:, :, :], a.emb_t[:, :, bass.ds(c * W, W)]).then_inc(s[f"emb_loaded{k}"], 16)

        @block.gpsimd
        def _(pool):
            pool.memset(we[:, :], 0.0)
            pool.memset(e.w[:, :], 0.0).then_inc(s["w_zeroed"], 1)

        @block.tensor
        def _(pe):
            grant(pe, s, "h_made")
            pe.wait_ge(s["w1_loaded"], 16)
            with pe.Fori(0, HALF) as i:
                for k in range(2):
                    c = i * 2 + k
                    pe.wait_ge(s[f"emb_loaded{k}"], (i + 1) * 16)
                    pe.wait_ge(s["h_copied"], went(c, 2))
                    for j in range(J):
                        for r in range(R):
                            t = j * R + r
                            last = pe.matmul(ps_h[:, k, t * K2:(t + 1) * K2], emb[k][:, r, j::J], w1[:, :], start=True, stop=True)
                    last.then_inc(s["h_made"], 1)

        @block.scalar
        def _(act):
            grant(act, s, "h_copied")
            act.wait_ge(s["sum_ready"], 1)
            act.activation(rt[:, :], rt[:, :], ACT.Sqrt).then_inc(s["root_ready"], 1)
            with act.Fori(0, HALF) as i:
                for k in range(2):
                    c = i * 2 + k
                    act.wait_ge(s["h_made"], went(c))
                    act.activation(e.hidden[:, bass.ds(c * T, T), :].rearrange("p t k -> p (t k)"), ps_h[:, k, 0:T * K2], ACT.Relu)\
                       .then_inc(s["h_copied"], 1)

        @block.vector
        def _(dve):
            n = [0]

            def step(ins):
                link(dve, s["chain"], n, ins)

            dve.wait_ge(s["vec_loaded"], 16)
            step(dve.tensor_tensor(sq[:, :, :], vec[:, :, :], vec[:, :, :], ALU.mult))
            dve.tensor_reduce(rt[:, :], sq[:, :, :], AX.X, ALU.add).then_inc(s["sum_ready"], 1)
            dve.wait_ge(s["root_ready"], 1)
            step(dve.reciprocal(rt[:, :], rt[:, :]))
            step(dve.tensor_tensor(e.unit[:, :, :], vec[:, :, :], rt[:, :].unsqueeze(2).broadcast_to([128, C * T, 3]), ALU.mult))
            step(dve.tensor_scalar(e.norm_s[:, :], m.ew[:, :], GAIN, None, ALU.mult))
            step(dve.tensor_scalar(e.norm_v[:, :], m.ew[:, :], GAIN * GAIN_V, None, ALU.mult))
            dve.wait_ge(s["w_loaded"], 16 * 8)
            dve.wait_ge(s["we_loaded"], 16 * 4)
            step(dve.tensor_scalar(e.w[32:64, :], e.w[32:64, :], INV_SQRT3, None, ALU.mult))
            step(dve.tensor_scalar(e.w[64:UA, :], e.w[64:UA, :], INV_SQRT3, None, ALU.mult))
            step(dve.scalar_tensor_tensor(e.w[0:32, :], we[0:32, :], SQRT_3_2, e.w[0:32, :], ALU.mult, ALU.add))
            step(dve.scalar_tensor_tensor(e.w[32:64, :], we[32:64, :], -SQRT_3_2 / 3.0, e.w[32:64, :], ALU.mult, ALU.add))
            step(dve.scalar_tensor_tensor(e.w[64:UA, :], we[64:UA, :], -SQRT_3_2 / 3.0, e.w[64:UA, :], ALU.mult, ALU.add))


GAIN_V = PW_V * W_SCALE


def equi_edges_step(nc, m, e):
    HK = K2 * OUT2 // 2
    with Step(nc, "equi_edges") as st:
        sb, ps = st.sb, st.ps
        s = st.sems(*front_sems(), *tail_sems(), "state_zeroed", "x_back", "a_copied", "x_left", "projected", "a_ready",
                    "a_transposed", "at_copied", "g_made", "g_weighed", "g_added", "acted", "spread", "ftr_ready", "chain")
        rows = [sb(f"rows{k}", [128, J, R, 2, D]) for k in range(2)]
        ids = [sb(f"ids{k}", [128, T], I32) for k in range(2)]
        xt = [sb(f"xt{k}", [128, 2, W]) for k in range(2)]
        inp = [sb(f"inputs{k}", [128, T, UA]) for k in range(2)]
        proj = sb("proj", [128, T, 3, 16])
        at = [sb(f"inputs_t{k}", [UA, R, 128]) for k in range(2)]
        prod = [sb(f"prod{k}", [128, K2 * OUT2]) for k in range(2)]
        res = [sb(f"res{k}", [128, T, OUT2]) for k in range(2)]
        gated = sb("gated", [128, T, 16])
        vec = sb("vec", [128, T, 3, 8])
        ftr = [sb(f"ftr{k}", [128, T, D]) for k in range(2)]
        sc = [sb(f"sc{k}", [128, W]) for k in range(2)]
        ob = [sb(f"ob{k}", [128, R * J * D]) for k in range(2)]
        ps_x = ps("x", [128, W])
        ps_e = ps("e", [128, J, 2, 2, D])
        ps_t = ps("t", [UA, R, 128])
        ps_g = ps("g", [128, 2, 2, 512])
        ps_s = ps("s", [128, J, 128])
        ps_m = ps_s[:, :, :].rearrange("p j n -> p (j n)")
        block = st.block()

        @block.sync
        def _(sp):
            grant(sp, s, "out_free")
            for c in range(2):
                load_starts(sp, m, s, rows, c, c)
            with sp.Fori(0, HALF - 1) as i:
                for k in range(2):
                    load_starts(sp, m, s, rows, i * 2 + k + 2, k)
                    store_sums(sp, m, s, ob, i * 2 + k, k, i)
            for k in range(2):
                store_sums(sp, m, s, ob, C - 2 + k, k, HALF - 1)

        @block.gpsimd
        def _(pool):
            with pool.Fori(0, HALF) as i:
                for k in range(2):
                    gather_sources(pool, m, s, rows, ids, i * 2 + k, k, i)

        @block.scalar
        def _(act):
            grant(act, s, "ids_copied", "a_copied", "at_copied", "acted", "sums_copied")
            for k in range(2):
                copy_ids(act, m, s, ids, k, k)
            with act.Fori(0, HALF) as i:
                for k in range(2):
                    c = i * 2 + k
                    for q in range(2):
                        act.wait_ge(s["x_back"], went(c * 2 + q))
                        act.wait_ge(s["a_transposed"], went(c * J, J))
                        tiles = inp[k][:, :, :].rearrange("p (j r) a -> p j r a", r=R)[:, :, 2 * q:2 * q + 2, :]
                        for sd in range(2):
                            act.activation(tiles[..., 8 * sd:8 * sd + 8], ps_e[:, :, :, sd, 0:8], ACT.Copy)
                            for x in range(3):
                                first = 32 + 16 * x + 8 * sd
                                last = act.activation(tiles[..., first:first + 8], ps_e[:, :, :, sd, 8 + x:D:3], ACT.Copy)
                        last.then_inc(s["a_copied"], 1)
                    copy_ids(act, m, s, ids, c + 2, k)
                    for j in range(J):
                        n = c * J + j
                        act.wait_ge(s["a_transposed"], went(n))
                        act.wait_ge(s["g_made"], went(n * R, 4))
                        act.activation(at[j % 2][:, :, :], ps_t[:, :, :], ACT.Copy).then_inc(s["at_copied"], 1)
                    act.wait_ge(s["g_added"], went(c * T + T - 1))
                    act.wait_ge(s["spread"], went(c, 1))
                    act.activation(gated[:, :, :], res[k][:, :, 0:16], ACT.Tanh, scale=PW_S * W_SCALE)\
                       .then_inc(s["acted"], 1)
                    copy_sums(act, s, ps_s, ob, c, k)

        @block.tensor
        def _(pe):
            grant(pe, s, "rows_transposed", "x_left", "x_back", "a_transposed", "g_made", "msg_ready", "sums_transposed")
            with pe.Fori(0, HALF) as i:
                for k in range(2):
                    c = i * 2 + k
                    pe.wait_ge(s[f"src_rows{k}"], (i + 1) * (16 * T))
                    pe.wait_ge(s[f"dst_rows{k}"], (i + 1) * (16 * J))
                    for q in range(2):
                        pe.wait_ge(s["x_scanned"], went(c * 2 + q, 1))
                        for j in range(J):
                            last = pe.transpose(ps_x[:, j::J], rows[k][:, j, 2 * q:2 * q + 2, :, :], m.ident[:, :])
                        last.then_inc(s["x_left"], 1)
                        pe.wait_ge(s["x_scanned"], went(c * 2 + q))
                        if q == 1:
                            pe.sem_inc(s["rows_transposed"], 1)
                        pe.wait_ge(s["a_copied"], went(c * 2 + q, 1))
                        for j in range(J):
                            last = pe.transpose(ps_e[:, j, :, :, :].rearrange("p r s f -> p (r s f)"), xt[k][:, q, j::J], m.ident[:, :])
                        last.then_inc(s["x_back"], 1)
                    pe.wait_ge(s["a_ready"], went(c))
                    for j in range(J):
                        n = c * J + j
                        pe.wait_ge(s["at_copied"], went(n, 1))
                        for r in range(R):
                            last = pe.transpose(ps_t[:, r, :], inp[k][:, j * R + r, :], m.ident[:, :])
                        last.then_inc(s["a_transposed"], 1)
                        pe.wait_ge(s["at_copied"], went(n))
                        for r in range(R):
                            t = j * R + r
                            pe.wait_ge(s["g_weighed"], went(c * T + t, 2))
                            for half in range(2):
                                last = pe.matmul(ps_g[:, t % 2, half, 0:HK], at[j % 2][:, r, :],
                                                 e.w[:, half * HK:(half + 1) * HK], start=True, stop=True)
                            last.then_inc(s["g_made"], 1)
                    pe.wait_ge(s["ftr_ready"], went(c))
                    pe.wait_ge(s["sums_copied"], went(c, 1))
                    for j in range(J):
                        last = pe.transpose(ps_m[:, j::J], ftr[k][:, j * R:(j + 1) * R, :].rearrange("p r f -> p (r f)"), m.ident[:, :])
                    last.then_inc(s["msg_ready"], 1)
                    transpose_sums(pe, m, s, sc, ps_s, c, k)

        @block.vector
        def _(dve):
            grant(dve, s, "x_scanned", "projected", "a_ready", "g_weighed", "g_added", "spread", "ftr_ready", "msg_scanned")
            dve.memset(xt[1][:, :, :], 0.0).then_inc(s["state_zeroed"], 1)
            dve.memset(sc[1][:, :], 0.0).then_inc(s["state_zeroed"], 1)
            dve.wait_ge(s["state_zeroed"], 2)

            def add(c, k, t):
                dve.wait_ge(s["g_weighed"], went(c * T + t))
                dve.tensor_reduce(res[k][:, t, :], prod[t % 2][:, :].rearrange("p (k o) -> p o k", o=OUT2), AX.X, ALU.add)\
                   .then_inc(s["g_added"], 1)

            with dve.Fori(0, HALF) as i:
                for k in range(2):
                    c = i * 2 + k
                    for q in range(2):
                        dve.wait_ge(s["x_left"], went(c * 2 + q))
                        dve.wait_ge(s["x_back"], went(c * 2 + q, 4))
                        dve.wait_ge(s["x_scanned"], went(c * 2 + q, 2))
                        dve.tensor_tensor_scan(xt[k][:, q, :], m.keep_pair[:, q, bass.ds(c * W, W)], ps_x[:, :],
                                               xt[1 - k][:, q, W - 1:W], ALU.mult, ALU.add).then_inc(s["x_scanned"], 1)
                    unit = e.unit[:, bass.ds(c * T, T), :]
                    dve.wait_ge(s["a_copied"], went(c * 2 + 1))
                    dve.tensor_tensor(proj[:, :, :, :].rearrange("p t i u -> p t i u"),
                                      inp[k][:, :, 32:UA].rearrange("p t (i u) -> p t i u", i=3),
                                      unit.unsqueeze(3).broadcast_to([128, T, 3, 16]), ALU.mult).then_inc(s["projected"], 1)
                    dve.wait_ge(s["projected"], went(c))
                    dve.tensor_reduce(inp[k][:, :, 16:32], proj[:, :, :, :].rearrange("p t i u -> p t u i"), AX.X, ALU.add)\
                       .then_inc(s["a_ready"], 1)
                    for t in range(T):
                        dve.wait_ge(s["g_made"], went(c * T + t))
                        dve.wait_ge(s["g_added"], went(c * T + t, 2))
                        dve.tensor_tensor(
                            prod[t % 2][:, :].rearrange("p (g k o) -> p g k o", g=2, o=OUT2),
                            ps_g[:, t % 2, :, 0:HK].rearrange("p g (k o) -> p g k o", o=OUT2),
                            e.hidden[:, bass.ds(c * T + t, 1), :].rearrange("p t (g k) -> p (t g) k", g=2)
                            .unsqueeze(3).broadcast_to([128, 2, K2 // 2, OUT2]), ALU.mult).then_inc(s["g_weighed"], 1)
                        if t >= 1:
                            add(c, k, t - 1)
                    add(c, k, T - 1)
                    r4 = res[k][:, :, 24:OUT2].rearrange("p t (i w) -> p t i w", i=3)
                    dve.wait_ge(s["g_added"], went(c * T + T - 1))
                    dve.tensor_tensor(vec[:, :, :, :], res[k][:, :, 16:24].unsqueeze(2).broadcast_to([128, T, 3, 8]),
                                      unit.unsqueeze(3).broadcast_to([128, T, 3, 8]), ALU.mult).then_inc(s["chain"], 1)
                    dve.wait_ge(s["chain"], c * 4 + 1)
                    dve.tensor_tensor(vec[:, :, :, :], vec[:, :, :, :], r4, ALU.add).then_inc(s["chain"], 1)
                    dve.wait_ge(s["acted"], went(c))
                    dve.wait_ge(s["msg_ready"], went(c, 2))
                    dve.tensor_tensor(ftr[k][:, :, 0:8], gated[:, :, 0:8],
                                      e.norm_s[:, bass.ds(c * T, T)].unsqueeze(2).broadcast_to([128, T, 8]), ALU.mult)\
                       .then_inc(s["chain"], 1)
                    dve.tensor_tensor(gated[:, :, 8:16], gated[:, :, 8:16],
                                      e.norm_v[:, bass.ds(c * T, T)].unsqueeze(2).broadcast_to([128, T, 8]), ALU.mult)\
                       .then_inc(s["chain"], 1)
                    dve.wait_ge(s["chain"], c * 4 + 4)
                    dve.tensor_tensor(ftr[k][:, :, 8:D].rearrange("p t (w i) -> p t i w", i=3), vec[:, :, :, :],
                                      gated[:, :, 8:16].unsqueeze(2).broadcast_to([128, T, 3, 8]), ALU.mult)\
                       .then_inc(s["ftr_ready"], 1)
                    dve.sem_inc(s["spread"], 1)
                    scan_messages(dve, m, s, ps_m, sc, c, k, "msg_ready")


def add_step(nc, m, name):
    with Step(nc, name) as st:
        block = st.block()

        @block.vector
        def _(dve):
            dve.tensor_tensor(m.x[:, :], m.x[:, :], m.agg[:, :], ALU.add)


def equi_layer(nc, m):
    norm_step(nc, m, "equi_norm")
    with Step(nc, "equi") as st:
        e = equi_memory(st)
        equi_prepare_step(nc, m, e)
        publish_step(nc, m, "equi_publish")
        equi_edges_step(nc, m, e)
    collect_step(nc, m, "equi_collect", m.sums, m.rows)
    add_step(nc, m, "equi_add")


HOPS = 3


def tag_hop_step(nc, m, name, x):
    with Step(nc, name) as st:
        sb, ps = st.sb, st.ps
        s = st.sems(*front_sems(), *tail_sems(), "table_stored", "state_zeroed", "weighed")
        rows = [sb(f"rows{k}", [128, J, R, D]) for k in range(2)]
        msg = [sb(f"msg{k}", [128, J, R * D]) for k in range(2)]
        ids = [sb(f"ids{k}", [128, T], I32) for k in range(2)]
        sc = [sb(f"sc{k}", [128, W]) for k in range(2)]
        ob = [sb(f"ob{k}", [128, R * J * D]) for k in range(2)]
        ps_m = ps("m", [128, 2, W])
        ps_s = ps("s", [128, J, 128])
        block = st.block()

        @block.sync
        def _(sp):
            grant(sp, s, "out_free")
            sp.dma_start(m.table.rearrange("(p b) f -> p b f", b=BN), x).then_inc(s["table_stored"], 16)
            with sp.Fori(0, HALF) as i:
                for k in range(2):
                    store_sums(sp, m, s, ob, i * 2 + k, k, i)

        @block.gpsimd
        def _(pool):
            pool.wait_ge(s["table_stored"], 16)
            with pool.Fori(0, HALF) as i:
                for k in range(2):
                    gather_sources(pool, m, s, rows, ids, i * 2 + k, k, i)

        @block.vector
        def _(dve):
            grant(dve, s, "rows_transposed", "msg_scanned")
            dve.memset(sc[1][:, :], 0.0).then_inc(s["state_zeroed"], 1)
            dve.wait_ge(s["state_zeroed"], 1)
            with dve.Fori(0, HALF) as i:
                for k in range(2):
                    c = i * 2 + k
                    dve.wait_ge(s[f"src_rows{k}"], (i + 1) * (16 * T))
                    dve.wait_ge(s["msg_ready"], went(c, 2))
                    dve.tensor_tensor(msg[k][:, :, :].rearrange("p j (r f) -> p (j r) f", f=D),
                                      rows[k][:, :, :, :].rearrange("p j r f -> p (j r) f"),
                                      m.ew[:, bass.ds(c * T, T)].unsqueeze(2).broadcast_to([128, T, D]), ALU.mult)\
                       .then_inc(s["rows_transposed"], 1)
                    scan_messages(dve, m, s, ps_m[:, k, :], sc, c, k, "msg_ready")

        @block.tensor
        def _(pe):
            grant(pe, s, "msg_ready", "sums_transposed")
            with pe.Fori(0, HALF) as i:
                for k in range(2):
                    c = i * 2 + k
                    pe.wait_ge(s["rows_transposed"], went(c))
                    pe.wait_ge(s["msg_scanned"], went(c, 2))
                    for j in range(J):
                        last = pe.transpose(ps_m[:, k, j::J], msg[k][:, j, :], m.ident[:, :])
                    last.then_inc(s["msg_ready"], 1)
                    transpose_sums(pe, m, s, sc, ps_s, c, k)

        @block.scalar
        def _(act):
            grant(act, s, "ids_copied", "sums_copied")
            for k in range(2):
                copy_ids(act, m, s, ids, k, k)
            with act.Fori(0, HALF) as i:
                for k in range(2):
                    c = i * 2 + k
                    copy_ids(act, m, s, ids, c + 2, k)
                    copy_sums(act, s, ps_s, ob, c, k)


def tag_mix_step(nc, m, name, hops, weights, bias_in, gamma_in, beta_in, last_layer):
    with Step(nc, name) as st:
        sb, ps = st.sb, st.ps
        s = st.sems("w_loaded", "transposed", "copied", "mixed", *bn_sems())
        b = bn_memory(st)
        w = sb("w", [HOPS * D, D])
        bias, gamma, beta = sb("bias", [PN, D]), sb("gamma", [PN, D]), sb("beta", [PN, D])
        ht = sb("hops_t", [HOPS * D, BN, PN])
        y = sb("y", [PN, BN * D])
        z = sb("z", [PN, BN * D])
        ps_t = ps("t", [HOPS * D, 2, 4, 128])
        ps_o = ps("o", [PN, 2, 512])
        groups = [list(range(t, min(t + 4, BN))) for t in range(0, BN, 4)]
        block = st.block()

        @block.sync
        def _(sp):
            sp.dma_start(w[:, :], weights.rearrange("k f o -> (k f) o")).then_inc(s["w_loaded"], 16)
            for to, v in ((bias, bias_in), (gamma, gamma_in), (beta, beta_in)):
                sp.dma_start(to[:, :], v.partition_broadcast(PN)).then_inc(s["w_loaded"], 16)

        @block.tensor
        def _(pe):
            for t, bs in enumerate(groups):
                if t >= 2:
                    pe.wait_ge(s["copied"], t - 1)
                for x, blk in enumerate(bs):
                    last = pe.transpose(ps_t[:, t % 2, x, 0:PN], hops[:, blk, :], m.ident[0:PN, 0:PN])
                last.then_inc(s["transposed"], 1)
            pe.wait_ge(s["w_loaded"], 64)
            pe.wait_ge(s["copied"], len(groups))
            for blk in range(BN):
                last = pe.matmul(ps_o[:, blk // 16, (blk % 16) * D:(blk % 16) * D + D], ht[:, blk, :], w[:, :],
                                 start=True, stop=True)
            last.then_inc(s["mixed"], 1)
            bn_pe(pe, m, s, b, y)

        @block.scalar
        def _(act):
            bn_act(act, s, b)

        @block.vector
        def _(dve):
            n = [0]

            def step(ins):
                link(dve, s["chain"], n, ins)

            for t, bs in enumerate(groups):
                dve.wait_ge(s["transposed"], t + 1)
                dve.tensor_copy(ht[:, bs[0]:bs[-1] + 1, :], ps_t[:, t % 2, 0:len(bs), 0:PN]).then_inc(s["copied"], 1)
            dve.wait_ge(s["w_loaded"], 64)
            dve.wait_ge(s["mixed"], 1)
            y3 = y[:, :].rearrange("p (b f) -> p b f", f=D)
            bias3 = bias[:, :].unsqueeze(1)
            dve.tensor_tensor(y3[:, 0:16, :], ps_o[:, 0, :].rearrange("p (b f) -> p b f", f=D), bias3.broadcast_to([PN, 16, D]), ALU.add)
            step(dve.tensor_tensor(y3[:, 16:BN, :], ps_o[:, 1, 0:(BN - 16) * D].rearrange("p (b f) -> p b f", f=D),
                                   bias3.broadcast_to([PN, BN - 16, D]), ALU.add))
            bn_dve(dve, s, n, b, y, z, gamma, beta)
            if last_layer:
                step(dve.scalar_tensor_tensor(z[:, :], z[:, :], 0.01, z[:, :], ALU.mult, ALU.max))
                step(dve.tensor_tensor(m.x[:, :], m.x[:, :], z[:, :], ALU.add))
            else:
                z3 = z[:, :].rearrange("p (b f) -> p b f", f=D)
                step(dve.scalar_tensor_tensor(hops[:, :, 0:D], z3, 0.01, z3, ALU.mult, ALU.max))


def take_h_step(nc, m, name, to):
    with Step(nc, name) as st:
        block = st.block()

        @block.vector
        def _(dve):
            dve.tensor_copy(to, m.h[:, :].rearrange("p (b f) -> p b f", f=D))


def tag_layer(nc, m):
    a = m.a
    norm_step(nc, m, "tag_norm")
    with Step(nc, "tag") as st:
        hops = st.sb("hops", [PN, BN, HOPS * D])
        take_h_step(nc, m, "tag_take", hops[:, :, 0:D])
        for conv, w in enumerate(((a.T1, a.tb1, a.tg1, a.tt1), (a.T2, a.tb2, a.tg2, a.tt2))):
            for hop in range(1, HOPS):
                tag_hop_step(nc, m, f"tag{conv}_hop{hop}", hops[:, :, (hop - 1) * D:hop * D])
                collect_step(nc, m, f"tag{conv}_collect{hop}", m.sums, m.rows, hops[:, :, hop * D:(hop + 1) * D])
            tag_mix_step(nc, m, f"tag{conv}_mix", hops, *w, last_layer=(conv == 1))


def store_step(nc, m, out):
    with Step(nc, "store") as st:
        s = st.sems("out_stored")
        block = st.block()

        @block.sync
        def _(sp):
            sp.dma_start(out.rearrange("(p b) f -> p (b f)", b=BN), m.x[:, :]).then_inc(s["out_stored"], 16)
            sp.wait_ge(s["out_stored"], 16)


STOP = 9


def program(nc, a, out):
    with ExitStack() as ctx:
        m = allocate(nc, ctx, a)
        graph_step(nc, m)
        norm_step(nc, m, "mp_norm")
        publish_step(nc, m, "mp_publish")
        mp_edges_step(nc, m)
        collect_step(nc, m, "mp_collect", m.sums, m.rows)
        mp_update_step(nc, m)
        gat_layers(nc, m)
        equi_layer(nc, m)
        tag_layer(nc, m)
        store_step(nc, m, out)


def _edge_major(v, fill):
    pad = np.full((EP - E,) + v.shape[1:], fill, v.dtype)
    w = np.concatenate([v, pad]).reshape((R, C, 128, J) + v.shape[1:])
    w = np.transpose(w, (2, 1, 3, 0) + tuple(range(4, w.ndim)))
    return np.ascontiguousarray(w.reshape((128, C * T) + v.shape[1:]))


def kernel(**inputs):
    import concourse.bacc as _bacc
    from concourse.bass_utils import run_bass_kernel_spmd as _run

    g = {k: np.asarray(v) for k, v in inputs.items()}
    arrays = {
        "x": g["x"],
        "src_t": _edge_major(g["src"], 0),
        "dst_t": _edge_major(g["dst"], N),
        "dst_ext": np.concatenate([np.full(1, -1, np.int32), g["dst"], np.full(EP - E + 1, N, np.int32)]),
        "ew_t": _edge_major(g["edge_weight"], 0),
        "vec_t": _edge_major(g["edge_attr_3"], 1).reshape(128, -1),
        "ef_t": np.pad(g["edge_attr_16"], ((0, EP - E), (0, 0))).reshape(R, RW, 16).transpose(0, 2, 1).reshape(R * 16, RW),
        "emb_t": np.pad(g["edge_attr_10"], ((0, EP - E), (0, 0))).reshape(R, RW, 10).transpose(2, 0, 1),
        "W2e": g["L2_gnn_W2"].reshape(16, 7, 16, 8).transpose(2, 1, 0, 3),
    }
    for short, name in [("W1m", "L0_gnn_W1m"), ("b1m", "L0_gnn_b1m"), ("W2m", "L0_gnn_W2m"), ("b2m", "L0_gnn_b2m"),
                        ("W1u", "L0_gnn_W1u"), ("b1u", "L0_gnn_b1u"), ("W2u", "L0_gnn_W2u"), ("b2u", "L0_gnn_b2u"),
                        ("Wl", "L1_gnn_Wl"), ("bl", "L1_gnn_bl"), ("Wr", "L1_gnn_Wr"), ("br", "L1_gnn_br"),
                        ("att", "L1_gnn_att"), ("cb", "L1_gnn_conv_bias"), ("bng", "L1_gnn_bn_gamma"),
                        ("bnb", "L1_gnn_bn_beta"), ("W1e", "L2_gnn_W1"), ("T1", "L3_gnn_W1"), ("tb1", "L3_gnn_bias1"),
                        ("tg1", "L3_gnn_gamma1"), ("tt1", "L3_gnn_beta1"), ("T2", "L3_gnn_W2"), ("tb2", "L3_gnn_bias2"),
                        ("tg2", "L3_gnn_gamma2"), ("tt2", "L3_gnn_beta2")]:
        arrays[short] = g[name]
    nc = _bacc.Bacc("TRN2", target_bir_lowering=False, num_devices=1)
    a, arrays_in = Mem(), {}
    for name, v in arrays.items():
        v = np.ascontiguousarray(v)
        arrays_in[f"in_{name}"] = v
        a.__dict__[name] = nc.dram_tensor(f"in_{name}", v.shape, mybir.dt.from_np(v.dtype), kind="ExternalInput").ap()
    out = nc.dram_tensor("out", (N, D), F32, kind="ExternalOutput").ap()
    program(nc, a, out)
    got = _run(nc, [arrays_in], core_ids=[0])
    return got.results[0]["out"]
```

```python
import concourse.bass as bass
from concourse import mybir
from concourse.alu_op_type import AluOpType as ALU
from contextlib import ExitStack
import itertools
import numpy as np

F32, I32, BF16, U8 = mybir.dt.float32, mybir.dt.int32, mybir.dt.bfloat16, mybir.dt.uint8
ACT = mybir.ActivationFunctionType
AX = mybir.AxisListType

N, D, E = 3125, 32, 53125
PN, BN = 125, 25
R, J, W = 4, 4, 512
C = -(-E // (R * W))
RW = C * W
EP = R * RW
T = R * J
RS, SW = 16, EP // 16
H = 8
DS = D + H
SR, ZD = EP + 128 * BN, 7
BIG = 1.0e30
HALF = C // 2
CREDIT = 4
EPS = 1e-5


def went(n, back=0):
    return n + 1 + CREDIT - back


class Mem:
    pass


class Step:

    def __init__(self, nc, name):
        self.nc, self.name, self.stack, self.semaphores = nc, name, ExitStack(), []

    def __enter__(self):
        self.stack.__enter__()
        return self

    def __exit__(self, *e):
        done = self.stack.__exit__(*e)
        if self.semaphores:
            self.nc.clear_and_free_semaphores(self.semaphores)
            self.nc.all_engine_barrier()
        return done

    def sb(self, name, shape, dt=F32):
        return self.stack.enter_context(self.nc.sbuf_tensor(f"{self.name}_{name}", shape, dt))

    def ps(self, name, shape, dt=F32):
        return self.stack.enter_context(self.nc.psum_tensor(f"{self.name}_ps_{name}", shape, dt))

    def sems(self, *names):
        made = {n: self.nc.alloc_semaphore(f"{self.name}_{n}") for n in names}
        self.semaphores += made.values()
        return made

    def block(self):
        return self.stack.enter_context(self.nc.Block())


def allocate(nc, ctx, a):
    m = Mem()

    def sb(name, shape, dt):
        return ctx.enter_context(nc.sbuf_tensor(name, shape, dt))

    m.ident = sb("ident", [128, 128], F32)
    m.keep = sb("keep", [128, RW], U8)
    m.keep_pair = sb("keep_pair", [128, 2, RW], U8)
    m.src = sb("src_ids", [128, (C + 2) * T], I32)
    m.ew = sb("edge_weight_sb", [128, C * T], F32)
    m.first = sb("first_edge", [PN, BN], I32)
    m.last = sb("last_edge", [PN, BN], I32)
    m.some = sb("some_edges", [PN, BN], F32)
    m.cross = sb("crosses", [PN, R - 1, BN], F32)
    m.range_dst = sb("range_dst", [R, 1], I32)
    m.x = sb("x_nodes", [PN, BN * D], F32)
    m.h = sb("h_nodes", [PN, BN * D], F32)
    m.h_self = sb("h_self_nodes", [PN, BN, DS], F32)
    m.agg = sb("agg_nodes", [PN, BN * D], F32)
    m.rows = sb("last_rows", [PN, BN, D], F32)
    m.ones = sb("ones_over_n", [PN, PN], F32)
    m.table = nc.dram_tensor("node_table", [N, D], F32).ap()
    m.starts = nc.dram_tensor("starts_dram", [SR, DS], F32).ap()
    m.wide = nc.dram_tensor("node_wide_table", [N, DS], F32).ap()
    m.sums = nc.dram_tensor("sums_dram", [EP, D], F32).ap()
    m.sums_chunks = m.sums.rearrange("(r c p j) f -> c p r (j f)", r=R, c=C, p=128, j=J)
    m.starts_chunks = m.starts[0:EP, :].rearrange("(r c p j) f -> c p j r f", r=R, c=C, p=128, j=J)[..., 0:D]
    m.self_chunks = m.starts[0:EP, :].rearrange("(r c p j) f -> c p j r f", r=R, c=C, p=128, j=J)[..., D:DS]
    m.a = a
    return m


def link(eng, sem, count, ins):
    count[0] += 1
    ins.then_inc(sem, 1)
    eng.wait_ge(sem, count[0])


def graph_step(nc, m):
    a = m.a
    QW = RW // 4
    with Step(nc, "graph") as st:
        sb = st.sb
        s = st.sems("consts_made", "dst_loaded", "small_loaded", "run_loaded0", "run_loaded1", "prep",
                 "onehots_made", "counted", "keep_made", "pair_zeroed", "tot_ready", "base_ready", "zero_made", "zero_stored",
                 "pair_copied", "src_loaded", "chain")
        run = [sb(f"dst_run{k}", [128, QW + 1], I32) for k in range(2)]
        dst = sb("dst_ids", [128, C * T], I32)
        dstf = sb("dst_f", [128, C * T], F32)
        hi = sb("dst_hi", [128, C * T], F32)
        lo = sb("dst_lo", [128, C * T], F32)
        iota_i = sb("iota_i", [128, PN], I32)
        iota = sb("iota_f", [128, PN], F32)
        node_i = sb("node_i", [PN, BN], I32)
        node = sb("node_f", [PN, BN], F32)
        upper = sb("upper", [PN, PN], F32)
        oh_hi = sb("oh_hi", [128, 2, T, PN], BF16)
        oh_lo = sb("oh_lo", [128, 2, T, BN], BF16)
        zeros = sb("zeros", [128, SR * DS // (128 * ZD)], F32)
        cnt = sb("cnt", [PN, BN], F32)
        incl = sb("incl", [PN, BN], F32)
        fst = sb("fst", [PN, BN], F32)
        lst = sb("lst", [PN, BN], F32)
        tmp = sb("tmp", [PN, BN], F32)
        tmp2 = sb("tmp2", [PN, BN], F32)
        base = sb("base", [PN, 1], F32)
        ps_cnt = st.ps("ps_cnt", [PN, BN], F32)
        ps_base = st.ps("ps_base", [PN, 1], F32)
        block = st.block()

        @block.sync
        def _(sp):
            sp.dma_start(dst[:, :], a.dst_t).then_inc(s["dst_loaded"], 16)
            sp.dma_start(m.src[:, 0:C * T], a.src_t).then_inc(s["src_loaded"], 16)
            sp.dma_start(m.ew[:, :], a.ew_t).then_inc(s["small_loaded"], 16)
            sp.dma_start(m.x[:, :], a.x.rearrange("(p b) f -> p (b f)", b=BN)).then_inc(s["small_loaded"], 16)
            sp.dma_start(m.range_dst[:, :], a.dst_ext[1:1 + EP].rearrange("(r e) -> r e", r=R)[:, 0:1],
                         allow_slow_non_contiguous=True).then_inc(s["small_loaded"], 16)
            for q in range(4):
                if q >= 2:
                    sp.wait_ge(s["keep_made"], q - 1)
                for r in range(R):
                    sp.dma_start(run[q % 2][32 * r:32 * r + 32, :],
                                 a.dst_ext[r * RW + q * QW:r * RW + q * QW + QW + 1].partition_broadcast(32))\
                      .then_inc(s["run_loaded0" if q % 2 == 0 else "run_loaded1"], 16)
            sp.wait_ge(s["zero_made"], 1)
            blank = m.starts.rearrange("(p z a) b -> p z (a b)", p=128, z=ZD)
            for z in range(ZD):
                sp.dma_start(blank[:, z, :], zeros[:, :]).then_inc(s["zero_stored"], 16)
            sp.wait_ge(s["pair_zeroed"], 1)
            sp.wait_ge(s["keep_made"], 4)
            for q in range(2):
                for rr in range(2):
                    r = 2 * q + rr
                    sp.dma_start(m.keep_pair[64 * rr + 32:64 * rr + 64, q, :], m.keep[32 * r:32 * r + 32, :])\
                      .then_inc(s["pair_copied"], 16)
            sp.wait_ge(s["pair_copied"], 64)
            sp.wait_ge(s["zero_stored"], 16 * ZD)
            sp.wait_ge(s["small_loaded"], 48)
            sp.wait_ge(s["src_loaded"], 16)

        @block.gpsimd
        def _(pool):
            pool.memset(m.ident[:, :], 0.0).then_inc(s["prep"], 1)
            pool.memset(upper[:, :], 1.0).then_inc(s["prep"], 1)
            pool.memset(m.ones[:, :], 1.0 / N)
            pool.memset(m.src[:, C * T:], 0)
            pool.memset(zeros[:, :], 0.0).then_inc(s["zero_made"], 1)
            pool.iota(iota_i[:, :], [[1, PN]], base=0, channel_multiplier=0)
            pool.iota(node_i[:, :], [[1, BN]], base=0, channel_multiplier=BN)
            pool.wait_ge(s["prep"], 2)
            pool.affine_select(out=m.ident[:, :], in_=m.ident[:, :], compare_op=ALU.not_equal, fill=1.0, base=0,
                               pattern=[[-1, 128]], channel_multiplier=1)
            pool.affine_select(out=upper[:, :], in_=upper[:, :], compare_op=ALU.is_gt, fill=0.0, base=0,
                               pattern=[[1, PN]], channel_multiplier=-1).then_inc(s["consts_made"], 1)
            pool.memset(m.keep_pair[:, :, :], 0).then_inc(s["pair_zeroed"], 1)

        @block.vector
        def _(dve):
            n = [0]
            dve.sem_inc(s["onehots_made"], CREDIT)
            dve.memset(m.h_self[:, :, :], 0.0)
            dve.wait_ge(s["dst_loaded"], 16)
            dve.wait_ge(s["consts_made"], 1)
            dve.tensor_copy(iota[:, :], iota_i[:, :])
            dve.tensor_copy(node[:, :], node_i[:, :])
            link(dve, s["chain"], n, dve.tensor_copy(dstf[:, :], dst[:, :]))
            link(dve, s["chain"], n, dve.tensor_scalar(hi[:, :], dstf[:, :], 1.0 / BN, 0.48, ALU.mult, ALU.subtract))
            link(dve, s["chain"], n, dve.tensor_scalar(hi[:, :], hi[:, :], 12582912.0, None, ALU.add))
            link(dve, s["chain"], n, dve.tensor_scalar(hi[:, :], hi[:, :], 12582912.0, None, ALU.subtract))
            link(dve, s["chain"], n, dve.scalar_tensor_tensor(lo[:, :], hi[:, :], -float(BN), dstf[:, :], ALU.mult, ALU.add))

            def onehots(c, k):
                dve.wait_ge(s["counted"], went(c, 2))
                dve.tensor_tensor(oh_hi[:, k, :, :], iota[:, :].unsqueeze(1).broadcast_to([128, T, PN]),
                                  hi[:, bass.ds(c * T, T)].unsqueeze(2).broadcast_to([128, T, PN]), ALU.is_equal)
                dve.tensor_tensor(oh_lo[:, k, :, :], iota[:, 0:BN].unsqueeze(1).broadcast_to([128, T, BN]),
                                  lo[:, bass.ds(c * T, T)].unsqueeze(2).broadcast_to([128, T, BN]), ALU.is_equal)\
                   .then_inc(s["onehots_made"], 1)

            with dve.Fori(0, HALF) as i:
                for k in range(2):
                    onehots(i * 2 + k, k)

            for q in range(4):
                dve.wait_ge(s["run_loaded0" if q % 2 == 0 else "run_loaded1"], 64 * (q // 2 + 1))
                dve.tensor_tensor(m.keep[:, q * QW:(q + 1) * QW], run[q % 2][:, 1:QW + 1], run[q % 2][:, 0:QW],
                                  ALU.is_equal).then_inc(s["keep_made"], 1)

            dve.wait_ge(s["counted"], went(C))
            link(dve, s["chain"], n, dve.tensor_copy(cnt[:, :], ps_cnt[:, :]))
            link(dve, s["chain"], n, dve.memset(tmp[:, :], 1.0))
            link(dve, s["chain"], n, dve.tensor_tensor_scan(incl[:, :], tmp[:, :], cnt[:, :], 0.0, ALU.mult, ALU.add))
            dve.sem_inc(s["tot_ready"], 1)
            dve.wait_ge(s["base_ready"], 1)
            link(dve, s["chain"], n, dve.tensor_copy(base[:, :], ps_base[:, :]))
            link(dve, s["chain"], n, dve.tensor_scalar(lst[:, :], incl[:, :], base[:, 0:1], 1.0, ALU.add, ALU.subtract))
            link(dve, s["chain"], n, dve.scalar_tensor_tensor(fst[:, :], lst[:, :], 1.0, cnt[:, :], ALU.add, ALU.subtract))
            link(dve, s["chain"], n, dve.tensor_scalar(m.some[:, :], cnt[:, :], 1.0, None, ALU.min))
            for r in range(1, R):
                link(dve, s["chain"], n, dve.tensor_scalar(tmp[:, :], fst[:, :], float(r * RW), None, ALU.is_lt))
                link(dve, s["chain"], n, dve.tensor_scalar(tmp2[:, :], lst[:, :], float(r * RW), None, ALU.is_ge))
                link(dve, s["chain"], n, dve.tensor_tensor(m.cross[:, r - 1, :], tmp[:, :], tmp2[:, :], ALU.mult))
            link(dve, s["chain"], n, dve.tensor_scalar(m.last[:, :], lst[:, :], 0.0, None, ALU.max))
            link(dve, s["chain"], n, dve.scalar_tensor_tensor(tmp[:, :], node[:, :], float(EP), fst[:, :], ALU.add, ALU.subtract))
            link(dve, s["chain"], n, dve.tensor_scalar(tmp2[:, :], m.some[:, :], -1.0, 1.0, ALU.mult, ALU.add))
            link(dve, s["chain"], n, dve.tensor_tensor(tmp[:, :], tmp[:, :], tmp2[:, :], ALU.mult))
            link(dve, s["chain"], n, dve.tensor_tensor(m.first[:, :], tmp[:, :], fst[:, :], ALU.add))

        @block.tensor
        def _(pe):
            pe.sem_inc(s["counted"], CREDIT)
            pe.wait_ge(s["zero_made"], 1)
            pe.wait_ge(s["onehots_made"], went(0))
            pe.matmul(ps_cnt[:, :], zeros[:, 0:PN], zeros[:, 0:BN], start=True, stop=False)
            with pe.Fori(0, HALF) as i:
                for k in range(2):
                    pe.wait_ge(s["onehots_made"], went(i * 2 + k))
                    for t in range(T):
                        last = pe.matmul(ps_cnt[:, :], oh_hi[:, k, t, :], oh_lo[:, k, t, :], start=False, stop=False)
                    last.then_inc(s["counted"], 1)
            pe.matmul(ps_cnt[:, :], zeros[:, 0:PN], zeros[:, 0:BN], start=False, stop=True).then_inc(s["counted"], 1)
            pe.wait_ge(s["tot_ready"], 1)
            pe.wait_ge(s["consts_made"], 1)
            pe.matmul(ps_base[:, :], upper[:, :], incl[:, BN - 1:BN], start=True, stop=True).then_inc(s["base_ready"], 1)


def norm_step(nc, m, name):
    with Step(nc, name) as st:
        s = st.sems("chain", "var_ready", "std_ready")
        tmp = st.sb("tmp", [PN, BN * D])
        mean = st.sb("mean", [PN, BN])
        var = st.sb("var", [PN, BN])
        block = st.block()

        @block.vector
        def _(dve):
            n = [0]

            def step(ins):
                link(dve, s["chain"], n, ins)

            x3 = m.x[:, :].rearrange("p (b f) -> p b f", f=D)
            t3 = tmp[:, :].rearrange("p (b f) -> p b f", f=D)
            o3 = m.h[:, :].rearrange("p (b f) -> p b f", f=D)
            step(dve.tensor_reduce(mean[:, :], x3, AX.X, ALU.add))
            step(dve.tensor_scalar(mean[:, :], mean[:, :], 1.0 / D, None, ALU.mult))
            step(dve.tensor_tensor(o3, x3, mean[:, :].unsqueeze(2).broadcast_to([PN, BN, D]), ALU.subtract))
            step(dve.tensor_tensor(t3, o3, o3, ALU.mult))
            step(dve.tensor_reduce(var[:, :], t3, AX.X, ALU.add))
            dve.tensor_scalar(var[:, :], var[:, :], 1.0 / D, EPS, ALU.mult, ALU.add).then_inc(s["var_ready"], 1)
            dve.wait_ge(s["std_ready"], 1)
            step(dve.reciprocal(var[:, :], var[:, :]))
            step(dve.tensor_tensor(t3, o3, var[:, :].unsqueeze(2).broadcast_to([PN, BN, D]), ALU.mult))
            step(dve.tensor_scalar(m.h[:, :], tmp[:, :], 0.0, None, ALU.max))

        @block.scalar
        def _(act):
            act.wait_ge(s["var_ready"], 1)
            act.activation(var[:, :], var[:, :], ACT.Sqrt).then_inc(s["std_ready"], 1)


def publish_step(nc, m, name):
    with Step(nc, name) as st:
        s = st.sems("rows_ready", "table_stored", "rows_scattered", "border_rows", "border_stored")
        border = st.sb("border", [R, DS])
        block = st.block()

        @block.vector
        def _(dve):
            dve.tensor_copy(m.h_self[:, :, 0:D], m.h[:, :].rearrange("p (b f) -> p b f", f=D)).then_inc(s["rows_ready"], 1)

        @block.sync
        def _(sp):
            sp.dma_start(m.table.rearrange("(p b) f -> p (b f)", b=BN), m.h[:, :]).then_inc(s["table_stored"], 16)
            sp.wait_ge(s["rows_ready"], 1)
            sp.dma_start(m.wide.rearrange("(p b) f -> p (b f)", b=BN), m.h_self[:, :, :].rearrange("p b f -> p (b f)"))\
              .then_inc(s["table_stored"], 16)
            sp.wait_ge(s["table_stored"], 32)
            sp.wait_ge(s["rows_scattered"], 16 * BN)
            sp.wait_ge(s["border_rows"], 16)
            sp.dma_start(m.starts[0:EP, :].rearrange("(r e) f -> r e f", r=R)[:, 0, :], border[:, :])\
              .then_inc(s["border_stored"], 16)
            sp.wait_ge(s["border_stored"], 16)

        @block.gpsimd
        def _(pool):
            pool.wait_ge(s["rows_ready"], 1)
            for b in range(BN):
                pool.indirect_dma_start(m.starts, bass.IndirectOffsetOnAxis(ap=m.first[:, b:b + 1], axis=0),
                                        m.h_self[:, b, :], None).then_inc(s["rows_scattered"], 16)
            pool.wait_ge(s["table_stored"], 32)
            pool.indirect_dma_start(border[:, :], None, m.wide,
                                    bass.IndirectOffsetOnAxis(ap=m.range_dst[:, 0:1], axis=0))\
                .then_inc(s["border_rows"], 16)
            pool.wait_ge(s["border_rows"], 16)


def collect_step(nc, m, name, sums, rows, to=None):
    width = rows.shape[2]
    with Step(nc, name) as st:
        s = st.sems("chain", "border_loaded", "rows_gathered")
        tmp = st.sb("tmp", [PN, BN, D])
        edge = st.sb("edge", [PN, R - 1, D])
        block = st.block()

        @block.sync
        def _(sp):
            for r in range(1, R):
                sp.dma_start(edge[:, r - 1, :], sums[r * RW - 1, 0:D].partition_broadcast(PN))\
                  .then_inc(s["border_loaded"], 16)
            sp.wait_ge(s["border_loaded"], 16 * (R - 1))

        @block.gpsimd
        def _(pool):
            for b in range(BN):
                pool.indirect_dma_start(rows[:, b, :], None, sums,
                                        bass.IndirectOffsetOnAxis(ap=m.last[:, b:b + 1], axis=0))\
                    .then_inc(s["rows_gathered"], 16)
            pool.wait_ge(s["rows_gathered"], 16 * BN)

        @block.vector
        def _(dve):
            n = [0]
            a3 = m.agg[:, :].rearrange("p (b f) -> p b f", f=D) if to is None else to
            dve.wait_ge(s["rows_gathered"], 16 * BN)
            dve.wait_ge(s["border_loaded"], 16 * (R - 1))
            link(dve, s["chain"], n, dve.tensor_tensor(a3, rows[:, :, 0:D], m.some[:, :].unsqueeze(2).broadcast_to([PN, BN, D]), ALU.mult))
            for r in range(R - 1):
                link(dve, s["chain"], n, dve.tensor_tensor(
                    tmp[:, :, :], m.cross[:, r, :].unsqueeze(2).broadcast_to([PN, BN, D]),
                    edge[:, r, :].unsqueeze(1).broadcast_to([PN, BN, D]), ALU.mult))
                link(dve, s["chain"], n, dve.tensor_tensor(a3, a3, tmp[:, :, :], ALU.add))


def front_sems():
    return ["ids_copied", "src_rows0", "src_rows1", "dst_rows0", "dst_rows1", "rows_transposed", "x_scanned",
            "pool_turn"]


def gather_sources(pool, m, s, rows, ids, c, k, i):
    pool.wait_ge(s["rows_transposed"], went(c, 2))
    pool.wait_ge(s["ids_copied"], went(c))
    pool.sem_inc(s["pool_turn"], 1)
    alone = len(rows[k].shape) == 4
    for j in range(J):
        for r in range(R):
            pool.indirect_dma_start(rows[k][:, j, r, :] if alone else rows[k][:, j, r, 0, :], None, m.table,
                                    bass.IndirectOffsetOnAxis(ap=ids[k][:, j * R + r:j * R + r + 1], axis=0))\
                .then_inc(s[f"src_rows{k}"], 16)


def copy_ids(act, m, s, ids, c, k):
    act.wait_ge(s["rows_transposed"], went(c, 2))
    act.activation(ids[k][:, :], m.src[:, bass.ds(c * T, T)], ACT.Copy).then_inc(s["ids_copied"], 1)


def load_starts(sp, m, s, rows, c, k):
    sp.wait_ge(s["rows_transposed"], went(c, 2))
    for j in range(J):
        sp.dma_start(rows[k][:, j, :, 1, :], m.starts_chunks[c, :, j, :, :]).then_inc(s[f"dst_rows{k}"], 16)


def transpose_rows(pe, m, s, rows, ps_x, c, k, i):
    pe.wait_ge(s[f"src_rows{k}"], (i + 1) * (16 * T))
    pe.wait_ge(s[f"dst_rows{k}"], (i + 1) * (16 * J))
    pe.wait_ge(s["x_scanned"], went(c, 1))
    for q in range(2):
        for j in range(J):
            last = pe.transpose(ps_x[:, q, j::J], rows[k][:, j, 2 * q:2 * q + 2, :, :], m.ident[:, :])
    last.then_inc(s["rows_transposed"], 1)


def scan_rows(dve, m, s, ps_x, xt, c, k):
    dve.wait_ge(s["rows_transposed"], went(c))
    dve.wait_ge(s["x_scanned"], went(c, 1))
    dve.tensor_tensor_scan(xt[k][:, 0, :], m.keep_pair[:, 0, bass.ds(c * W, W)], ps_x[:, 0, :],
                           xt[1 - k][:, 0, W - 1:W], ALU.mult, ALU.add)
    dve.tensor_tensor_scan(xt[k][:, 1, :], m.keep_pair[:, 1, bass.ds(c * W, W)], ps_x[:, 1, :],
                           xt[1 - k][:, 1, W - 1:W], ALU.mult, ALU.add).then_inc(s["x_scanned"], 1)


def tail_sems():
    return ["msg_ready", "msg_scanned", "sums_transposed", "sums_copied", "sums_stored0", "sums_stored1", "out_free"]


def scan_messages(dve, m, s, msg, sc, c, k, ready):
    dve.wait_ge(s[ready], went(c))
    dve.wait_ge(s["sums_transposed"], went(c, 2))
    dve.wait_ge(s["msg_scanned"], went(c, 1))
    dve.tensor_tensor_scan(sc[k][:, :], m.keep[:, bass.ds(c * W, W)], msg, sc[1 - k][:, W - 1:W],
                           ALU.mult, ALU.add).then_inc(s["msg_scanned"], 1)


def transpose_sums(pe, m, s, sc, ps_s, c, k):
    pe.wait_ge(s["msg_scanned"], went(c))
    pe.wait_ge(s["sums_copied"], went(c, 1))
    for j in range(J):
        last = pe.transpose(ps_s[:, j, :], sc[k][:, j::J], m.ident[:, :])
    last.then_inc(s["sums_transposed"], 1)


def copy_sums(act, s, ps_s, ob, c, k):
    act.wait_ge(s["sums_transposed"], went(c))
    act.wait_ge(s["out_free"], went(c, 2))
    act.activation(ob[k][:, :].rearrange("p (r j f) -> p j r f", r=R, j=J),
                   ps_s[:, :, :].rearrange("p j (r f) -> p j r f", r=R), ACT.Copy).then_inc(s["sums_copied"], 1)


def store_sums(sp, m, s, ob, c, k, i):
    sp.wait_ge(s["sums_copied"], went(c))
    sp.dma_start(m.sums_chunks[c], ob[k][:, :].rearrange("p (r n) -> p r n", r=R)).then_inc(s[f"sums_stored{k}"], 16)
    sp.wait_ge(s[f"sums_stored{k}"], (i + 1) * 16)
    sp.sem_inc(s["out_free"], 1)


def grant(eng, s, *names):
    for n in names:
        eng.sem_inc(s[n], CREDIT)


def mp_edges_step(nc, m):
    a = m.a
    with Step(nc, "mp_edges") as st:
        sb = st.sb
        ps = st.ps
        s = st.sems(*front_sems(), *tail_sems(), "w_zeroed", "w_loaded", "ef_loaded0", "ef_loaded1",
                 "hidden_ready", "msg_made", "state_zeroed", "x_used")
        rows = [sb(f"rows{k}", [128, J, R, 2, D]) for k in range(2)]
        ids = [sb(f"ids{k}", [128, T], I32) for k in range(2)]
        xt = [sb(f"xt{k}", [128, 2, W]) for k in range(2)]
        ef = [sb(f"ef{k}", [R * 16, W]) for k in range(2)]
        hid = [sb(f"hid{k}", [128, 2, W]) for k in range(2)]
        msg = [sb(f"msg{k}", [128, W]) for k in range(2)]
        sc = [sb(f"sc{k}", [128, W]) for k in range(2)]
        ob = [sb(f"ob{k}", [128, R * J * D]) for k in range(2)]
        w1x = sb("w1x", [128, 2 * 64])
        w1e = sb("w1e", [R * 16, 2, 2 * 64])
        w2 = sb("w2m", [128, 2, 128])
        b1 = sb("b1m", [128, 1])
        b2 = sb("b2m", [128, 1])
        ps_x = ps("ps_x", [128, 2, W])
        ps_u = ps("ps_u", [128, 2, W])
        ps_m = ps("ps_m", [128, W])
        ps_s = ps("ps_s", [128, J, 128])
        block = st.block()
        n_w = 4 + 4 + 4 + 2 + 4

        @block.sync
        def _(sp):
            grant(sp, s, "out_free")
            for c in range(2):
                load_starts(sp, m, s, rows, c, c)
                sp.dma_start(ef[c][:, :], a.ef_t[:, c * W:(c + 1) * W]).then_inc(s[f"ef_loaded{c}"], 16)
            sp.wait_ge(s["w_zeroed"], 1)
            for rr in range(2):
                for sd in range(2):
                    sp.dma_start(w1x[64 * rr + 32 * sd:64 * rr + 32 * sd + 32, 64 * rr:64 * rr + 64],
                                 a.W1m[32 * (1 - sd):32 * (1 - sd) + 32, :]).then_inc(s["w_loaded"], 16)
                sp.dma_start(b1[64 * rr:64 * rr + 64, :], a.b1m.unsqueeze(1), allow_slow_non_contiguous=True).then_inc(s["w_loaded"], 16)
            for r in range(R):
                q, rr = r // 2, r % 2
                sp.dma_start(w1e[16 * r:16 * r + 16, q, 64 * rr:64 * rr + 64], a.W1m[64:80, :]).then_inc(s["w_loaded"], 16)
                sp.dma_start(w2[64 * rr:64 * rr + 64, q, 32 * r:32 * r + 32], a.W2m).then_inc(s["w_loaded"], 16)
                sp.dma_start(b2[32 * r:32 * r + 32, :], a.b2m.unsqueeze(1), allow_slow_non_contiguous=True).then_inc(s["w_loaded"], 16)

            def load(c, k):
                load_starts(sp, m, s, rows, c, k)
                sp.wait_ge(s["x_used"], went(c, 2))
                sp.dma_start(ef[k][:, :], a.ef_t[:, bass.ds(c * W, W)]).then_inc(s[f"ef_loaded{k}"], 16)

            with sp.Fori(0, HALF - 1) as i:
                for k in range(2):
                    load(i * 2 + k + 2, k)
                    store_sums(sp, m, s, ob, i * 2 + k, k, i)
            for k in range(2):
                store_sums(sp, m, s, ob, C - 2 + k, k, HALF - 1)

        @block.gpsimd
        def _(pool):
            pool.memset(w1x[:, :], 0.0)
            pool.memset(w1e[:, :, :], 0.0)
            pool.memset(w2[:, :, :], 0.0).then_inc(s["w_zeroed"], 1)
            with pool.Fori(0, HALF) as i:
                for k in range(2):
                    gather_sources(pool, m, s, rows, ids, i * 2 + k, k, i)

        @block.scalar
        def _(act):
            grant(act, s, "ids_copied", "hidden_ready", "msg_ready", "sums_copied")
            for k in range(2):
                copy_ids(act, m, s, ids, k, k)
            act.wait_ge(s["w_loaded"], 16 * n_w)
            with act.Fori(0, HALF) as i:
                for k in range(2):
                    c = i * 2 + k
                    copy_ids(act, m, s, ids, c + 2, k)
                    act.wait_ge(s["x_used"], went(c))
                    act.wait_ge(s["msg_made"], went(c, 2))
                    for q in range(2):
                        last = act.activation(hid[k][:, q, :], ps_u[:, q, :], ACT.Relu, bias=b1[:, 0:1])
                    last.then_inc(s["hidden_ready"], 1)
                    act.wait_ge(s["msg_made"], went(c))
                    act.wait_ge(s["msg_scanned"], went(c, 2))
                    act.activation(msg[k][:, :], ps_m[:, :], ACT.Identity, bias=b2[:, 0:1]).then_inc(s["msg_ready"], 1)
                    copy_sums(act, s, ps_s, ob, c, k)

        @block.tensor
        def _(pe):
            grant(pe, s, "rows_transposed", "x_used", "msg_made", "sums_transposed")
            pe.wait_ge(s["w_loaded"], 16 * n_w)
            with pe.Fori(0, HALF) as i:
                for k in range(2):
                    c = i * 2 + k
                    transpose_rows(pe, m, s, rows, ps_x, c, k, i)
                    pe.wait_ge(s["x_scanned"], went(c))
                    pe.wait_ge(s[f"ef_loaded{k}"], (i + 1) * 16)
                    pe.wait_ge(s["hidden_ready"], went(c, 1))
                    for q in range(2):
                        pe.matmul(ps_u[:, q, :], w1x[:, :], xt[k][:, q, :], start=True, stop=False)
                        last = pe.matmul(ps_u[:, q, :], w1e[:, q, :], ef[k][:, :], start=False, stop=True)
                    last.then_inc(s["x_used"], 1)
                    pe.wait_ge(s["hidden_ready"], went(c))
                    pe.wait_ge(s["msg_ready"], went(c, 1))
                    pe.matmul(ps_m[:, :], w2[:, 0, :], hid[k][:, 0, :], start=True, stop=False)
                    pe.matmul(ps_m[:, :], w2[:, 1, :], hid[k][:, 1, :], start=False, stop=True).then_inc(s["msg_made"], 1)
                    transpose_sums(pe, m, s, sc, ps_s, c, k)

        @block.vector
        def _(dve):
            grant(dve, s, "x_scanned", "msg_scanned")
            dve.memset(xt[1][:, :, :], 0.0).then_inc(s["state_zeroed"], 1)
            dve.memset(sc[1][:, :], 0.0).then_inc(s["state_zeroed"], 1)
            dve.wait_ge(s["state_zeroed"], 2)
            with dve.Fori(0, HALF) as i:
                for k in range(2):
                    c = i * 2 + k
                    dve.wait_ge(s["x_used"], went(c, 2))
                    scan_rows(dve, m, s, ps_x, xt, c, k)
                    scan_messages(dve, m, s, msg[k][:, :], sc, c, k, "msg_ready")


def mp_update_step(nc, m):
    a = m.a
    GB = 4
    with Step(nc, "mp_update") as st:
        sb = st.sb
        ps = st.ps
        s = st.sems("w_loaded", "joined", "transposed", "copied", "hidden_made", "hidden_ready", "out_made", "added", "bias_added")
        both = sb("both", [PN, BN, 2 * D])
        bt = sb("both_t", [2 * D, BN, PN])
        hid = sb("hid_u", [64, BN, PN])
        w1 = sb("w1u", [64, 64])
        w2 = sb("w2u", [64, D])
        b1 = sb("b1u", [64, 1])
        b2 = sb("b2u", [PN, D])
        ps_t = ps("ps_t", [64, 2, GB, 128])
        ps_h = ps("ps_h", [64, 2, GB * PN + 12])
        ps_o = ps("ps_o", [PN, 2, 512])
        groups = [list(range(g, min(g + GB, BN))) for g in range(0, BN, GB)]
        block = st.block()

        @block.sync
        def _(sp):
            sp.dma_start(w1[:, :], a.W1u).then_inc(s["w_loaded"], 16)
            sp.dma_start(w2[:, :], a.W2u).then_inc(s["w_loaded"], 16)
            sp.dma_start(b1[:, :], a.b1u.unsqueeze(1), allow_slow_non_contiguous=True).then_inc(s["w_loaded"], 16)
            sp.dma_start(b2[:, :], a.b2u.partition_broadcast(PN)).then_inc(s["w_loaded"], 16)

        @block.vector
        def _(dve):
            dve.tensor_copy(both[:, :, 0:D], m.h[:, :].rearrange("p (b f) -> p b f", f=D))
            dve.tensor_copy(both[:, :, D:2 * D], m.agg[:, :].rearrange("p (b f) -> p b f", f=D)).then_inc(s["joined"], 1)
            for g, bs in enumerate(groups):
                dve.wait_ge(s["transposed"], g + 1)
                dve.tensor_copy(bt[:, bs[0]:bs[-1] + 1, :], ps_t[:, g % 2, 0:len(bs), 0:PN]).then_inc(s["copied"], 1)
            dve.wait_ge(s["w_loaded"], 64)
            x3 = m.x[:, :].rearrange("p (b f) -> p b f", f=D)
            dve.tensor_tensor(x3, x3, b2[:, :].unsqueeze(1).broadcast_to([PN, BN, D]), ALU.add).then_inc(s["bias_added"], 1)
            dve.wait_ge(s["bias_added"], 1)
            dve.wait_ge(s["out_made"], 1)
            dve.tensor_tensor(m.x[:, 0:512], m.x[:, 0:512], ps_o[:, 0, :], ALU.add)
            dve.tensor_tensor(m.x[:, 512:800], m.x[:, 512:800], ps_o[:, 1, 0:288], ALU.add).then_inc(s["added"], 1)

        @block.scalar
        def _(act):
            act.wait_ge(s["w_loaded"], 64)
            for g, bs in enumerate(groups):
                act.wait_ge(s["hidden_made"], g + 1)
                act.activation(hid[:, bs[0]:bs[-1] + 1, :],
                               ps_h[:, g % 2, 0:len(bs) * PN].rearrange("p (b n) -> p b n", n=PN), ACT.Relu,
                               bias=b1[:, 0:1]).then_inc(s["hidden_ready"], 1)

        @block.tensor
        def _(pe):
            pe.wait_ge(s["joined"], 1)
            pe.wait_ge(s["w_loaded"], 64)
            for g, bs in enumerate(groups):
                if g >= 2:
                    pe.wait_ge(s["copied"], g - 1)
                for t, b in enumerate(bs):
                    last = pe.transpose(ps_t[:, g % 2, t, 0:PN], both[:, b, :], m.ident[0:PN, 0:PN])
                last.then_inc(s["transposed"], 1)
                pe.wait_ge(s["copied"], g + 1)
                if g >= 2:
                    pe.wait_ge(s["hidden_ready"], g - 1)
                pe.matmul(ps_h[:, g % 2, 0:len(bs) * PN], w1[:, :], bt[:, bs[0]:bs[-1] + 1, :], start=True, stop=True)\
                  .then_inc(s["hidden_made"], 1)
            pe.wait_ge(s["hidden_ready"], len(groups))
            for b in range(BN):
                last = pe.matmul(ps_o[:, b // 16, (b % 16) * D:(b % 16) * D + D], hid[:, b, :], w2[:, :],
                                 start=True, stop=True)
            last.then_inc(s["out_made"], 1)


BA = 13


def bn_sems():
    return ["chain", "stat_in", "stat_out", "bn_var", "bn_std"]


def bn_memory(st):
    return dict(sq=st.sb("bn_sq", [PN, BN * D]), part=st.sb("bn_part", [PN, 2, D]), mean=st.sb("bn_mean", [PN, D]),
                rstd=st.sb("bn_rstd", [PN, D]), ps=st.ps("bn_ps", [PN, 2, 512]))


def bn_dve(dve, s, n, b, y, out, gamma, beta):
    y3 = y[:, :].rearrange("p (b f) -> p b f", f=D)
    o3 = out[:, :].rearrange("p (b f) -> p b f", f=D)

    def over_nodes(turn, to):
        dve.sem_inc(s["stat_in"], 1)
        dve.wait_ge(s["stat_out"], turn)
        dve.tensor_reduce(b["part"][:, 0, :], b["ps"][:, 0, 0:BA * D].rearrange("p (b f) -> p f b", f=D), AX.X, ALU.add)
        link(dve, s["chain"], n, dve.tensor_reduce(
            b["part"][:, 1, :], b["ps"][:, 1, 0:(BN - BA) * D].rearrange("p (b f) -> p f b", f=D), AX.X, ALU.add))
        link(dve, s["chain"], n, dve.tensor_tensor(to[:, :], b["part"][:, 0, :], b["part"][:, 1, :], ALU.add))

    over_nodes(1, b["mean"])
    link(dve, s["chain"], n, dve.tensor_tensor(y3, y3, b["mean"][:, :].unsqueeze(1).broadcast_to([PN, BN, D]), ALU.subtract))
    link(dve, s["chain"], n, dve.tensor_tensor(b["sq"][:, :], y[:, :], y[:, :], ALU.mult))
    over_nodes(2, b["rstd"])
    dve.tensor_scalar(b["rstd"][:, :], b["rstd"][:, :], EPS, None, ALU.add).then_inc(s["bn_var"], 1)
    dve.wait_ge(s["bn_std"], 1)
    link(dve, s["chain"], n, dve.reciprocal(b["rstd"][:, :], b["rstd"][:, :]))
    link(dve, s["chain"], n, dve.tensor_tensor(b["rstd"][:, :], b["rstd"][:, :], gamma[:, :], ALU.mult))
    link(dve, s["chain"], n, dve.tensor_tensor(y3, y3, b["rstd"][:, :].unsqueeze(1).broadcast_to([PN, BN, D]), ALU.mult))
    link(dve, s["chain"], n, dve.tensor_tensor(o3, y3, beta[:, :].unsqueeze(1).broadcast_to([PN, BN, D]), ALU.add))


def bn_pe(pe, m, s, b, y):
    for turn, v in enumerate((y, b["sq"])):
        pe.wait_ge(s["stat_in"], turn + 1)
        pe.matmul(b["ps"][:, 0, 0:BA * D], m.ones[:, :], v[:, 0:BA * D], start=True, stop=True)
        pe.matmul(b["ps"][:, 1, 0:(BN - BA) * D], m.ones[:, :], v[:, BA * D:BN * D], start=True, stop=True)\
          .then_inc(s["stat_out"], 1)


def bn_act(act, s, b):
    act.wait_ge(s["bn_var"], 1)
    act.activation(b["rstd"][:, :], b["rstd"][:, :], ACT.Sqrt).then_inc(s["bn_std"], 1)


def gat_memory(nc, st, m):
    g = Mem()
    g.keep = st.sb("keep", [128, SW], U8)
    g.keep_back = st.sb("keep_back", [128, SW], U8)
    g.head = st.sb("head", [128, SW], U8)
    g.tail = st.sb("tail", [128, SW], U8)
    g.keep_pen = st.sb("keep_pen", [128, SW], BF16)
    g.back_pen = st.sb("back_pen", [128, SW], BF16)
    g.head_pen = st.sb("head_pen", [128, SW], BF16)
    g.tail_pen = st.sb("tail_pen", [128, SW], BF16)
    g.of_head = st.sb("of_head", [128, H])
    g.of_range = st.sb("of_range", [128, RS])
    g.of_head_t = st.sb("of_head_t", [H, 128])
    g.one_run = st.sb("one_run", [H, 2, RS])
    g.one_pen = st.sb("one_pen", [H, 2, RS])
    g.rep = st.sb("rep", [3 * R * H, H, 128], BF16)
    g.keep_heads = st.sb("keep_heads", [R * H, RW], U8)
    g.h_t = st.sb("h_t", [D, BN, PN])
    g.rows = st.sb("rows", [PN, BN, DS])
    g.self_logits = nc.dram_tensor("gat_self_logits", [R, H, RW], F32).ap()
    g.self_alpha = nc.dram_tensor("gat_self_alpha", [R * H, RW], F32).ap()
    g.sums = nc.dram_tensor("gat_sums", [EP, DS], F32).ap()
    g.values = nc.dram_tensor("gat_values", [128, RW], F32).ap()
    g.logits = nc.dram_tensor("gat_logits", [R, H, RW], F32).ap()
    g.alpha = nc.dram_tensor("gat_alpha", [3 * R * H, RW], BF16).ap()
    return g


def gat_prepare_step(nc, m, g):
    with Step(nc, "gat_prepare") as st:
        s = st.sems("keep_copied", "ids_loaded", "chain", "flags_ready", "flags_small", "head_ready", "head_t_made")
        run = st.sb("run", [128, SW + 2], I32)
        flags = st.sb("flags", [128, 2, RS])
        ps_f = st.ps("flags", [H, 2, RS])
        ps_h = st.ps("head_t", [H, 128])
        block = st.block()

        @block.sync
        def _(sp):
            for q in range(RS):
                sp.dma_start(run[H * q:H * q + H, :], m.a.dst_ext[q * SW:q * SW + SW + 2].partition_broadcast(H))\
                  .then_inc(s["ids_loaded"], 16)
            for r in range(R):
                sp.dma_start(g.keep_heads[H * r:H * r + H, :], m.keep[32 * r:32 * r + H, :]).then_inc(s["keep_copied"], 16)
            sp.wait_ge(s["keep_copied"], 16 * R)

        @block.vector
        def _(dve):
            n = [0]

            def step(ins):
                link(dve, s["chain"], n, ins)

            dve.wait_ge(s["ids_loaded"], 16 * RS)
            step(dve.tensor_tensor(g.keep[:, :], run[:, 1:SW + 1], run[:, 0:SW], ALU.is_equal))
            step(dve.tensor_tensor(g.keep_back[:, :], run[:, 1:SW + 1], run[:, 2:SW + 2], ALU.is_equal))
            step(dve.tensor_tensor_scan(g.head[:, :], g.keep[:, :], g.keep[:, :], 1.0, ALU.mult, ALU.mult))
            step(dve.tensor_tensor_scan(g.tail[:, ::-1], g.keep_back[:, ::-1], g.keep_back[:, ::-1], 1.0, ALU.mult, ALU.mult))
            for flag, pen in ((g.keep, g.keep_pen), (g.keep_back, g.back_pen), (g.head, g.head_pen), (g.tail, g.tail_pen)):
                step(dve.tensor_scalar(pen[:, :], flag[:, :], -1.0, BIG, ALU.add, ALU.mult))
            ident3 = m.ident[:, :].rearrange("p (r h) -> p r h", h=H)
            step(dve.tensor_reduce(g.of_range[:, :], ident3, AX.X, ALU.add))
            dve.tensor_reduce(g.of_head[:, :], m.ident[:, :].rearrange("p (r h) -> p h r", h=H), AX.X, ALU.add)\
               .then_inc(s["head_ready"], 1)
            step(dve.tensor_scalar(flags[:, 0, :], g.of_range[:, :], g.head[:, SW - 1:SW], None, ALU.mult))
            dve.tensor_scalar(flags[:, 1, :], g.of_range[:, :], g.tail[:, 0:1], None, ALU.mult).then_inc(s["flags_ready"], 1)
            dve.wait_ge(s["flags_small"], 1)
            step(dve.tensor_copy(g.one_run[:, :, :], ps_f[:, :, :]))
            step(dve.tensor_scalar(g.one_pen[:, :, :], g.one_run[:, :, :], -1.0, BIG, ALU.add, ALU.mult))
            dve.wait_ge(s["head_t_made"], 1)
            step(dve.tensor_copy(g.of_head_t[:, :], ps_h[:, :]))
            for h in range(H):
                step(dve.tensor_copy(g.rep[0:R * H, h, :].rearrange("p (r f) -> p r f", f=D),
                                     m.ident[0:R * H, 0:R * H].rearrange("p (r h) -> p h r", h=H)[:, h, :]
                                     .unsqueeze(2).broadcast_to([R * H, R, D])))
            for part in range(1, 3):
                step(dve.tensor_copy(g.rep[part * R * H:(part + 1) * R * H, :, :], g.rep[0:R * H, :, :]))

        @block.tensor
        def _(pe):
            pe.wait_ge(s["head_ready"], 1)
            pe.transpose(ps_h[:, :], g.of_head[:, :], m.ident[:, :]).then_inc(s["head_t_made"], 1)
            pe.wait_ge(s["flags_ready"], 1)
            pe.matmul(ps_f[:, :, :], g.of_head[:, :], flags[:, :, :], start=True, stop=True).then_inc(s["flags_small"], 1)


def gat_self_step(nc, m, g, layer):
    a = m.a
    GB = 4
    groups = [list(range(b, min(b + GB, BN))) for b in range(0, BN, GB)]
    with Step(nc, f"gat_self{layer}") as st:
        sb, ps = st.sb, st.ps
        s = st.sems("w_zeroed", "w_loaded", "w_ready", "transposed", "copied", "u_made", "u_biased", "u_leaky", "l_made", "chain")
        wl, wr = sb("wl", [D, 2, 128]), sb("wr", [D, 2, 128])
        bias = sb("bias", [128, 2, 2])
        bsum = sb("bsum", [128, 2])
        wa = sb("wa", [128, 2 * H])
        biased = sb("biased", [128, 4, GB, PN])
        leaky = sb("leaky", [128, 4, GB, PN])
        ps_t = ps("t", [D, 2, GB, 128])
        ps_u = ps("u", [128, 4, 512])
        ps_l = ps("l", [PN, BN, H])
        block = st.block()

        @block.sync
        def _(sp):
            for to, w in ((wl, a.Wl), (wr, a.Wr)):
                sp.dma_start(to[:, :, :], w[layer].rearrange("f (g n) -> f g n", n=128)).then_inc(s["w_loaded"], 16)
            for side, b in enumerate((a.bl, a.br)):
                sp.dma_start(bias[:, side, :], b[layer].rearrange("(g n) -> n g", n=128),
                             allow_slow_non_contiguous=True).then_inc(s["w_loaded"], 16)
            sp.wait_ge(s["w_zeroed"], 1)
            for hh in range(4):
                sp.dma_start(wa[32 * hh:32 * hh + 32, hh:hh + H + 5:H + 4],
                             a.att[layer].rearrange("(g hh) c -> hh c g", hh=4)[hh],
                             allow_slow_non_contiguous=True).then_inc(s["w_loaded"], 16)

        @block.vector
        def _(dve):
            n = [0]
            dve.memset(wa[:, :], 0.0).then_inc(s["w_zeroed"], 1)
            for t, bs in enumerate(groups):
                dve.wait_ge(s["transposed"], t + 1)
                dve.tensor_copy(g.h_t[:, bs[0]:bs[-1] + 1, :], ps_t[:, t % 2, 0:len(bs), 0:PN]).then_inc(s["copied"], 1)
            dve.wait_ge(s["w_loaded"], 16 * 8)
            dve.tensor_tensor(wl[:, :, :], wl[:, :, :], wr[:, :, :], ALU.add)
            dve.tensor_tensor(bsum[:, :], bias[:, 0, :], bias[:, 1, :], ALU.add).then_inc(s["w_ready"], 1)
            for t, bs in enumerate(groups):
                for half in range(2):
                    u = 2 * t + half
                    dve.wait_ge(s["u_biased"], u + 1)
                    if t >= 2:
                        dve.wait_ge(s["l_made"], t - 1)
                    dve.scalar_tensor_tensor(leaky[:, u % 4, 0:len(bs), :], biased[:, u % 4, 0:len(bs), :], 0.2,
                                             biased[:, u % 4, 0:len(bs), :], ALU.mult, ALU.max).then_inc(s["u_leaky"], 1)
            dve.wait_ge(s["l_made"], len(groups))
            link(dve, s["chain"], n, dve.tensor_copy(m.h_self[:, :, D:DS], ps_l[:, :, :]))

        @block.scalar
        def _(act):
            act.wait_ge(s["w_ready"], 1)
            for t, bs in enumerate(groups):
                for half in range(2):
                    u = 2 * t + half
                    act.wait_ge(s["u_made"], u + 1)
                    if t >= 2:
                        act.wait_ge(s["u_leaky"], u - 3)
                    act.activation(biased[:, u % 4, 0:len(bs), :],
                                   ps_u[:, u % 4, 0:len(bs) * PN].rearrange("p (b n) -> p b n", n=PN), ACT.Identity,
                                   bias=bsum[:, half:half + 1]).then_inc(s["u_biased"], 1)

        @block.tensor
        def _(pe):
            for t, bs in enumerate(groups):
                if t >= 2:
                    pe.wait_ge(s["copied"], t - 1)
                for x, b in enumerate(bs):
                    last = pe.transpose(ps_t[:, t % 2, x, 0:PN], m.h[:, b * D:(b + 1) * D], m.ident[0:PN, 0:PN])
                last.then_inc(s["transposed"], 1)
            pe.wait_ge(s["w_ready"], 1)

            def logits(t):
                pe.wait_ge(s["u_leaky"], 2 * t + 2)
                for x, b in enumerate(groups[t]):
                    pe.matmul(ps_l[:, b, :], leaky[:, 2 * t % 4, x, :], wa[:, 0:H], start=True, stop=False)
                    last = pe.matmul(ps_l[:, b, :], leaky[:, 2 * t % 4 + 1, x, :], wa[:, H:2 * H], start=False, stop=True)
                last.then_inc(s["l_made"], 1)

            for t, bs in enumerate(groups):
                for half in range(2):
                    u = 2 * t + half
                    if t >= 2:
                        pe.wait_ge(s["u_biased"], u - 3)
                    pe.matmul(ps_u[:, u % 4, 0:len(bs) * PN], wl[:, half, :], g.h_t[:, bs[0]:bs[-1] + 1, :],
                              start=True, stop=True).then_inc(s["u_made"], 1)
                if t >= 1:
                    logits(t - 1)
            logits(len(groups) - 1)


def gat_scores_step(nc, m, g, layer):
    a = m.a
    G = 2 * (H // 2)
    U = 4
    LAG = 2
    with Step(nc, f"gat_scores{layer}") as st:
        sb, ps = st.sb, st.ps
        s = st.sems(*front_sems(), "w_zeroed", "w_loaded", "bias_ready", "state_zeroed", "u_made", "u_biased", "u_leaky",
                    "l_made", "logits_copied", "self_rows0", "self_rows1", "self_made", "self_scanned", "chunk_stored0", "chunk_stored1", "out_free")
        rows = [sb(f"rows{k}", [128, J, R, 2, D]) for k in range(2)]
        selfs = [sb(f"selfs{k}", [128, J, R, H]) for k in range(2)]
        ls = [sb(f"self_logits{k}", [R * H, W]) for k in range(2)]
        ids = [sb(f"ids{k}", [128, T], I32) for k in range(2)]
        xt = [sb(f"xt{k}", [128, 2, W]) for k in range(2)]
        biased = [sb(f"biased{k}", [128, W]) for k in range(U)]
        leaky = [sb(f"leaky{k}", [128, W]) for k in range(U)]
        lg = [sb(f"logits{k}", [R * H, W]) for k in range(2)]
        wu = sb("wu", [128, H // 2, 128])
        wa = sb("wa", [128, 2, H // 2 * R * H])
        bias = sb("bias", [128, 2, H // 2])
        bsum = sb("bsum", [128, H // 2])
        ps_x = ps("x", [128, 2, W])
        ps_u = ps("u", [128, U, W])
        ps_l = ps("l", [R * H, W])
        ps_f = ps("self", [R * H, W])
        n_w = 4 + 8 + 4
        block = st.block()

        @block.sync
        def _(sp):
            grant(sp, s, "out_free")

            def load(c, k):
                load_starts(sp, m, s, rows, c, k)
                for j in range(J):
                    sp.dma_start(selfs[k][:, j, :, :], m.self_chunks[c, :, j, :, :]).then_inc(s[f"self_rows{k}"], 16)

            for c in range(2):
                load(c, c)
            sp.wait_ge(s["w_zeroed"], 1)
            for rr in range(2):
                for sd, w in enumerate((a.Wl, a.Wr)):
                    sp.dma_start(wu[64 * rr + 32 * sd:64 * rr + 32 * sd + 32, :, 64 * rr:64 * rr + 64],
                                 w[layer].rearrange("f (g n) -> f g n", n=64)).then_inc(s["w_loaded"], 16)
                for side, b in enumerate((a.bl, a.br)):
                    sp.dma_start(bias[64 * rr:64 * rr + 64, side, :], b[layer].rearrange("(g n) -> n g", n=64),
                                 allow_slow_non_contiguous=True).then_inc(s["w_loaded"], 16)
                for hh in range(2):
                    for q in range(2):
                        first = (2 * q + rr) * H + hh
                        stride = R * H + 2
                        sp.dma_start(wa[64 * rr + 32 * hh:64 * rr + 32 * hh + 32, q, first:first + 3 * stride + 1:stride],
                                     a.att[layer].rearrange("(g two) c -> two c g", two=2)[hh],
                                     allow_slow_non_contiguous=True).then_inc(s["w_loaded"], 16)

            def store(c, k, i):
                sp.wait_ge(s["x_scanned"], went(c))
                for r in range(R):
                    sp.dma_start(g.values[32 * r:32 * r + 32, bass.ds(c * W, W)],
                                 xt[k][64 * (r % 2):64 * (r % 2) + 32, r // 2, :]).then_inc(s[f"chunk_stored{k}"], 16)
                sp.wait_ge(s["self_scanned"], went(c))
                sp.dma_start(g.self_logits.rearrange("r h e -> (r h) e")[:, bass.ds(c * W, W)], ls[k][:, :])\
                  .then_inc(s[f"chunk_stored{k}"], 16)
                sp.wait_ge(s["logits_copied"], went(c))
                sp.dma_start(g.logits.rearrange("r h e -> (r h) e")[:, bass.ds(c * W, W)], lg[k][:, :])\
                  .then_inc(s[f"chunk_stored{k}"], 16)
                sp.wait_ge(s[f"chunk_stored{k}"], (i + 1) * (16 * (R + 2)))
                sp.sem_inc(s["out_free"], 1)

            with sp.Fori(0, HALF - 1) as i:
                for k in range(2):
                    load(i * 2 + k + 2, k)
                    store(i * 2 + k, k, i)
            for k in range(2):
                store(C - 2 + k, k, HALF - 1)

        def trips(eng, chunk):
            with eng.Fori(0, HALF - 1) as i:
                for k in range(2):
                    chunk(i * 2 + k, k, i)
            for k in range(2):
                chunk(C - 2 + k, k, HALF - 1)

        def has_next(c):
            return not (isinstance(c, int) and c == C - 1)

        @block.gpsimd
        def _(pool):
            pool.memset(wu[:, :, :], 0.0)
            pool.memset(wa[:, :, :], 0.0).then_inc(s["w_zeroed"], 1)
            with pool.Fori(0, HALF) as i:
                for k in range(2):
                    gather_sources(pool, m, s, rows, ids, i * 2 + k, k, i)

        @block.scalar
        def _(act):
            grant(act, s, "ids_copied", "u_biased")
            for k in range(2):
                copy_ids(act, m, s, ids, k, k)
            act.wait_ge(s["bias_ready"], 1)
            with act.Fori(0, HALF) as i:
                for k in range(2):
                    c = i * 2 + k
                    copy_ids(act, m, s, ids, c + 2, k)
                    for t in range(G):
                        n = c * G + t
                        act.wait_ge(s["u_made"], went(n))
                        act.wait_ge(s["u_leaky"], went(n, U))
                        act.activation(biased[t % U][:, :], ps_u[:, t % U, :], ACT.Identity,
                                       bias=bsum[:, t % 4:t % 4 + 1]).then_inc(s["u_biased"], 1)

        @block.tensor
        def _(pe):
            grant(pe, s, "rows_transposed", "self_made", "u_made", "l_made")
            pe.wait_ge(s["w_loaded"], 16 * n_w)

            def logits(c, t):
                n = c * G + t
                pe.wait_ge(s["u_leaky"], went(n))
                if t == 0:
                    pe.wait_ge(s["logits_copied"], went(c, 1))
                pe.matmul(ps_l[:, :], wa[:, t // 4, (t % 4) * R * H:(t % 4 + 1) * R * H], leaky[t % U][:, :],
                          start=(t == 0), stop=(t == G - 1)).then_inc(s["l_made"], 1)

            def front(c, k, i):
                pe.wait_ge(s[f"self_rows{k}"], (i + 1) * (16 * J))
                pe.wait_ge(s["self_scanned"], went(c, 1))
                for j in range(J):
                    last = pe.transpose(ps_f[:, j::J], selfs[k][:, j, :, :], m.ident[:, :])
                last.then_inc(s["self_made"], 1)
                transpose_rows(pe, m, s, rows, ps_x, c, k, i)

            def chunk(c, k, i):
                pe.wait_ge(s["x_scanned"], went(c))
                for t in range(G):
                    n = c * G + t
                    pe.wait_ge(s["u_biased"], went(n, U))
                    pe.matmul(ps_u[:, t % U, :], wu[:, t % 4, :], xt[k][:, t // 4, :], start=True, stop=True)\
                      .then_inc(s["u_made"], 1)
                    if t >= LAG:
                        logits(c, t - LAG)
                    if t == G - 2 and has_next(c):
                        front(c + 1, 1 - k, i + k)
                for t in range(G - LAG, G):
                    logits(c, t)

            front(0, 0, 0)
            trips(pe, chunk)

        @block.vector
        def _(dve):
            grant(dve, s, "x_scanned", "self_scanned", "u_leaky", "logits_copied")
            dve.memset(ls[1][:, :], 0.0).then_inc(s["state_zeroed"], 1)
            dve.memset(xt[1][:, :, :], 0.0).then_inc(s["state_zeroed"], 1)
            dve.wait_ge(s["w_loaded"], 16 * n_w)
            dve.tensor_tensor(bsum[:, :], bias[:, 0, :], bias[:, 1, :], ALU.add).then_inc(s["bias_ready"], 1)
            dve.wait_ge(s["state_zeroed"], 2)
            def scans(c, k):
                dve.wait_ge(s["out_free"], went(c, 2))
                scan_rows(dve, m, s, ps_x, xt, c, k)
                dve.wait_ge(s["self_made"], went(c))
                dve.wait_ge(s["self_scanned"], went(c, 1))
                dve.tensor_tensor_scan(ls[k][:, :], g.keep_heads[:, bass.ds(c * W, W)], ps_f[:, :],
                                       ls[1 - k][:, W - 1:W], ALU.mult, ALU.add).then_inc(s["self_scanned"], 1)

            def chunk(c, k, i):
                for t in range(G):
                    n = c * G + t
                    dve.wait_ge(s["u_biased"], went(n))
                    dve.wait_ge(s["l_made"], went(n, U))
                    dve.scalar_tensor_tensor(leaky[t % U][:, :], biased[t % U][:, :], 0.2, biased[t % U][:, :],
                                             ALU.mult, ALU.max).then_inc(s["u_leaky"], 1)
                if has_next(c):
                    scans(c + 1, 1 - k)
                dve.wait_ge(s["l_made"], went(c * G + G - 1))
                dve.tensor_copy(lg[k][:, :], ps_l[:, :]).then_inc(s["logits_copied"], 1)

            scans(0, 0)
            trips(dve, chunk)


def gat_softmax_step(nc, m, g, layer):
    with Step(nc, f"gat_softmax{layer}") as st:
        sb, ps = st.sb, st.ps
        halves = ((0, SW // 2), (SW // 2, SW))
        s = st.sems("own_ready", "own_loaded", "own_shifted", "own_stored", "max_ready", "inverted", "alpha_ready", "rest_ready",
                    "part0_ready", "part1_ready", "part2_ready", "loaded", "chain", "ends_ready", "ends_small", "carry_ready", "carry_made", "shifted", "exp_made",
                    "stored")
        lg = sb("logits", [128, SW])
        one = sb("one", [128, SW])
        two = sb("two", [128, SW])
        own = sb("own", [128, SW])
        parts = sb("parts", [128, 3, SW], BF16)
        ends = sb("ends", [128, 2, RS])
        small = sb("small", [H, 2, RS + 1])
        masked = sb("masked", [128, 2, RS])
        carry = sb("carry", [128, 2])
        ps_e = ps("ends", [H, 2, RS])
        ps_c = ps("carry", [128, 2, RS])
        block = st.block()

        @block.sync
        def _(sp):
            for q in range(RS):
                r, sub = q // 4, q % 4
                sp.dma_start(lg[H * q:H * q + H, :], g.logits[r, :, sub * SW:(sub + 1) * SW]).then_inc(s["loaded"], 16)
            by_part = g.alpha.rearrange("(part r h) e -> r h part e", part=3, r=R)
            for first_part, last_part in ((0, 1), (1, 3)):
                sp.wait_ge(s[f"part{last_part - 1}_ready"], 2)
                for q in range(RS):
                    r, sub = q // 4, q % 4
                    sp.dma_start(by_part[r, :, first_part:last_part, sub * SW:(sub + 1) * SW],
                                 parts[H * q:H * q + H, first_part:last_part, :]).then_inc(s["stored"], 16)
            sp.wait_ge(s["stored"], 16 * 2 * RS)

        @block.gpsimd
        def _(pool):
            for q in range(RS):
                r, sub = q // 4, q % 4
                pool.dma_start(own[H * q:H * q + H, :], g.self_logits[r, :, sub * SW:(sub + 1) * SW]).then_inc(s["own_loaded"], 16)
            pool.wait_ge(s["max_ready"], 1)
            pool.wait_ge(s["own_loaded"], 16 * RS)
            pool.tensor_tensor(own[:, :], own[:, :], two[:, :], ALU.subtract).then_inc(s["own_shifted"], 1)
            pool.wait_ge(s["exp_made"], 2)
            for half, (first_col, last_col) in enumerate(halves):
                pool.wait_ge(s["inverted"], half + 1)
                pool.tensor_tensor(own[:, first_col:last_col], own[:, first_col:last_col], two[:, first_col:last_col],
                                   ALU.mult).then_inc(s["own_ready"], 1)
            pool.wait_ge(s["own_ready"], 2)
            for q in range(RS):
                r, sub = q // 4, q % 4
                pool.dma_start(g.self_alpha[H * r:H * r + H, sub * SW:(sub + 1) * SW], own[H * q:H * q + H, :])\
                    .then_inc(s["own_stored"], 16)
            pool.wait_ge(s["own_stored"], 16 * RS)

        @block.tensor
        def _(pe):
            for turn in range(2):
                pe.wait_ge(s["ends_ready"], turn + 1)
                pe.matmul(ps_e[:, :, :], g.of_head[:, :], ends[:, :, :], start=True, stop=True).then_inc(s["ends_small"], 1)
                pe.wait_ge(s["carry_ready"], turn + 1)
                pe.matmul(ps_c[:, 0, :], g.of_head_t[:, :], small[:, 0, 0:RS], start=True, stop=True)
                pe.matmul(ps_c[:, 1, :], g.of_head_t[:, :], small[:, 1, 1:RS + 1], start=True, stop=True)\
                  .then_inc(s["carry_made"], 1)

        @block.scalar
        def _(act):
            act.wait_ge(s["shifted"], 1)
            act.activation(one[:, :], one[:, :], ACT.Exp).then_inc(s["exp_made"], 1)
            act.wait_ge(s["own_shifted"], 1)
            act.activation(own[:, :], own[:, :], ACT.Exp).then_inc(s["exp_made"], 1)
            for half, (first_col, last_col) in enumerate(halves):
                act.wait_ge(s["alpha_ready"], half + 1)
                act.activation(parts[:, 0, first_col:last_col], one[:, first_col:last_col], ACT.Copy).then_inc(s["part0_ready"], 1)
            for half, (first_col, last_col) in enumerate(halves):
                act.wait_ge(s["rest_ready"], half + 1)
                act.activation(parts[:, 1, first_col:last_col], one[:, first_col:last_col], ACT.Copy).then_inc(s["part1_ready"], 1)

        @block.vector
        def _(dve):
            n = [0]

            def step(ins):
                link(dve, s["chain"], n, ins)

            def carries(turn, local, flags, op, op1, empty):
                step(dve.tensor_scalar(ends[:, 0, :], g.of_range[:, :], local[:, SW - 1:SW], None, ALU.mult))
                step(dve.tensor_scalar(ends[:, 1, :], g.of_range[:, :], local[:, 0:1], None, ALU.mult))
                step(dve.memset(small[:, :, :], empty))
                dve.sem_inc(s["ends_ready"], 1)
                dve.wait_ge(s["ends_small"], turn)
                step(dve.tensor_tensor_scan(small[:, 0, 1:RS + 1], flags[:, 0, :], ps_e[:, 0, :], empty, op, op1))
                step(dve.tensor_tensor_scan(small[:, 1, 0:RS][:, ::-1], flags[:, 1, ::-1], ps_e[:, 1, ::-1], empty, op, op1))
                dve.sem_inc(s["carry_ready"], 1)
                dve.wait_ge(s["carry_made"], turn)
                step(dve.tensor_tensor(masked[:, :, :], ps_c[:, :, :],
                                       g.of_range[:, :].unsqueeze(1).broadcast_to([128, 2, RS]), ALU.mult))
                step(dve.tensor_reduce(carry[:, :], masked[:, :, :], AX.X, ALU.add))

            dve.wait_ge(s["loaded"], 16 * RS)
            step(dve.tensor_tensor_scan(one[:, :], g.keep_pen[:, :], lg[:, :], -BIG, ALU.add, ALU.max))
            step(dve.tensor_tensor_scan(two[:, ::-1], g.back_pen[:, ::-1], one[:, ::-1], -BIG, ALU.add, ALU.max))
            carries(1, two, g.one_pen, ALU.add, ALU.max, -BIG)
            step(dve.scalar_tensor_tensor(two[:, :], g.head_pen[:, :], carry[:, 0:1], two[:, :], ALU.add, ALU.max))
            step(dve.scalar_tensor_tensor(two[:, :], g.tail_pen[:, :], carry[:, 1:2], two[:, :], ALU.add, ALU.max))
            dve.wait_ge(s["own_loaded"], 16 * RS)
            dve.tensor_tensor(two[:, :], two[:, :], own[:, :], ALU.max).then_inc(s["max_ready"], 1)
            dve.wait_ge(s["max_ready"], 1)
            dve.tensor_tensor(one[:, :], lg[:, :], two[:, :], ALU.subtract).then_inc(s["shifted"], 1)
            dve.wait_ge(s["exp_made"], 1)
            step(dve.tensor_tensor_scan(lg[:, :], g.keep[:, :], one[:, :], 0.0, ALU.mult, ALU.add))
            dve.wait_ge(s["own_shifted"], 1)
            step(dve.tensor_tensor_scan(two[:, ::-1], g.keep_back[:, ::-1], lg[:, ::-1], 0.0, ALU.mult, ALU.max))
            carries(2, two, g.one_run, ALU.mult, ALU.add, 0.0)
            step(dve.scalar_tensor_tensor(two[:, :], g.head[:, :], carry[:, 0:1], two[:, :], ALU.mult, ALU.add))
            step(dve.scalar_tensor_tensor(two[:, :], g.tail[:, :], carry[:, 1:2], two[:, :], ALU.mult, ALU.add))
            dve.wait_ge(s["exp_made"], 2)
            step(dve.scalar_tensor_tensor(two[:, :], two[:, :], 1e-16, own[:, :], ALU.add, ALU.add))
            for half, (first_col, last_col) in enumerate(halves):
                dve.reciprocal(two[:, first_col:last_col], two[:, first_col:last_col]).then_inc(s["inverted"], 1)
                dve.wait_ge(s["inverted"], half + 1)
                dve.tensor_tensor(one[:, first_col:last_col], one[:, first_col:last_col], two[:, first_col:last_col],
                                  ALU.mult).then_inc(s["alpha_ready"], 1)
            for half, (first_col, last_col) in enumerate(halves):
                dve.wait_ge(s["part0_ready"], half + 1)
                dve.tensor_tensor(one[:, first_col:last_col], one[:, first_col:last_col], parts[:, 0, first_col:last_col],
                                  ALU.subtract).then_inc(s["rest_ready"], 1)
            for half, (first_col, last_col) in enumerate(halves):
                dve.wait_ge(s["part1_ready"], half + 1)
                dve.tensor_tensor(parts[:, 2, first_col:last_col], one[:, first_col:last_col], parts[:, 1, first_col:last_col],
                                  ALU.subtract).then_inc(s["part2_ready"], 1)


def gat_messages_step(nc, m, g, layer):
    a = m.a
    DEEP, LAG = 4, 3
    with Step(nc, f"gat_messages{layer}") as st:
        sb, ps = st.sb, st.ps
        s = st.sems(*tail_sems(), "w_zeroed", "w_loaded", "w_scaled", "state_zeroed", "alpha_loaded0", "alpha_loaded1",
                    "values_loaded0", "values_loaded1", "own_loaded0", "own_loaded1",
                    "own_made", "own_copied", "a_made", "weighted", "m_made")
        al = [sb(f"alpha{k}", [3 * R * H, W], BF16) for k in range(2)]
        xv = [sb(f"values{k}", [128, W]) for k in range(2)]
        wx = [sb(f"weighted{k}", [128, W]) for k in range(DEEP)]
        sc = [sb(f"sc{k}", [128, W]) for k in range(2)]
        ob = [sb(f"ob{k}", [128, R, J, DS]) for k in range(2)]
        own = [sb(f"own{k}", [R * H, W]) for k in range(2)]
        wl = sb("wl", [128, H, 128])
        ps_a = ps("a", [128, DEEP, W])
        ps_m = ps("m", [128, 2, W])
        ps_s = ps("s", [128, J, 128])
        ps_o = ps("own", [128, J, R * H])
        sums_chunks = g.sums.rearrange("(r c p j) f -> c p r (j f)", r=R, c=C, p=128, j=J)
        block = st.block()

        @block.sync
        def _(sp):
            grant(sp, s, "out_free")

            def load(c, k):
                sp.dma_start(al[k][:, :], g.alpha[:, bass.ds(c * W, W)]).then_inc(s[f"alpha_loaded{k}"], 16)
                sp.dma_start(own[k][:, :], g.self_alpha[:, bass.ds(c * W, W)]).then_inc(s[f"own_loaded{k}"], 16)
                sp.dma_start(xv[k][:, :], g.values[:, bass.ds(c * W, W)]).then_inc(s[f"values_loaded{k}"], 16)

            load(0, 0)
            sp.wait_ge(s["w_zeroed"], 1)
            for r in range(R):
                sp.dma_start(wl[32 * r:32 * r + 32, :, 32 * r:32 * r + 32],
                             a.Wl[layer].rearrange("f (h c) -> f h c", h=H)).then_inc(s["w_loaded"], 16)
            load(1, 1)

            def store(c, k, i):
                sp.wait_ge(s["sums_copied"], went(c))
                sp.dma_start(sums_chunks[c], ob[k][:, :, :, :].rearrange("p r j f -> p r (j f)"))\
                  .then_inc(s[f"sums_stored{k}"], 16)
                sp.wait_ge(s[f"sums_stored{k}"], (i + 1) * 16)
                sp.sem_inc(s["out_free"], 1)

            with sp.Fori(0, HALF - 1) as i:
                for k in range(2):
                    c = i * 2 + k
                    sp.wait_ge(s["weighted"], went(c * H + H - 1))
                    load(c + 2, k)
                    store(c, k, i)
            for k in range(2):
                store(C - 2 + k, k, HALF - 1)

        @block.gpsimd
        def _(pool):
            pool.memset(wl[:, :, :], 0.0).then_inc(s["w_zeroed"], 1)

        def trips(eng, chunk):
            for k in range(2):
                chunk(k, k, 0)
            with eng.Fori(1, HALF) as i:
                for k in range(2):
                    chunk(i * 2 + k, k, i)

        def has_last(c):
            return not (isinstance(c, int) and c == 0)

        @block.tensor
        def _(pe):
            grant(pe, s, "own_made", "a_made", "m_made", "sums_transposed")

            def spread(c, k, h):
                pe.wait_ge(s["weighted"], went(c * H + h, DEEP))
                pe.matmul(ps_a[:, h % DEEP, :], g.rep[:, h, :], al[k][:, :], start=True, stop=True)\
                  .then_inc(s["a_made"], 1)

            def product(c, k, h):
                pe.wait_ge(s["weighted"], went(c * H + h))
                if h == 0:
                    pe.wait_ge(s["msg_scanned"], went(c, 2))
                pe.matmul(ps_m[:, k, :], wl[:, h, :], wx[h % DEEP][:, :], start=(h == 0), stop=(h == H - 1))\
                  .then_inc(s["m_made"], 1)

            def chunk(c, k, i):
                pe.wait_ge(s[f"alpha_loaded{k}"], (i + 1) * 16)
                for h in range(H):
                    if h == 1:
                        pe.wait_ge(s[f"own_loaded{k}"], (i + 1) * 16)
                        pe.wait_ge(s["own_copied"], went(c, 1))
                    spread(c, k, h)
                    if h >= LAG:
                        product(c, k, h - LAG)
                    elif has_last(c):
                        product(c - 1, 1 - k, H - LAG + h)
                    if h == 1:
                        for j in range(J):
                            last = pe.transpose(ps_o[:, j, :], own[k][:, j::J], m.ident[0:R * H, 0:R * H])
                        last.then_inc(s["own_made"], 1)
                    if h == H - 2 and has_last(c):
                        transpose_sums(pe, m, s, sc, ps_s, c - 1, 1 - k)

            pe.wait_ge(s["w_scaled"], 1)
            trips(pe, chunk)
            for h in range(H - LAG, H):
                product(C - 1, 1, h)
            transpose_sums(pe, m, s, sc, ps_s, C - 1, 1)

        @block.vector
        def _(dve):
            grant(dve, s, "weighted", "msg_scanned")
            dve.memset(sc[1][:, :], 0.0).then_inc(s["state_zeroed"], 1)
            dve.wait_ge(s["state_zeroed"], 1)
            dve.wait_ge(s["w_loaded"], 16 * R)
            dve.tensor_scalar(wl[:, :, :], wl[:, :, :], 1.0 / H, None, ALU.mult).then_inc(s["w_scaled"], 1)

            def scan(c, k):
                dve.wait_ge(s["m_made"], went(c * H + H - 1))
                dve.wait_ge(s["sums_transposed"], went(c, 2))
                dve.wait_ge(s["msg_scanned"], went(c, 1))
                dve.tensor_tensor_scan(sc[k][:, :], m.keep[:, bass.ds(c * W, W)], ps_m[:, k, :],
                                       sc[1 - k][:, W - 1:W], ALU.mult, ALU.add).then_inc(s["msg_scanned"], 1)

            def chunk(c, k, i):
                dve.wait_ge(s[f"values_loaded{k}"], (i + 1) * 16)
                for h in range(H):
                    dve.wait_ge(s["a_made"], went(c * H + h))
                    dve.wait_ge(s["m_made"], went(c * H + h, DEEP))
                    dve.tensor_tensor(wx[h % DEEP][:, :], ps_a[:, h % DEEP, :], xv[k][:, :], ALU.mult)\
                       .then_inc(s["weighted"], 1)
                    if h == LAG and has_last(c):
                        scan(c - 1, 1 - k)

            trips(dve, chunk)
            scan(C - 1, 1)

        @block.scalar
        def _(act):
            grant(act, s, "sums_copied", "own_copied")

            def take_own(c, k):
                act.wait_ge(s["own_made"], went(c))
                act.wait_ge(s["out_free"], went(c, 2))
                act.activation(ob[k][:, :, :, D:DS].rearrange("p r j h -> p j r h"),
                               ps_o[:, :, :].rearrange("p j (r h) -> p j r h", r=R), ACT.Copy).then_inc(s["own_copied"], 1)

            def take_sums(c, k):
                act.wait_ge(s["sums_transposed"], went(c))
                act.activation(ob[k][:, :, :, 0:D].rearrange("p r j f -> p j r f"),
                               ps_s[:, :, :].rearrange("p j (r f) -> p j r f", r=R), ACT.Copy)\
                   .then_inc(s["sums_copied"], 1)

            def chunk(c, k, i):
                take_own(c, k)
                if has_last(c):
                    take_sums(c - 1, 1 - k)

            trips(act, chunk)
            take_sums(C - 1, 1)


def gat_norm_step(nc, m, g, layer):
    a = m.a
    with Step(nc, f"gat_norm{layer}") as st:
        sb = st.sb
        s = st.sems("w_loaded", "v_made", "v_used", *bn_sems())
        b = bn_memory(st)
        y = sb("y", [PN, BN * D])
        wl = sb("wl", [D, H * D])
        alpha = sb("alpha", [PN, BN, H])
        none = sb("none", [PN, BN])
        weighted = sb("weighted", [PN, 2, 2, H * D])
        ps_v = st.ps("v", [PN, 2, 2, H * D])
        bl = sb("bl", [PN, H * D])
        blm = sb("bl_mean", [PN, D])
        cb = sb("conv_bias", [PN, D])
        gamma = sb("gamma", [PN, D])
        beta = sb("beta", [PN, D])
        block = st.block()

        @block.sync
        def _(sp):
            for to, v in ((bl, a.bl), (cb, a.cb), (gamma, a.bng), (beta, a.bnb)):
                sp.dma_start(to[:, :], v[layer].partition_broadcast(PN)).then_inc(s["w_loaded"], 16)
            sp.dma_start(wl[:, :], a.Wl[layer]).then_inc(s["w_loaded"], 16)

        @block.vector
        def _(dve):
            n = [0]

            def step(ins):
                link(dve, s["chain"], n, ins)

            y3 = y[:, :].rearrange("p (b f) -> p b f", f=D)
            dve.wait_ge(s["w_loaded"], 80)
            step(dve.tensor_reduce(blm[:, :], bl[:, :].rearrange("p (h f) -> p f h", f=D), AX.X, ALU.add))
            step(dve.tensor_scalar(blm[:, :], blm[:, :], 1.0 / H, None, ALU.mult))
            step(dve.tensor_tensor(blm[:, :], blm[:, :], cb[:, :], ALU.add))
            step(dve.tensor_scalar(none[:, :], m.some[:, :], -1.0, 1.0, ALU.mult, ALU.add))
            step(dve.tensor_tensor(alpha[:, :, :], g.rows[:, :, D:DS], m.some[:, :].unsqueeze(2).broadcast_to([PN, BN, H]), ALU.mult))
            step(dve.tensor_tensor(alpha[:, :, :], alpha[:, :, :], none[:, :].unsqueeze(2).broadcast_to([PN, BN, H]), ALU.add))
            step(dve.tensor_scalar(alpha[:, :, :], alpha[:, :, :], 1.0 / H, None, ALU.mult))
            for t in range(0, BN, 2):
                u, nb = t // 2, min(2, BN - t)
                dve.wait_ge(s["v_made"], u + 1)
                dve.tensor_tensor(weighted[:, u % 2, 0:nb, :].rearrange("p b (h f) -> p (b h) f", f=D),
                                  ps_v[:, u % 2, 0:nb, :].rearrange("p b (h f) -> p (b h) f", f=D),
                                  alpha[:, t:t + nb, :].rearrange("p b h -> p (b h)").unsqueeze(2)
                                  .broadcast_to([PN, nb * H, D]), ALU.mult).then_inc(s["v_used"], 1)
                dve.wait_ge(s["v_used"], u + 1)
                last = dve.tensor_reduce(y3[:, t:t + nb, :], weighted[:, u % 2, 0:nb, :].rearrange("p b (h f) -> p b f h", f=D),
                                         AX.X, ALU.add)
            step(last)
            step(dve.tensor_tensor(y3, y3, blm[:, :].unsqueeze(1).broadcast_to([PN, BN, D]), ALU.add))
            step(dve.tensor_tensor(y[:, :], y[:, :], m.agg[:, :], ALU.add))
            if layer < 2:
                step(dve.scalar_tensor_tensor(y[:, :], y[:, :], 0.01, y[:, :], ALU.mult, ALU.max))
            step(dve.tensor_tensor(y[:, :], y[:, :], m.h[:, :], ALU.add))
            bn_dve(dve, s, n, b, y, m.h, gamma, beta)
            if layer == 2:
                step(dve.tensor_tensor(m.x[:, :], m.x[:, :], m.h[:, :], ALU.add))

        @block.tensor
        def _(pe):
            pe.wait_ge(s["w_loaded"], 80)
            for b0 in range(BN):
                u = b0 // 2
                if b0 % 2 == 0 and u >= 2:
                    pe.wait_ge(s["v_used"], u - 1)
                last = pe.matmul(ps_v[:, u % 2, b0 % 2, :], g.h_t[:, b0, :], wl[:, :], start=True, stop=True)
                if b0 % 2 == 1 or b0 == BN - 1:
                    last.then_inc(s["v_made"], 1)
            bn_pe(pe, m, s, b, y)

        @block.scalar
        def _(act):
            bn_act(act, s, b)


def gat_layers(nc, m):
    with Step(nc, "gat") as st:
        g = gat_memory(nc, st, m)
        gat_prepare_step(nc, m, g)
        norm_step(nc, m, "gat_layernorm")
        for layer in range(3):
            gat_self_step(nc, m, g, layer)
            publish_step(nc, m, f"gat_publish{layer}")
            gat_scores_step(nc, m, g, layer)
            gat_softmax_step(nc, m, g, layer)
            gat_messages_step(nc, m, g, layer)
            collect_step(nc, m, f"gat_collect{layer}", g.sums, g.rows)
            gat_norm_step(nc, m, g, layer)


K2, UA, OUT2 = 16, 80, 48
UP = 112
GAIN, PW_S, PW_V = 1.593, 0.17677669529663687, 0.25
W_SCALE = 2.0 ** 0.5 / 10.0 ** 0.5 / 4.0
INV_SQRT3 = 0.5773502691896258
SQRT_3_2 = 1.5 ** 0.5


def equi_memory(st):
    e = Mem()
    e.hidden = st.sb("hidden", [128, C * T, K2])
    e.unit = st.sb("unit", [128, C * T, 3])
    e.norm_s = st.sb("norm_s", [128, C * T])
    e.norm_v = st.sb("norm_v", [128, C * T])
    e.w = st.sb("w", [UP, K2 * OUT2])
    return e


def equi_prepare_step(nc, m, e):
    a = m.a
    with Step(nc, "equi_prepare") as st:
        sb, ps = st.sb, st.ps
        s = st.sems("vec_loaded", "w1_loaded", "w_zeroed", "w_loaded", "we_loaded", "chain", "sum_ready", "root_ready",
                    "w1_zeroed", "emb_loaded0", "emb_loaded1", "h_made", "h_copied")
        vec = sb("vec", [128, C * T, 3])
        sq = sb("sq", [128, C * T, 3])
        rt = sb("root", [128, C * T])
        w1 = sb("w1", [R * 10, R * K2])
        we = sb("we", [UA, K2 * OUT2])
        emb = [sb(f"emb{k}", [R * 10, W]) for k in range(2)]
        ps_h = ps("h", [128, 2, 512])
        block = st.block()

        @block.sync
        def _(sp):
            sp.dma_start(vec[:, :, :].rearrange("p t i -> p (t i)"), a.vec_t).then_inc(s["vec_loaded"], 16)
            for k in range(2):
                sp.dma_start(emb[k][:, :], a.emb_t[:, k * W:(k + 1) * W]).then_inc(s[f"emb_loaded{k}"], 16)
            sp.wait_ge(s["w1_zeroed"], 1)
            for r in range(R):
                sp.dma_start(w1[10 * r:10 * r + 10, K2 * r:K2 * r + K2], a.W1e).then_inc(s["w1_loaded"], 16)
            sp.wait_ge(s["w_zeroed"], 1)

            def put(to, sem, first_row, path, first_out):
                sp.dma_start(to[first_row:first_row + 16, :].rearrange("u (k o) -> u k o", o=OUT2)[:, :, first_out:first_out + 8],
                             a.W2e[:, path, :, :]).then_inc(s[sem], 16)

            put(e.w, "w_loaded", 0, 0, 0)
            put(e.w, "w_loaded", 0, 2, 8)
            put(e.w, "w_loaded", 0, 4, 16)
            put(e.w, "w_loaded", 16, 1, 0)
            put(e.w, "w_loaded", 16, 3, 8)
            put(we, "we_loaded", 16, 6, 16)
            for i in range(3):
                put(e.w, "w_loaded", 32 + 16 * i, 5, 24 + 8 * i)
                put(we, "we_loaded", 32 + 16 * i, 6, 24 + 8 * i)
            with sp.Fori(0, HALF - 1) as i:
                for k in range(2):
                    c = i * 2 + k + 2
                    sp.wait_ge(s["h_made"], went(c, 2))
                    sp.dma_start(emb[k][:, :], a.emb_t[:, bass.ds(c * W, W)]).then_inc(s[f"emb_loaded{k}"], 16)

        @block.gpsimd
        def _(pool):
            pool.memset(w1[:, :], 0.0).then_inc(s["w1_zeroed"], 1)
            pool.memset(we[:, :], 0.0)
            pool.memset(e.w[:, :], 0.0).then_inc(s["w_zeroed"], 1)

        @block.tensor
        def _(pe):
            grant(pe, s, "h_made")
            pe.wait_ge(s["w1_loaded"], 16 * R)
            with pe.Fori(0, HALF) as i:
                for k in range(2):
                    c = i * 2 + k
                    pe.wait_ge(s[f"emb_loaded{k}"], (i + 1) * 16)
                    pe.wait_ge(s["h_copied"], went(c, 2))
                    for j in range(J):
                        last = pe.matmul(ps_h[:, k, j * R * K2:(j + 1) * R * K2], emb[k][:, j::J], w1[:, :], start=True, stop=True)
                    last.then_inc(s["h_made"], 1)

        @block.scalar
        def _(act):
            grant(act, s, "h_copied")
            act.wait_ge(s["sum_ready"], 1)
            act.activation(rt[:, :], rt[:, :], ACT.Sqrt).then_inc(s["root_ready"], 1)
            with act.Fori(0, HALF) as i:
                for k in range(2):
                    c = i * 2 + k
                    act.wait_ge(s["h_made"], went(c))
                    act.activation(e.hidden[:, bass.ds(c * T, T), :].rearrange("p t k -> p (t k)"), ps_h[:, k, 0:T * K2], ACT.Relu)\
                       .then_inc(s["h_copied"], 1)

        @block.vector
        def _(dve):
            n = [0]

            def step(ins):
                link(dve, s["chain"], n, ins)

            dve.wait_ge(s["vec_loaded"], 16)
            step(dve.tensor_tensor(sq[:, :, :], vec[:, :, :], vec[:, :, :], ALU.mult))
            dve.tensor_reduce(rt[:, :], sq[:, :, :], AX.X, ALU.add).then_inc(s["sum_ready"], 1)
            dve.wait_ge(s["root_ready"], 1)
            step(dve.reciprocal(rt[:, :], rt[:, :]))
            step(dve.tensor_tensor(e.unit[:, :, :], vec[:, :, :], rt[:, :].unsqueeze(2).broadcast_to([128, C * T, 3]), ALU.mult))
            step(dve.tensor_scalar(e.norm_s[:, :], m.ew[:, :], GAIN, None, ALU.mult))
            step(dve.tensor_scalar(e.norm_v[:, :], m.ew[:, :], GAIN * GAIN_V, None, ALU.mult))
            dve.wait_ge(s["w_loaded"], 16 * 8)
            dve.wait_ge(s["we_loaded"], 16 * 4)
            step(dve.tensor_scalar(e.w[32:64, :], e.w[32:64, :], INV_SQRT3, None, ALU.mult))
            step(dve.tensor_scalar(e.w[64:UA, :], e.w[64:UA, :], INV_SQRT3, None, ALU.mult))
            step(dve.scalar_tensor_tensor(e.w[0:32, :], we[0:32, :], SQRT_3_2, e.w[0:32, :], ALU.mult, ALU.add))
            step(dve.scalar_tensor_tensor(e.w[32:64, :], we[32:64, :], -SQRT_3_2 / 3.0, e.w[32:64, :], ALU.mult, ALU.add))
            step(dve.scalar_tensor_tensor(e.w[64:UA, :], we[64:UA, :], -SQRT_3_2 / 3.0, e.w[64:UA, :], ALU.mult, ALU.add))


GAIN_V = PW_V * W_SCALE


def equi_edges_step(nc, m, e):
    HK = K2 * OUT2 // 2
    LAG = 2
    DEEP = 4
    with Step(nc, "equi_edges") as st:
        sb, ps = st.sb, st.ps
        s = st.sems(*front_sems(), *tail_sems(), "state_zeroed", "x_back", "a_copied", "x_left", "projected", "a_ready",
                    "a_transposed", "at_copied", "pad_zeroed", "g_made", "g_weighed", "g_halved", "g_added", "acted", "spread", "ftr_ready", "chain")
        rows = [sb(f"rows{k}", [128, J, R, 2, D]) for k in range(2)]
        ids = [sb(f"ids{k}", [128, T], I32) for k in range(2)]
        xt = [sb(f"xt{k}", [128, 2, W]) for k in range(2)]
        inp = [sb(f"inputs{k}", [128, T, UP]) for k in range(2)]
        proj = sb("proj", [128, T, 3, 16])
        at = [sb(f"inputs_t{k}", [UP, R, 128]) for k in range(2)]
        prod = [sb(f"prod{k}", [128, K2 * OUT2]) for k in range(DEEP)]
        halved = [sb(f"halved{k}", [128, HK]) for k in range(DEEP - 1)]
        res = [sb(f"res{k}", [128, T, OUT2]) for k in range(2)]
        gated = sb("gated", [128, T, 16])
        vec = sb("vec", [128, T, 3, 8])
        ftr = [sb(f"ftr{k}", [128, T, D]) for k in range(2)]
        sc = [sb(f"sc{k}", [128, W]) for k in range(2)]
        ob = [sb(f"ob{k}", [128, R * J * D]) for k in range(2)]
        ps_x = ps("x", [128, W])
        ps_e = ps("e", [128, J, 2, 2, D])
        ps_t = ps("t", [UP, R, 128])
        ps_g = ps("g", [128, 2, 2, 512])
        ps_s = ps("s", [128, J, 128])
        ps_m = ps_s[:, :, :].rearrange("p j n -> p (j n)")
        block = st.block()

        @block.sync
        def _(sp):
            grant(sp, s, "out_free")
            for c in range(4):
                load_starts(sp, m, s, rows, c, c % 2)
            with sp.Fori(0, HALF - 2) as i:
                for k in range(2):
                    load_starts(sp, m, s, rows, i * 2 + k + 4, k)
                    store_sums(sp, m, s, ob, i * 2 + k, k, i)
            for c in range(C - 4, C):
                store_sums(sp, m, s, ob, c, c % 2, c // 2)

        def trips(eng, chunk):
            for k in range(2):
                chunk(k, k, 0)
            with eng.Fori(1, HALF - 1) as i:
                for k in range(2):
                    chunk(i * 2 + k, k, i)
            for k in range(2):
                chunk(C - 2 + k, k, HALF - 1)

        def has_last(c):
            return not (isinstance(c, int) and c == 0)

        def has_next(c):
            return not (isinstance(c, int) and c == C - 1)

        @block.gpsimd
        def _(pool):
            grant(pool, s, "g_halved")
            for k in range(2):
                pool.memset(inp[k][:, :, UA:], 0.0).then_inc(s["pad_zeroed"], 1)

            def gather(c, k, t):
                if t == 0:
                    pool.wait_ge(s["rows_transposed"], went(c, 2))
                    pool.wait_ge(s["ids_copied"], went(c))
                    pool.sem_inc(s["pool_turn"], 1)
                pool.indirect_dma_start(rows[k][:, t // R, t % R, 0, :], None, m.table,
                                        bass.IndirectOffsetOnAxis(ap=ids[k][:, t:t + 1], axis=0))\
                    .then_inc(s[f"src_rows{k}"], 16)

            def halve(c, t):
                pool.wait_ge(s["g_weighed"], went(c * T + t))
                pool.wait_ge(s["g_added"], went(c * T + t, DEEP))
                pool.tensor_tensor(halved[t % DEEP - 1][:, :], prod[t % DEEP][:, 0:HK], prod[t % DEEP][:, HK:], ALU.add)\
                    .then_inc(s["g_halved"], 1)

            def chunk(c, k, i):
                ahead = iter([] if isinstance(c, int) and c >= C - 2 else range(T))
                for t in range(T):
                    for tile in itertools.islice(ahead, 2 if t % 2 == 0 else 1):
                        gather(c + 2, k, tile)
                    if t % DEEP != 0:
                        halve(c, t)

            for c in range(2):
                for t in range(T):
                    gather(c, c, t)
            trips(pool, chunk)

        @block.scalar
        def _(act):
            grant(act, s, "ids_copied", "a_copied", "at_copied", "acted", "sums_copied")

            def inputs(c, k, q):
                act.wait_ge(s["x_back"], went(c * 2 + q))
                if has_last(c):
                    act.wait_ge(s["a_transposed"], went(c * J, J + 1))
                tiles = inp[k][:, :, :].rearrange("p (j r) a -> p j r a", r=R)[:, :, 2 * q:2 * q + 2, :]
                for sd in range(2):
                    act.activation(tiles[..., 8 * sd:8 * sd + 8], ps_e[:, :, :, sd, 0:8], ACT.Copy)
                    for x in range(3):
                        first = 32 + 16 * x + 8 * sd
                        last = act.activation(tiles[..., first:first + 8], ps_e[:, :, :, sd, 8 + x:D:3], ACT.Copy)
                last.then_inc(s["a_copied"], 1)

            def turned(c, j):
                n = c * J + j
                act.wait_ge(s["a_transposed"], went(n))
                act.wait_ge(s["g_made"], went(n * R, 4))
                act.activation(at[j % 2][:, :, :], ps_t[:, :, :], ACT.Copy).then_inc(s["at_copied"], 1)

            def tanh(c, k):
                act.wait_ge(s["g_added"], went(c * T + T - 1))
                act.wait_ge(s["spread"], went(c, 1))
                act.activation(gated[:, :, :], res[k][:, :, 0:16], ACT.Tanh, scale=PW_S * W_SCALE)\
                   .then_inc(s["acted"], 1)

            def chunk(c, k, i):
                if has_last(c):
                    tanh(c - 1, 1 - k)
                turned(c, 1)
                if has_next(c):
                    inputs(c + 1, 1 - k, 0)
                turned(c, 2)
                if has_next(c):
                    inputs(c + 1, 1 - k, 1)
                    copy_ids(act, m, s, ids, c + 3, 1 - k)
                turned(c, 3)
                if has_last(c):
                    copy_sums(act, s, ps_s, ob, c - 1, 1 - k)
                if has_next(c):
                    turned(c + 1, 0)

            for k in range(2):
                copy_ids(act, m, s, ids, k, k)
            for q in range(2):
                inputs(0, 0, q)
            copy_ids(act, m, s, ids, 2, 0)
            turned(0, 0)
            trips(act, chunk)
            tanh(C - 1, 1)
            copy_sums(act, s, ps_s, ob, C - 1, 1)

        @block.tensor
        def _(pe):
            grant(pe, s, "rows_transposed", "x_left", "x_back", "a_transposed", "g_made", "msg_ready", "sums_transposed")

            def forth(c, k, i, q):
                if q == 0:
                    pe.wait_ge(s[f"src_rows{k}"], (i + 1) * (16 * T))
                    pe.wait_ge(s[f"dst_rows{k}"], (i + 1) * (16 * J))
                pe.wait_ge(s["x_scanned"], went(c * 2 + q, 1))
                for j in range(J):
                    last = pe.transpose(ps_x[:, j::J], rows[k][:, j, 2 * q:2 * q + 2, :, :], m.ident[:, :])
                last.then_inc(s["x_left"], 1)

            def back(c, k, q):
                pe.wait_ge(s["x_scanned"], went(c * 2 + q))
                if q == 1:
                    pe.sem_inc(s["rows_transposed"], 1)
                pe.wait_ge(s["a_copied"], went(c * 2 + q, 1))
                for j in range(J):
                    last = pe.transpose(ps_e[:, j, :, :, :].rearrange("p r s f -> p (r s f)"), xt[k][:, q, j::J], m.ident[:, :])
                last.then_inc(s["x_back"], 1)

            def turn(c, k, j):
                if j == 0:
                    pe.wait_ge(s["a_ready"], went(c))
                pe.wait_ge(s["at_copied"], went(c * J + j, 1))
                for r in range(R):
                    last = pe.transpose(ps_t[:, r, :], inp[k][:, j * R + r, :], m.ident[:, :])
                last.then_inc(s["a_transposed"], 1)

            def product(c, t):
                j, r = t // R, t % R
                if r == 0:
                    pe.wait_ge(s["at_copied"], went(c * J + j))
                pe.wait_ge(s["g_weighed"], went(c * T + t, 2))
                for half in range(2):
                    last = pe.matmul(ps_g[:, t % 2, half, 0:HK], at[j % 2][:, r, :],
                                     e.w[:, half * HK:(half + 1) * HK], start=True, stop=True)
                last.then_inc(s["g_made"], 1)

            def features(c, k):
                pe.wait_ge(s["ftr_ready"], went(c))
                pe.wait_ge(s["sums_copied"], went(c, 1))
                for j in range(J):
                    last = pe.transpose(ps_m[:, j::J], ftr[k][:, j * R:(j + 1) * R, :].rearrange("p r f -> p (r f)"), m.ident[:, :])
                last.then_inc(s["msg_ready"], 1)

            def chunk(c, k, i):
                if has_next(c):
                    n, kn, i_n = c + 1, 1 - k, i + k
                for t in range(T):
                    product(c, t)
                    if t == 1:
                        turn(c, k, 1)
                        if has_next(c):
                            forth(n, kn, i_n, 0)
                    elif t == 5:
                        if has_next(c):
                            back(n, kn, 0)
                            forth(n, kn, i_n, 1)
                        turn(c, k, 2)
                    elif t == 9:
                        if has_next(c):
                            back(n, kn, 1)
                        turn(c, k, 3)
                        if has_last(c):
                            features(c - 1, 1 - k)
                    elif t == 14:
                        if has_last(c):
                            transpose_sums(pe, m, s, sc, ps_s, c - 1, 1 - k)
                        if has_next(c):
                            turn(n, kn, 0)

            for q in range(2):
                forth(0, 0, 0, q)
                back(0, 0, q)
            pe.wait_ge(s["pad_zeroed"], 2)
            turn(0, 0, 0)
            trips(pe, chunk)
            features(C - 1, 1)
            transpose_sums(pe, m, s, sc, ps_s, C - 1, 1)

        @block.vector
        def _(dve):
            grant(dve, s, "x_scanned", "projected", "a_ready", "g_weighed", "g_added", "spread", "ftr_ready", "msg_scanned")
            dve.memset(xt[1][:, :, :], 0.0).then_inc(s["state_zeroed"], 1)
            dve.memset(sc[1][:, :], 0.0).then_inc(s["state_zeroed"], 1)
            dve.wait_ge(s["state_zeroed"], 2)

            def unit_of(c):
                return e.unit[:, bass.ds(c * T, T), :]

            def scan_pair(c, k, q):
                dve.wait_ge(s["x_left"], went(c * 2 + q))
                dve.wait_ge(s["x_back"], went(c * 2 + q, 4))
                dve.wait_ge(s["x_scanned"], went(c * 2 + q, 2))
                dve.tensor_tensor_scan(xt[k][:, q, :], m.keep_pair[:, q, bass.ds(c * W, W)], ps_x[:, :],
                                       xt[1 - k][:, q, W - 1:W], ALU.mult, ALU.add).then_inc(s["x_scanned"], 1)

            def project(c, k):
                dve.wait_ge(s["a_copied"], went(c * 2 + 1))
                dve.tensor_tensor(proj[:, :, :, :], inp[k][:, :, 32:UA].rearrange("p t (i u) -> p t i u", i=3),
                                  unit_of(c).unsqueeze(3).broadcast_to([128, T, 3, 16]), ALU.mult).then_inc(s["projected"], 1)

            def inner(c, k):
                dve.wait_ge(s["projected"], went(c))
                dve.tensor_reduce(inp[k][:, :, 16:32], proj[:, :, :, :].rearrange("p t i u -> p t u i"), AX.X, ALU.add)\
                   .then_inc(s["a_ready"], 1)

            def weigh(c, t):
                dve.wait_ge(s["g_made"], went(c * T + t))
                dve.wait_ge(s["g_added"], went(c * T + t, DEEP))
                dve.tensor_tensor(
                    prod[t % DEEP][:, :].rearrange("p (g k o) -> p g k o", g=2, o=OUT2),
                    ps_g[:, t % 2, :, 0:HK].rearrange("p g (k o) -> p g k o", o=OUT2),
                    e.hidden[:, bass.ds(c * T + t, 1), :].rearrange("p t (g k) -> p (t g) k", g=2)
                    .unsqueeze(3).broadcast_to([128, 2, K2 // 2, OUT2]), ALU.mult).then_inc(s["g_weighed"], 1)

            def add(c, k, t):
                if t % DEEP != 0:
                    dve.wait_ge(s["g_halved"], went(c * (T - T // DEEP) + t - 1 - t // DEEP))
                    weighed = halved[t % DEEP - 1]
                else:
                    dve.wait_ge(s["g_weighed"], went(c * T + t))
                    weighed = prod[t % DEEP]
                dve.tensor_reduce(res[k][:, t, :], weighed[:, :].rearrange("p (k o) -> p o k", o=OUT2), AX.X, ALU.add)\
                   .then_inc(s["g_added"], 1)

            def vectors(c, k):
                r4 = res[k][:, :, 24:OUT2].rearrange("p t (i w) -> p t i w", i=3)
                dve.wait_ge(s["g_added"], went(c * T + T - 1))
                dve.tensor_tensor(vec[:, :, :, :], res[k][:, :, 16:24].unsqueeze(2).broadcast_to([128, T, 3, 8]),
                                  unit_of(c).unsqueeze(3).broadcast_to([128, T, 3, 8]), ALU.mult).then_inc(s["chain"], 1)
                dve.wait_ge(s["chain"], c * 4 + 1)
                dve.tensor_tensor(vec[:, :, :, :], vec[:, :, :, :], r4, ALU.add).then_inc(s["chain"], 1)

            def gate(c, k):
                dve.wait_ge(s["acted"], went(c))
                dve.wait_ge(s["msg_ready"], went(c, 2))
                dve.tensor_tensor(ftr[k][:, :, 0:8], gated[:, :, 0:8],
                                  e.norm_s[:, bass.ds(c * T, T)].unsqueeze(2).broadcast_to([128, T, 8]), ALU.mult)\
                   .then_inc(s["chain"], 1)
                dve.tensor_tensor(gated[:, :, 8:16], gated[:, :, 8:16],
                                  e.norm_v[:, bass.ds(c * T, T)].unsqueeze(2).broadcast_to([128, T, 8]), ALU.mult)\
                   .then_inc(s["chain"], 1)
                dve.wait_ge(s["chain"], c * 4 + 4)
                dve.tensor_tensor(ftr[k][:, :, 8:D].rearrange("p t (w i) -> p t i w", i=3), vec[:, :, :, :],
                                  gated[:, :, 8:16].unsqueeze(2).broadcast_to([128, T, 3, 8]), ALU.mult)\
                   .then_inc(s["ftr_ready"], 1)
                dve.wait_ge(s["ftr_ready"], went(c))
                dve.sem_inc(s["spread"], 1)

            def chunk(c, k, i):
                for t in range(T):
                    weigh(c, t)
                    if t >= LAG:
                        add(c, k, t - LAG)
                    elif has_last(c):
                        add(c - 1, 1 - k, T - LAG + t)
                    if has_next(c):
                        if t == 2:
                            scan_pair(c + 1, 1 - k, 0)
                        elif t == 6:
                            scan_pair(c + 1, 1 - k, 1)
                        elif t == 9:
                            project(c + 1, 1 - k)
                        elif t == 10:
                            inner(c + 1, 1 - k)
                    if has_last(c):
                        if t == LAG + 1:
                            vectors(c - 1, 1 - k)
                        elif t == 4:
                            gate(c - 1, 1 - k)
                        elif t == 11:
                            scan_messages(dve, m, s, ps_m, sc, c - 1, 1 - k, "msg_ready")

            for q in range(2):
                scan_pair(0, 0, q)
            project(0, 0)
            inner(0, 0)
            trips(dve, chunk)
            for t in range(T - LAG, T):
                add(C - 1, 1, t)
            vectors(C - 1, 1)
            gate(C - 1, 1)
            scan_messages(dve, m, s, ps_m, sc, C - 1, 1, "msg_ready")


def add_step(nc, m, name):
    with Step(nc, name) as st:
        block = st.block()

        @block.vector
        def _(dve):
            dve.tensor_tensor(m.x[:, :], m.x[:, :], m.agg[:, :], ALU.add)


def equi_layer(nc, m):
    norm_step(nc, m, "equi_norm")
    with Step(nc, "equi") as st:
        e = equi_memory(st)
        equi_prepare_step(nc, m, e)
        publish_step(nc, m, "equi_publish")
        equi_edges_step(nc, m, e)
    collect_step(nc, m, "equi_collect", m.sums, m.rows)
    add_step(nc, m, "equi_add")


HOPS = 3
S = 5
TP = T - S


def pick_memory(st):
    o = Mem()
    o.hi = st.sb("pick_hi", [PN, C * S * 128], BF16)
    o.lo = st.sb("pick_lo", [128, C * S, BN])
    return o


def pick_prepare_step(nc, m, o, name, x):
    PIECES = 5
    PW = C * S * 128 // PIECES
    with Step(nc, name) as st:
        sb = st.sb
        s = st.sems("iotas_made", "chain", "ids_loaded0", "ids_loaded1", "above_made", "piece_made")
        ids = [sb(f"ids{k}", [PN, PW], I32) for k in range(2)]
        above = [sb(f"above{k}", [PN, PW], BF16) for k in range(2)]
        first_i, block_i = sb("first_i", [PN, 1], I32), sb("block_i", [128, BN], I32)
        first, block_f = sb("first", [PN, 2]), sb("block_f", [128, BN])
        src, hi, ew = sb("src", [128, C, S]), sb("hi", [128, C, S]), m.ew[:, :].rearrange("p (c t) -> p c t", t=T)[:, :, TP:]
        block = st.block()

        @block.sync
        def _(sp):
            for q in range(PIECES):
                if q >= 2:
                    sp.wait_ge(s["piece_made"], q - 1)
                sp.dma_start(ids[q % 2][:, :], m.a.src_row[q * PW:(q + 1) * PW].partition_broadcast(PN))\
                  .then_inc(s[f"ids_loaded{q % 2}"], 16)

        @block.gpsimd
        def _(pool):
            pool.iota(first_i[:, :], [[1, 1]], base=0, channel_multiplier=BN)
            pool.iota(block_i[:, :], [[1, BN]], base=0, channel_multiplier=0).then_inc(s["iotas_made"], 1)

        @block.vector
        def _(dve):
            n = [0]

            def step(ins):
                link(dve, s["chain"], n, ins)

            dve.tensor_copy(x, m.h[:, :].rearrange("p (b f) -> p b f", f=D))
            dve.wait_ge(s["iotas_made"], 1)
            step(dve.tensor_copy(first[:, 0:1], first_i[:, :]))
            step(dve.tensor_scalar(first[:, 1:2], first[:, 0:1], float(BN), None, ALU.add))
            step(dve.tensor_copy(block_f[:, :], block_i[:, :]))
            step(dve.tensor_copy(src[:, :, :], m.src[:, 0:C * T].rearrange("p (c t) -> p c t", t=T)[:, :, TP:]))
            step(dve.tensor_scalar(hi[:, :, :], src[:, :, :], 1.0 / BN, 0.48, ALU.mult, ALU.subtract))
            step(dve.tensor_scalar(hi[:, :, :], hi[:, :, :], 12582912.0, None, ALU.add))
            step(dve.tensor_scalar(hi[:, :, :], hi[:, :, :], 12582912.0, None, ALU.subtract))
            step(dve.scalar_tensor_tensor(src[:, :, :], hi[:, :, :], -float(BN), src[:, :, :], ALU.mult, ALU.add))
            lo4 = o.lo[:, :, :].rearrange("p (c s) b -> p c s b", s=S)
            for t in range(S):
                step(dve.tensor_tensor(lo4[:, :, t, :], block_f[:, :].unsqueeze(1).broadcast_to([128, C, BN]),
                                       src[:, :, t].unsqueeze(2).broadcast_to([128, C, BN]), ALU.is_equal))
                step(dve.tensor_tensor(lo4[:, :, t, :], lo4[:, :, t, :],
                                       ew[:, :, t].unsqueeze(2).broadcast_to([128, C, BN]), ALU.mult))
            for q in range(PIECES):
                dve.wait_ge(s[f"ids_loaded{q % 2}"], 16 * (q // 2 + 1))
                dve.tensor_scalar(above[q % 2][:, :], ids[q % 2][:, :], first[:, 0:1], None, ALU.is_ge)\
                   .then_inc(s["above_made"], 1)
                dve.wait_ge(s["above_made"], q + 1)
                dve.scalar_tensor_tensor(o.hi[:, q * PW:(q + 1) * PW], ids[q % 2][:, :], first[:, 1:2], above[q % 2][:, :],
                                         ALU.is_lt, ALU.mult).then_inc(s["piece_made"], 1)


def tag_hop_step(nc, m, o, name, x):
    F0 = 512
    with Step(nc, name) as st:
        sb, ps = st.sb, st.ps
        s = st.sems(*tail_sems(), "table_stored", "state_zeroed", "ids_copied", "pool_turn", "src_rows0", "src_rows1",
                    "rows_weighed", "part_made", "table_made", "picks_made", "picks_weighed", "picked")
        rows = [sb(f"rows{k}", [128, TP, D]) for k in range(2)]
        msg = [sb(f"msg{k}", [128, T, D]) for k in range(2)]
        ids = [sb(f"ids{k}", [128, T], I32) for k in range(2)]
        sc = [sb(f"sc{k}", [128, W]) for k in range(2)]
        ob = [sb(f"ob{k}", [128, R * J * D]) for k in range(2)]
        table = sb("table", [PN, 3, BN * D], BF16)
        rest = sb("rest", [PN, BN * D])
        prod = [sb(f"prod{k}", [128, BN * D]) for k in range(2)]
        ps_p = [ps(f"p{k}", [128, 1024]) for k in range(2)]
        ps_m = ps("m", [128, 2, W])
        ps_s = ps("s", [128, J, 128])
        block = st.block()

        def trips(eng, chunk):
            with eng.Fori(0, HALF - 1) as i:
                for k in range(2):
                    chunk(i * 2 + k, k, i)
            for k in range(2):
                chunk(C - 2 + k, k, HALF - 1)

        def has_next(c):
            return not (isinstance(c, int) and c == C - 1)

        @block.sync
        def _(sp):
            grant(sp, s, "out_free")
            sp.dma_start(m.table.rearrange("(p b) f -> p b f", b=BN), x).then_inc(s["table_stored"], 16)
            with sp.Fori(0, HALF) as i:
                for k in range(2):
                    store_sums(sp, m, s, ob, i * 2 + k, k, i)

        @block.gpsimd
        def _(pool):
            pool.wait_ge(s["table_stored"], 16)
            with pool.Fori(0, HALF) as i:
                for k in range(2):
                    c = i * 2 + k
                    pool.wait_ge(s["rows_weighed"], went(c, 2))
                    pool.wait_ge(s["ids_copied"], went(c))
                    pool.sem_inc(s["pool_turn"], 1)
                    for t in range(TP):
                        pool.indirect_dma_start(rows[k][:, t, :], None, m.table,
                                                bass.IndirectOffsetOnAxis(ap=ids[k][:, t:t + 1], axis=0))\
                            .then_inc(s[f"src_rows{k}"], 16)

        @block.vector
        def _(dve):
            grant(dve, s, "rows_weighed", "msg_scanned", "picks_weighed", "picked")
            n = [0]
            rest3 = rest[:, :].rearrange("p (b f) -> p b f", f=D)
            parts = [table[:, q, :].rearrange("p (b f) -> p b f", f=D) for q in range(3)]
            link(dve, s["part_made"], n, dve.tensor_copy(parts[0], x))
            link(dve, s["part_made"], n, dve.tensor_tensor(rest3, x, parts[0], ALU.subtract))
            link(dve, s["part_made"], n, dve.tensor_copy(parts[1], rest3))
            dve.tensor_tensor(parts[2], rest3, parts[1], ALU.subtract).then_inc(s["table_made"], 1)
            dve.memset(sc[1][:, :], 0.0).then_inc(s["state_zeroed"], 1)
            dve.wait_ge(s["state_zeroed"], 1)

            def weigh(c, k, t):
                n, b = c * S + t, (k + t) % 2
                dve.wait_ge(s["picks_made"], went(n))
                dve.wait_ge(s["picked"], went(n, 2))
                dve.tensor_tensor(prod[b][:, :].rearrange("p (b f) -> p b f", f=D),
                                  ps_p[b][:, 0:BN * D].rearrange("p (b f) -> p b f", f=D),
                                  o.lo[:, bass.ds(n, 1), :].rearrange("p n b -> p (n b)").unsqueeze(2)
                                  .broadcast_to([128, BN, D]), ALU.mult).then_inc(s["picks_weighed"], 1)

            def pick(c, k, t):
                n, b = c * S + t, (k + t) % 2
                if t == 0:
                    dve.wait_ge(s["msg_ready"], went(c, 2))
                dve.wait_ge(s["picks_weighed"], went(n))
                dve.tensor_reduce(msg[k][:, TP + t, :], prod[b][:, :].rearrange("p (b f) -> p f b", f=D), AX.X, ALU.add)\
                   .then_inc(s["picked"], 1)

            def picks(c, k, tiles):
                for t in tiles:
                    weigh(c, k, t)
                    if t >= 1:
                        pick(c, k, t - 1)
                    if t == S - 1:
                        pick(c, k, t)

            def chunk(c, k, i):
                dve.wait_ge(s[f"src_rows{k}"], (i + 1) * (16 * TP))
                dve.wait_ge(s["msg_ready"], went(c, 2))
                dve.tensor_tensor(msg[k][:, 0:TP, :], rows[k][:, :, :],
                                  m.ew[:, bass.ds(c * T, TP)].unsqueeze(2).broadcast_to([128, TP, D]), ALU.mult)\
                   .then_inc(s["rows_weighed"], 1)
                if has_next(c):
                    picks(c + 1, 1 - k, range(2))
                scan_messages(dve, m, s, ps_m[:, k, :], sc, c, k, "msg_ready")
                if has_next(c):
                    picks(c + 1, 1 - k, range(2, S))

            picks(0, 0, range(S))
            trips(dve, chunk)

        @block.tensor
        def _(pe):
            grant(pe, s, "msg_ready", "sums_transposed", "picks_made")
            pe.wait_ge(s["table_made"], 1)

            def picks(c, k, tiles):
                for t in tiles:
                    n, b = c * S + t, (k + t) % 2
                    pe.wait_ge(s["picks_weighed"], went(n, 2))
                    for first, last_col in ((0, F0), (F0, BN * D)):
                        for q in range(3):
                            last = pe.matmul(ps_p[b][:, first:last_col], o.hi[:, bass.ds(n * 128, 128)],
                                             table[:, q, first:last_col], start=(q == 0), stop=(q == 2))
                    last.then_inc(s["picks_made"], 1)

            def chunk(c, k, i):
                if has_next(c):
                    picks(c + 1, 1 - k, range(2))
                pe.wait_ge(s["picked"], went(c * S + S - 1))
                pe.wait_ge(s["rows_weighed"], went(c))
                pe.wait_ge(s["msg_scanned"], went(c, 2))
                for j in range(J):
                    last = pe.transpose(ps_m[:, k, j::J], msg[k][:, j * R:(j + 1) * R, :].rearrange("p r f -> p (r f)"), m.ident[:, :])
                last.then_inc(s["msg_ready"], 1)
                if has_next(c):
                    picks(c + 1, 1 - k, range(2, 4))
                transpose_sums(pe, m, s, sc, ps_s, c, k)
                if has_next(c):
                    picks(c + 1, 1 - k, range(4, S))

            picks(0, 0, range(S))
            trips(pe, chunk)

        @block.scalar
        def _(act):
            grant(act, s, "ids_copied", "sums_copied")

            def take_ids(c, k):
                act.wait_ge(s["rows_weighed"], went(c, 2))
                act.activation(ids[k][:, :], m.src[:, bass.ds(c * T, T)], ACT.Copy).then_inc(s["ids_copied"], 1)

            for k in range(2):
                take_ids(k, k)
            with act.Fori(0, HALF) as i:
                for k in range(2):
                    c = i * 2 + k
                    take_ids(c + 2, k)
                    copy_sums(act, s, ps_s, ob, c, k)


def tag_mix_step(nc, m, name, hops, weights, bias_in, gamma_in, beta_in, last_layer):
    with Step(nc, name) as st:
        sb, ps = st.sb, st.ps
        s = st.sems("w_loaded", "transposed", "copied", "mixed", *bn_sems())
        b = bn_memory(st)
        w = sb("w", [HOPS * D, D])
        bias, gamma, beta = sb("bias", [PN, D]), sb("gamma", [PN, D]), sb("beta", [PN, D])
        ht = sb("hops_t", [HOPS * D, BN, PN])
        y = sb("y", [PN, BN * D])
        z = sb("z", [PN, BN * D])
        ps_t = ps("t", [HOPS * D, 2, 4, 128])
        ps_o = ps("o", [PN, 2, 512])
        groups = [list(range(t, min(t + 4, BN))) for t in range(0, BN, 4)]
        block = st.block()

        @block.sync
        def _(sp):
            sp.dma_start(w[:, :], weights.rearrange("k f o -> (k f) o")).then_inc(s["w_loaded"], 16)
            for to, v in ((bias, bias_in), (gamma, gamma_in), (beta, beta_in)):
                sp.dma_start(to[:, :], v.partition_broadcast(PN)).then_inc(s["w_loaded"], 16)

        @block.tensor
        def _(pe):
            for t, bs in enumerate(groups):
                if t >= 2:
                    pe.wait_ge(s["copied"], t - 1)
                for x, blk in enumerate(bs):
                    last = pe.transpose(ps_t[:, t % 2, x, 0:PN], hops[:, blk, :], m.ident[0:PN, 0:PN])
                last.then_inc(s["transposed"], 1)
            pe.wait_ge(s["w_loaded"], 64)
            pe.wait_ge(s["copied"], len(groups))
            for blk in range(BN):
                last = pe.matmul(ps_o[:, blk // 16, (blk % 16) * D:(blk % 16) * D + D], ht[:, blk, :], w[:, :],
                                 start=True, stop=True)
            last.then_inc(s["mixed"], 1)
            bn_pe(pe, m, s, b, y)

        @block.scalar
        def _(act):
            bn_act(act, s, b)

        @block.vector
        def _(dve):
            n = [0]

            def step(ins):
                link(dve, s["chain"], n, ins)

            for t, bs in enumerate(groups):
                dve.wait_ge(s["transposed"], t + 1)
                dve.tensor_copy(ht[:, bs[0]:bs[-1] + 1, :], ps_t[:, t % 2, 0:len(bs), 0:PN]).then_inc(s["copied"], 1)
            dve.wait_ge(s["w_loaded"], 64)
            dve.wait_ge(s["mixed"], 1)
            y3 = y[:, :].rearrange("p (b f) -> p b f", f=D)
            bias3 = bias[:, :].unsqueeze(1)
            dve.tensor_tensor(y3[:, 0:16, :], ps_o[:, 0, :].rearrange("p (b f) -> p b f", f=D), bias3.broadcast_to([PN, 16, D]), ALU.add)
            step(dve.tensor_tensor(y3[:, 16:BN, :], ps_o[:, 1, 0:(BN - 16) * D].rearrange("p (b f) -> p b f", f=D),
                                   bias3.broadcast_to([PN, BN - 16, D]), ALU.add))
            bn_dve(dve, s, n, b, y, z, gamma, beta)
            if last_layer:
                step(dve.scalar_tensor_tensor(z[:, :], z[:, :], 0.01, z[:, :], ALU.mult, ALU.max))
                step(dve.tensor_tensor(m.x[:, :], m.x[:, :], z[:, :], ALU.add))
            else:
                z3 = z[:, :].rearrange("p (b f) -> p b f", f=D)
                step(dve.scalar_tensor_tensor(hops[:, :, 0:D], z3, 0.01, z3, ALU.mult, ALU.max))


def tag_layer(nc, m):
    a = m.a
    norm_step(nc, m, "tag_norm")
    with Step(nc, "tag") as st:
        hops = st.sb("hops", [PN, BN, HOPS * D])
        o = pick_memory(st)
        pick_prepare_step(nc, m, o, "pick_prepare", hops[:, :, 0:D])
        for conv, w in enumerate(((a.T1, a.tb1, a.tg1, a.tt1), (a.T2, a.tb2, a.tg2, a.tt2))):
            for hop in range(1, HOPS):
                tag_hop_step(nc, m, o, f"tag{conv}_hop{hop}", hops[:, :, (hop - 1) * D:hop * D])
                collect_step(nc, m, f"tag{conv}_collect{hop}", m.sums, m.rows, hops[:, :, hop * D:(hop + 1) * D])
            tag_mix_step(nc, m, f"tag{conv}_mix", hops, *w, last_layer=(conv == 1))


def store_step(nc, m, out):
    with Step(nc, "store") as st:
        s = st.sems("out_stored")
        block = st.block()

        @block.sync
        def _(sp):
            sp.dma_start(out.rearrange("(p b) f -> p (b f)", b=BN), m.x[:, :]).then_inc(s["out_stored"], 16)
            sp.wait_ge(s["out_stored"], 16)


def program(nc, a, out):
    with ExitStack() as ctx:
        m = allocate(nc, ctx, a)
        graph_step(nc, m)
        norm_step(nc, m, "mp_norm")
        publish_step(nc, m, "mp_publish")
        mp_edges_step(nc, m)
        collect_step(nc, m, "mp_collect", m.sums, m.rows)
        mp_update_step(nc, m)
        gat_layers(nc, m)
        equi_layer(nc, m)
        tag_layer(nc, m)
        store_step(nc, m, out)


def _edge_major(v, fill):
    pad = np.full((EP - E,) + v.shape[1:], fill, v.dtype)
    w = np.concatenate([v, pad]).reshape((R, C, 128, J) + v.shape[1:])
    w = np.transpose(w, (2, 1, 3, 0) + tuple(range(4, w.ndim)))
    return np.ascontiguousarray(w.reshape((128, C * T) + v.shape[1:]))


def kernel(**inputs):
    import concourse.bacc as _bacc
    from concourse.bass_utils import run_bass_kernel_spmd as _run

    g = {k: np.asarray(v) for k, v in inputs.items()}
    arrays = {
        "x": g["x"],
        "src_t": _edge_major(g["src"], 0),
        "src_row": _edge_major(g["src"], 0).reshape(128, C, T)[:, :, TP:].transpose(1, 2, 0).reshape(-1),
        "dst_t": _edge_major(g["dst"], N),
        "dst_ext": np.concatenate([np.full(1, -1, np.int32), g["dst"], np.full(EP - E + 1, N, np.int32)]),
        "ew_t": _edge_major(g["edge_weight"], 0),
        "vec_t": _edge_major(g["edge_attr_3"], 1).reshape(128, -1),
        "ef_t": np.pad(g["edge_attr_16"], ((0, EP - E), (0, 0))).reshape(R, RW, 16).transpose(0, 2, 1).reshape(R * 16, RW),
        "emb_t": np.pad(g["edge_attr_10"], ((0, EP - E), (0, 0))).reshape(R, RW, 10).transpose(0, 2, 1).reshape(R * 10, RW),
        "W2e": g["L2_gnn_W2"].reshape(16, 7, 16, 8).transpose(2, 1, 0, 3),
    }
    for short, name in [("W1m", "L0_gnn_W1m"), ("b1m", "L0_gnn_b1m"), ("W2m", "L0_gnn_W2m"), ("b2m", "L0_gnn_b2m"),
                        ("W1u", "L0_gnn_W1u"), ("b1u", "L0_gnn_b1u"), ("W2u", "L0_gnn_W2u"), ("b2u", "L0_gnn_b2u"),
                        ("Wl", "L1_gnn_Wl"), ("bl", "L1_gnn_bl"), ("Wr", "L1_gnn_Wr"), ("br", "L1_gnn_br"),
                        ("att", "L1_gnn_att"), ("cb", "L1_gnn_conv_bias"), ("bng", "L1_gnn_bn_gamma"),
                        ("bnb", "L1_gnn_bn_beta"), ("W1e", "L2_gnn_W1"), ("T1", "L3_gnn_W1"), ("tb1", "L3_gnn_bias1"),
                        ("tg1", "L3_gnn_gamma1"), ("tt1", "L3_gnn_beta1"), ("T2", "L3_gnn_W2"), ("tb2", "L3_gnn_bias2"),
                        ("tg2", "L3_gnn_gamma2"), ("tt2", "L3_gnn_beta2")]:
        arrays[short] = g[name]
    nc = _bacc.Bacc("TRN2", target_bir_lowering=False, num_devices=1)
    a, arrays_in = Mem(), {}
    for name, v in arrays.items():
        v = np.ascontiguousarray(v)
        arrays_in[f"in_{name}"] = v
        a.__dict__[name] = nc.dram_tensor(f"in_{name}", v.shape, mybir.dt.from_np(v.dtype), kind="ExternalInput").ap()
    out = nc.dram_tensor("out", (N, D), F32, kind="ExternalOutput").ap()
    program(nc, a, out)
    got = _run(nc, [arrays_in], core_ids=[0])
    return got.results[0]["out"]
```
